# Optimizing a Trainium2 kernel written in Bass

```python
import numpy as np
import jax
import jax.numpy as jnp

def _softmax(x, axis=-1):
    return jax.nn.softmax(x, axis=axis)

def _gelu(x):
    return jax.nn.gelu(x, approximate=True)

def _silu(x):
    return jax.nn.silu(x)

def _sigmoid(x):
    return jax.nn.sigmoid(x)

def _layernorm(x, axis=-1, eps=1e-05):
    m = jnp.mean(x, axis=axis, keepdims=True)
    v = jnp.var(x, axis=axis, keepdims=True)
    return (x - m) / jnp.sqrt(v + eps)

def _scatter_add(tgt, idx, src, axis=0):
    return tgt.at[idx].add(src)

def _segment_sum(src, seg, n):
    return jax.ops.segment_sum(src, seg, n)
kernel_name = 'mk_seq_postln_d1_jaxref_r8_2b4ec6'

def setup_inputs(seed: int=0):
    np.random.seed(seed)
    _w = jnp.asarray

    def _L0_attn_setup():
        import jax, jax.numpy as jnp
        import numpy as np
        HID = 128
        NH = 16
        NKV = 4
        HD = 64
        C = 64
        RATIO = 0.125
        KS = 7

        def _block_causal_attention(x, qw, kw, vw, ow, k):
            B, nc, _, D = x.shape
            T = nc * k
            xf = x.reshape(B, T, D)
            q = (xf @ qw.T).reshape(B, T, NH, HD).transpose(0, 2, 1, 3)
            kk = (xf @ kw.T).reshape(B, T, NKV, HD).transpose(0, 2, 1, 3)
            v = (xf @ vw.T).reshape(B, T, NKV, HD).transpose(0, 2, 1, 3)
            rep = NH // NKV
            kk = jnp.repeat(kk, rep, axis=1)
            v = jnp.repeat(v, rep, axis=1)
            chunk_ids = jnp.arange(T) // k
            mask = chunk_ids[:, None] >= chunk_ids[None, :]
            scores = jnp.einsum('bhqd,bhkd->bhqk', q, kk) / np.float32(np.sqrt(HD))
            scores = jnp.where(mask[None, None], scores, jnp.finfo(scores.dtype).min)
            p = jax.nn.softmax(scores, axis=-1)
            o = jnp.einsum('bhqk,bhkd->bhqd', p, v)
            o = o.transpose(0, 2, 1, 3).reshape(B, T, NH * HD)
            return (o @ ow.T).reshape(B, nc, k, D)

        def _causal_conv(x, dw, pw):
            B, nc, L, D = x.shape
            xc = x.reshape(B * nc, L, D).transpose(0, 2, 1)
            xp = jnp.pad(xc, ((0, 0), (0, 0), (KS - 1, 0)))
            y = jax.lax.conv_general_dilated(xp, dw, window_strides=(1,), padding='VALID', dimension_numbers=('NCH', 'OIH', 'NCH'), feature_group_count=D)
            y = jax.nn.gelu(y, approximate=False)
            y = jnp.einsum('ncl,oc->nol', y, pw)
            return y.transpose(0, 2, 1).reshape(B, nc, L, D)

        def _forward(hidden_states, q_w, k_w, v_w, o_w, dw_r, pw_r, dw_i, pw_i, gate_w, alpha_raw):
            B, N, D = hidden_states.shape
            pad_len = -N % C
            x = jnp.pad(hidden_states, ((0, 0), (0, pad_len), (0, 0))) if pad_len else hidden_states
            nc = x.shape[1] // C
            chunks = x.reshape(B, nc, C, D)
            Xh = jnp.fft.rfft(chunks.astype(jnp.float32), axis=2)
            M = Xh.shape[2]
            k = max(1, int(M * RATIO))
            X_low, X_high = (Xh[:, :, :k, :], Xh[:, :, k:, :])
            A_r = _block_causal_attention(X_low.real, q_w, k_w, v_w, o_w, k)
            A_i = _block_causal_attention(X_low.imag, q_w, k_w, v_w, o_w, k)
            A_low = jax.lax.complex(A_r, A_i)
            H_r = _causal_conv(X_high.real, dw_r, pw_r)
            H_i = _causal_conv(X_high.imag, dw_i, pw_i)
            g = jax.nn.sigmoid(chunks.mean(axis=2) @ gate_w.T)[:, :, None, :]
            A_high = jax.lax.complex(H_r * g, H_i * g) + X_high
            alpha = jax.nn.sigmoid(alpha_raw)
            A_low_fused = alpha * A_low + (1.0 - alpha) * X_low
            Y_hat = jnp.concatenate([A_low_fused, A_high], axis=2)
            Y = jnp.fft.irfft(Y_hat, n=C, axis=2)
            return Y.reshape(B, -1, D)[:, :N, :].astype(hidden_states.dtype)
        key = jax.random.key(seed)
        ks = jax.random.split(key, 11)
        B, N = (4, 512)
        s = 0.02
        return {'hidden_states': jax.random.normal(ks[0], (B, N, HID), jnp.float32), 'q_w': jax.random.normal(ks[1], (NH * HD, HID), jnp.float32) * s, 'k_w': jax.random.normal(ks[2], (NKV * HD, HID), jnp.float32) * s, 'v_w': jax.random.normal(ks[3], (NKV * HD, HID), jnp.float32) * s, 'o_w': jax.random.normal(ks[4], (HID, NH * HD), jnp.float32) * s, 'dw_r': jax.random.normal(ks[5], (HID, 1, KS), jnp.float32) * 0.3, 'pw_r': jax.random.normal(ks[6], (HID, HID), jnp.float32) * s, 'dw_i': jax.random.normal(ks[7], (HID, 1, KS), jnp.float32) * 0.3, 'pw_i': jax.random.normal(ks[8], (HID, HID), jnp.float32) * s, 'gate_w': jax.random.normal(ks[9], (HID, HID), jnp.float32) * s, 'alpha_raw': jnp.zeros((1,), jnp.float32)}
    _L0_attn_in = _L0_attn_setup()

    def _L0_ffn_setup():
        import jax, jax.numpy as jnp
        import numpy as np
        E = 8
        K = 2
        D = 128
        H = 342
        B, S = (2, 256)

        def _moe_forward(x, centroid, Wg, bg, W1, b1, W2, b2):
            T = x.shape[0] * x.shape[1]
            xs = x.reshape(T, D)
            d2 = jnp.sum(xs * xs, axis=-1, keepdims=True) + jnp.sum(centroid * centroid, axis=-1)[None, :] - 2.0 * (xs @ centroid.T)
            dist = jnp.sqrt(jnp.maximum(d2, 1e-12))
            w, sel = jax.lax.top_k(dist, K)
            w = jax.nn.softmax(w.astype(jnp.float32), axis=1).astype(x.dtype)
            we = jnp.zeros((T, E), dtype=x.dtype).at[jnp.arange(T)[:, None], sel].add(w)
            out = jnp.zeros_like(xs)
            for e in range(E):
                h = jax.nn.silu(xs @ Wg[e] + bg[e]) * (xs @ W1[e] + b1[e])
                out = out + we[:, e:e + 1] * (h @ W2[e] + b2[e])
            return out.reshape(x.shape)
        key = jax.random.key(seed)
        ks = jax.random.split(key, 9)
        scale = 0.02
        return {'x': jax.random.normal(ks[0], (B, S, D), dtype=jnp.float32), 'centroid': jax.random.normal(ks[1], (E, D), dtype=jnp.float32), 'Wg': jax.random.normal(ks[2], (E, D, H), dtype=jnp.float32) * scale, 'bg': jnp.zeros((E, H), dtype=jnp.float32), 'W1': jax.random.normal(ks[3], (E, D, H), dtype=jnp.float32) * scale, 'b1': jnp.zeros((E, H), dtype=jnp.float32), 'W2': jax.random.normal(ks[4], (E, H, D), dtype=jnp.float32) * scale, 'b2': jnp.zeros((E, D), dtype=jnp.float32)}
    _L0_ffn_in = _L0_ffn_setup()
    _d = {'L0_attn_hidden_states': _L0_attn_in['hidden_states'], 'L0_attn_q_w': _L0_attn_in['q_w'], 'L0_attn_k_w': _L0_attn_in['k_w'], 'L0_attn_v_w': _L0_attn_in['v_w'], 'L0_attn_o_w': _L0_attn_in['o_w'], 'L0_attn_dw_r': _L0_attn_in['dw_r'], 'L0_attn_pw_r': _L0_attn_in['pw_r'], 'L0_attn_dw_i': _L0_attn_in['dw_i'], 'L0_attn_pw_i': _L0_attn_in['pw_i'], 'L0_attn_gate_w': _L0_attn_in['gate_w'], 'L0_attn_alpha_raw': _L0_attn_in['alpha_raw'], 'L0_ffn_centroid': _L0_ffn_in['centroid'], 'L0_ffn_Wg': _L0_ffn_in['Wg'], 'L0_ffn_bg': _L0_ffn_in['bg'], 'L0_ffn_W1': _L0_ffn_in['W1'], 'L0_ffn_b1': _L0_ffn_in['b1'], 'L0_ffn_W2': _L0_ffn_in['W2'], 'L0_ffn_b2': _L0_ffn_in['b2']}
    _x0 = _d['L0_attn_hidden_states']
    _d['L0_attn_hidden_states'] = jax.random.normal(jax.random.fold_in(jax.random.key(seed), 1), (8, 1024, 128), dtype=_x0.dtype)
    del _x0
    return _d

def reference(L0_attn_hidden_states, L0_attn_q_w, L0_attn_k_w, L0_attn_v_w, L0_attn_o_w, L0_attn_dw_r, L0_attn_pw_r, L0_attn_dw_i, L0_attn_pw_i, L0_attn_gate_w, L0_attn_alpha_raw, L0_ffn_centroid, L0_ffn_Wg, L0_ffn_bg, L0_ffn_W1, L0_ffn_b1, L0_ffn_W2, L0_ffn_b2):

    def _L0_attn_ref(hidden_states, q_w, k_w, v_w, o_w, dw_r, pw_r, dw_i, pw_i, gate_w, alpha_raw):
        import jax, jax.numpy as jnp
        import numpy as np
        HID = 128
        NH = 16
        NKV = 4
        HD = 64
        C = 64
        RATIO = 0.125
        KS = 7

        def _block_causal_attention(x, qw, kw, vw, ow, k):
            B, nc, _, D = x.shape
            T = nc * k
            xf = x.reshape(B, T, D)
            q = (xf @ qw.T).reshape(B, T, NH, HD).transpose(0, 2, 1, 3)
            kk = (xf @ kw.T).reshape(B, T, NKV, HD).transpose(0, 2, 1, 3)
            v = (xf @ vw.T).reshape(B, T, NKV, HD).transpose(0, 2, 1, 3)
            rep = NH // NKV
            kk = jnp.repeat(kk, rep, axis=1)
            v = jnp.repeat(v, rep, axis=1)
            chunk_ids = jnp.arange(T) // k
            mask = chunk_ids[:, None] >= chunk_ids[None, :]
            scores = jnp.einsum('bhqd,bhkd->bhqk', q, kk) / np.float32(np.sqrt(HD))
            scores = jnp.where(mask[None, None], scores, jnp.finfo(scores.dtype).min)
            p = jax.nn.softmax(scores, axis=-1)
            o = jnp.einsum('bhqk,bhkd->bhqd', p, v)
            o = o.transpose(0, 2, 1, 3).reshape(B, T, NH * HD)
            return (o @ ow.T).reshape(B, nc, k, D)

        def _causal_conv(x, dw, pw):
            B, nc, L, D = x.shape
            xc = x.reshape(B * nc, L, D).transpose(0, 2, 1)
            xp = jnp.pad(xc, ((0, 0), (0, 0), (KS - 1, 0)))
            y = jax.lax.conv_general_dilated(xp, dw, window_strides=(1,), padding='VALID', dimension_numbers=('NCH', 'OIH', 'NCH'), feature_group_count=D)
            y = jax.nn.gelu(y, approximate=False)
            y = jnp.einsum('ncl,oc->nol', y, pw)
            return y.transpose(0, 2, 1).reshape(B, nc, L, D)

        def _forward(hidden_states, q_w, k_w, v_w, o_w, dw_r, pw_r, dw_i, pw_i, gate_w, alpha_raw):
            B, N, D = hidden_states.shape
            pad_len = -N % C
            x = jnp.pad(hidden_states, ((0, 0), (0, pad_len), (0, 0))) if pad_len else hidden_states
            nc = x.shape[1] // C
            chunks = x.reshape(B, nc, C, D)
            Xh = jnp.fft.rfft(chunks.astype(jnp.float32), axis=2)
            M = Xh.shape[2]
            k = max(1, int(M * RATIO))
            X_low, X_high = (Xh[:, :, :k, :], Xh[:, :, k:, :])
            A_r = _block_causal_attention(X_low.real, q_w, k_w, v_w, o_w, k)
            A_i = _block_causal_attention(X_low.imag, q_w, k_w, v_w, o_w, k)
            A_low = jax.lax.complex(A_r, A_i)
            H_r = _causal_conv(X_high.real, dw_r, pw_r)
            H_i = _causal_conv(X_high.imag, dw_i, pw_i)
            g = jax.nn.sigmoid(chunks.mean(axis=2) @ gate_w.T)[:, :, None, :]
            A_high = jax.lax.complex(H_r * g, H_i * g) + X_high
            alpha = jax.nn.sigmoid(alpha_raw)
            A_low_fused = alpha * A_low + (1.0 - alpha) * X_low
            Y_hat = jnp.concatenate([A_low_fused, A_high], axis=2)
            Y = jnp.fft.irfft(Y_hat, n=C, axis=2)
            return Y.reshape(B, -1, D)[:, :N, :].astype(hidden_states.dtype)
        return _forward(hidden_states, q_w, k_w, v_w, o_w, dw_r, pw_r, dw_i, pw_i, gate_w, alpha_raw)

    def _L0_ffn_ref(x, centroid, Wg, bg, W1, b1, W2, b2):
        import jax, jax.numpy as jnp
        import numpy as np
        E = 8
        K = 2
        D = 128
        H = 342
        B, S = (2, 256)

        def _moe_forward(x, centroid, Wg, bg, W1, b1, W2, b2):
            T = x.shape[0] * x.shape[1]
            xs = x.reshape(T, D)
            d2 = jnp.sum(xs * xs, axis=-1, keepdims=True) + jnp.sum(centroid * centroid, axis=-1)[None, :] - 2.0 * (xs @ centroid.T)
            dist = jnp.sqrt(jnp.maximum(d2, 1e-12))
            w, sel = jax.lax.top_k(dist, K)
            w = jax.nn.softmax(w.astype(jnp.float32), axis=1).astype(x.dtype)
            we = jnp.zeros((T, E), dtype=x.dtype).at[jnp.arange(T)[:, None], sel].add(w)
            out = jnp.zeros_like(xs)
            for e in range(E):
                h = jax.nn.silu(xs @ Wg[e] + bg[e]) * (xs @ W1[e] + b1[e])
                out = out + we[:, e:e + 1] * (h @ W2[e] + b2[e])
            return out.reshape(x.shape)
        return _moe_forward(x, centroid, Wg, bg, W1, b1, W2, b2)
    x = L0_attn_hidden_states
    x = _layernorm(x + _L0_attn_ref(x, L0_attn_q_w, L0_attn_k_w, L0_attn_v_w, L0_attn_o_w, L0_attn_dw_r, L0_attn_pw_r, L0_attn_dw_i, L0_attn_pw_i, L0_attn_gate_w, L0_attn_alpha_raw), axis=-1)
    x = _layernorm(x + _L0_ffn_ref(x, L0_ffn_centroid, L0_ffn_Wg, L0_ffn_bg, L0_ffn_W1, L0_ffn_b1, L0_ffn_W2, L0_ffn_b2), axis=-1)
    return x

_drawn_inputs = setup_inputs


def setup_inputs(seed=0):
    import zlib

    import numpy as np

    out = dict(_drawn_inputs(seed))
    spreads = {'L0_ffn_bg': (0.0, 0.8), 'L0_ffn_b1': (0.0, 0.8), 'L0_ffn_b2': (0.0, 0.458)}
    factors = {'L0_attn_q_w': 8.0,
     'L0_attn_k_w': 8.0,
     'L0_attn_v_w': 7.144,
     'L0_attn_o_w': 7.282,
     'L0_attn_dw_r': 3.036,
     'L0_attn_dw_i': 3.267,
     'L0_attn_pw_i': 2.769,
     'L0_attn_gate_w': 8.0,
     'L0_ffn_Wg': 7.419,
     'L0_ffn_W1': 7.383,
     'L0_ffn_W2': 6.711}
    for name, (base, spread) in spreads.items():
        noise = np.random.default_rng([zlib.crc32(name.encode()), seed]).standard_normal(out[name].shape)
        drawn = base * np.exp(spread * noise) if base else spread * noise
        out[name] = jnp.asarray(drawn.astype(out[name].dtype))
    for name, factor in factors.items():
        out[name] = (out[name] * factor).astype(out[name].dtype)
    return out
```

```python
from contextlib import ExitStack

import numpy as np

import concourse.bass as bass
from concourse import mybir

P = 128
B, SEQ, D = 8, 1024, 128
C = 64
NC = SEQ // C
FR, FI = C // 2 + 1, C // 2
LOW = 4
HR, HI = FR - LOW, FI - LOW
KS = 7
NH, NKV, HD = 16, 4, 64
NHP = NH // 2
TB = SEQ // P
NT = B * TB
LT = NC * LOW
E, HF, TOPK = 8, 342, 2
HG = HF // 3
NPAIR = E * (E - 1) // 2
EPS = 1e-5
ROW = 144
RD = D + E
UNITS = TOPK * NT + NPAIR - 1
ITER = (UNITS + 1) // 2
LAGF = ITER - NT
UPAD = 2 * ITER

F32 = mybir.dt.float32
F32R = mybir.dt.float32r
BF16 = mybir.dt.bfloat16
U32 = mybir.dt.uint32
I32 = mybir.dt.int32
ALU = mybir.AluOpType
ACT = mybir.ActivationFunctionType
AX = mybir.AxisListType.X
BIG = 3.0e38
MAGIC = 0x5F3759DF


def pair_order():
    out = []
    for a in range(E - 1):
        rest = list(range(a + 1, E))
        out += [(a, b) for b in (rest if a % 2 == 0 else rest[::-1])]
    return out


def constants():
    n = np.arange(C)
    parts = {}
    fwd = np.zeros((P, P))
    for c in range(2):
        for f in range(FR):
            fwd[c * C + n, c * C + f] = np.cos(2 * np.pi * f * n / C)
        for f in range(1, FI):
            fwd[c * C + n, c * C + FR + f - 1] = -np.sin(2 * np.pi * f * n / C)
    parts["fwd"] = fwd
    high = np.zeros((P, P))
    for c in range(2):
        for f in range(LOW, FR):
            high[c * HR + f - LOW, c * C + n] = (2 if f < C // 2 else 1) / C * np.cos(2 * np.pi * f * n / C)
        for f in range(LOW, FI):
            high[C + c * HI + f - LOW, c * C + n] = -2 / C * np.sin(2 * np.pi * f * n / C)
    parts["high"] = high
    low = np.zeros((P, TB, P))
    for j in range(TB):
        for c in range(2):
            for f in range(LOW):
                row = (2 * j + c) * LOW + f
                low[row, j, c * C + n] = (2 if f else 1) / C * np.cos(2 * np.pi * f * n / C)
                if f:
                    low[LT + row, j, c * C + n] = -2 / C * np.sin(2 * np.pi * f * n / C)
    parts["low"] = low.reshape(P, TB * P)
    sel = np.zeros((P, TB, P))
    for j in range(TB):
        for c in range(2):
            sel[2 * j + c, j, c * HR:(c + 1) * HR] = 1
            sel[2 * j + c, j, C + c * HI:C + (c + 1) * HI] = 1
    parts["sel"] = sel.reshape(P, TB * P)
    q = np.arange(P) % C // LOW
    mq = np.zeros((P, P))
    mq[q, np.arange(P)] = 1
    parts["mq"] = mq
    mk = np.zeros((P, NHP, C))
    for c in range(NC):
        mk[c, :, (c + 1) * LOW:] = -BIG
    parts["mk"] = mk.reshape(P, NHP * C)
    return parts


def resident_constants():
    parts = {"ident": np.eye(P)}
    tri = np.triu(np.ones((P, P)), 1)
    parts["tri"] = tri
    parts["trim"] = tri - 1
    inc = np.zeros((P, E))
    for p, (a, b) in enumerate(pair_order()):
        inc[p, a] = inc[p, b] = 1
    parts["inc"] = inc
    parts["rev"] = np.tile(E - np.arange(E), (P, 1))
    parts["iota"] = np.tile(np.arange(P), (P, 1))
    parts["unit"] = np.tile(np.arange(UPAD), (P, 1))
    parts["part"] = np.arange(P)[:, None]
    parts["tstart"] = np.arange(P)[:, None] * P
    parts["tend"] = np.arange(P)[:, None] * P + P
    off = np.zeros((P, 1))
    off[2] = E
    parts["off"] = off
    parts["ev"] = np.tile(np.arange(E), (P, 1))
    return parts


def packed(parts):
    cols, at = {}, 0
    for k, v in parts.items():
        cols[k] = (at, at + v.shape[1])
        at += v.shape[1]
    return np.concatenate(list(parts.values()), axis=1).astype(np.float32), cols


def program(nc, x, qw, kw, vw, ow, dwr, pwr, dwi, pwi, gw, alpha, cent, Wg, bg, W1, b1, W2, b2, cst1, cst2, out):
    c1, c2 = packed(constants())[1], packed(resident_constants())[1]
    n1, n2 = cst1.shape[1], cst2.shape[1]
    rows_dram = nc.dram_tensor("rows_dram", (NT * P, RD), F32).ap()
    rows_t = rows_dram.rearrange("(b j p) d -> b p j d", p=P, j=TB)
    x_t = x.rearrange("b (j p) d -> b p j d", p=P)
    ctx = ExitStack()
    with ctx:
        def sb(name, shape, dt=F32, where=ctx):
            return where.enter_context(nc.sbuf_tensor(name, shape, dt))

        def sem(name):
            return ctx.enter_context(nc.semaphore(name))

        ps = ctx.enter_context(nc.psum_tensor("ps", [P, 8, 512], F32))
        cr = sb("cr", [P, n2])
        ident = cr[:, c2["ident"][0]:c2["ident"][1]]
        w13h = sb("w13h", [P, E, 2 * HF], F32R)
        w13l = sb("w13l", [P, E, 2 * HF], F32R)
        w2h = sb("w2h", [HG, E, 3, D], F32R)
        w2l = sb("w2l", [HG, E, 3, D], F32R)
        lg = sb("lg", [P, NT, E])
        sq = sb("sq", [P, NT])
        cn = sb("cn", [P, E])

        idx = sb("idx", [P, NT], U32)
        tab = sb("tab", [3, UPAD], I32)
        phase1(nc, locals())
        phase2(nc, locals())


def phase1(nc, g):
    ps, cr, ident, w13h, w13l, w2h, w2l = (g[k] for k in ("ps", "cr", "ident", "w13h", "w13l", "w2h", "w2l"))
    lg, sq, cn, rows_t, x_t, c1 = (g[k] for k in ("lg", "sq", "cn", "rows_t", "x_t", "c1"))
    ctx = ExitStack()
    with ctx:
        def sb(name, shape, dt=F32):
            return ctx.enter_context(nc.sbuf_tensor(name, shape, dt))

        def sem(name):
            return ctx.enter_context(nc.semaphore(name))

        cs = sb("cs1", [P, g["n1"]])
        fwd, high, mq, mk = (cs[:, c1[k][0]:c1[k][1]] for k in ("fwd", "high", "mq", "mk"))
        low = cs[:, c1["low"][0]:c1["low"][1]].rearrange("p (j m) -> p j m", j=TB)
        sel = cs[0:NC, c1["sel"][0]:c1["sel"][1]].rearrange("p (j m) -> p j m", j=TB)
        mqb = sb("mqb", [NC, P], BF16)
        mkb = sb("mkb", [NC, 512], BF16)
        qwT = sb("qwT", [P, NH * HD])
        kwT = sb("kwT", [P, NKV, 2, HD])
        vwT = sb("vwT", [P, NKV * HD])
        owT = sb("owT", [P, NKV, 2, D])
        pwT = sb("pwT", [P, 3, D])
        cT = sb("cT", [P, E])
        cT2 = sb("cT2", [P, E])
        ones = sb("ones", [P, P])
        dw = sb("dw", [P, 2, KS])
        al = sb("al", [P, 1])
        alz = sb("alz", [P, 1])
        araw = sb("araw", [P, 1])
        xt = sb("xt", [P, TB, D])
        xres = sb("xres", [P, TB, D])
        x1s = sb("x1s", [P, TB, D])
        XF = sb("XF", [P, NC, C])
        XR, XI = XF[:, :, 0:FR], XF[:, :, FR:C]
        XL = sb("XL", [P, 2, 2, LT])
        YR = sb("YR", [P, NC, HR])
        YI = sb("YI", [P, NC, HI])
        G = sb("G", [P, 2, TB, C])
        QB = sb("QB", [P, 2, NHP, 2, LT])
        kT = sb("kT", [P, NKV, 2, LT])
        VB = sb("VB", [P, 2, NKV, 2, HD])
        xln = sb("xln", [P, D])
        gate = sb("gate", [NC, D])
        gtan = sb("gtan", [NC, D])
        Sb = sb("Sb", [P, 2, NHP, LT])
        Pb = sb("Pb", [P, 2, NHP, LT])
        mx = sb("mx", [P, 2, NHP])
        sm = sb("sm", [P, 2, NHP])
        rs = sb("rs", [P, 2, NHP])
        PT = sb("PT", [P, 2, NKV, P])
        OT = sb("OT", [P, NKV, 2, 2, LT])
        AL = sb("AL", [P, D])
        Gs = sb("Gs", [P, TB, D])
        Vs = sb("Vs", [P, TB, D])
        x1T = sb("x1T", [P, TB, P])
        bn = sb("bn", [P, TB, 6])
        mv = sb("mv", [P, TB, 2])
        vh = sb("vh", [P, TB])
        y0 = sb("y0", [P, TB])
        ya = sb("ya", [P, TB])
        yb = sb("yb", [P, TB])
        c15 = sb("c15", [P, TB])
        xsq = sb("xsq", [P, TB, D])
        st = sb("st", [P, 2 * HF + 3 * D])
        raw = Gs[:, :, :].rearrange("p a b -> p (a b)")
        raw2 = Vs[:, :, :].rearrange("p a b -> p (a b)")
        raw3 = x1T[:, :, :].rearrange("p a b -> p (a b)")

        s = {k: sem("p1_" + k) for k in (
            "const_in", "raw_in", "raw3_in", "x_in", "xres_in", "w_in", "rows_out", "prep_mm", "prep_cp", "prep_cst", "prep_al", "dw_in",
            "dft_done", "proj_done", "s_done", "pt_done", "ot_done", "a_done", "g_done", "pw_done",
            "z_done", "t_done", "r_done", "xln_done",
            "xr_ev", "q_ev", "k_ev", "v_ev", "gelu_done", "pt_ev", "ot_ev", "exp_done", "g_ev", "gate_done", "tan_done",
            "x1t_ev", "whi_done", "xln_ev",
            "xl_done", "conv", "conv_done", "max_done", "sub_done", "sum_done", "rec_done", "al_done", "vg_done", "zs_done",
            "bn_done", "bn_seen", "mv_done", "seed_done", "x1_done", "lg_ev", "sq_done", "wlo_done",
            "pn_done", "c15_done", "xsq_done", "newton", "rstd_done")}

        def bank(i, n=1):
            return ps[:, i, :] if n == 1 else ps[:, i:i + n, :]

        preps = []
        qr = raw.rearrange("p (j d) -> p j d", j=8)
        owr = raw2.rearrange("p (k h a e) -> p k h a e", k=NKV, a=2, h=2)
        kvr = raw3.rearrange("p (j d) -> p j d", j=8)
        for j in range(8):
            preps.append((qr[:, j, :], P))
        for j in range(8):
            preps.append((raw2[:, j * P:(j + 1) * P], P))
        for j in range(8):
            preps.append((kvr[0:E if j == 7 else P, j, :], E if j == 7 else P))

        def steps(eng, step):
            step(0, True, False, False)
            step(1, True, True, False)
            step(2, True, True, True)
            with eng.Fori(3, B) as s_:
                step(s_, True, True, True)
            step(B, False, True, True)
            step(B + 1, False, False, True)

        block = ctx.enter_context(nc.Block())

        @block.sync
        def _(sp):
            sp.dma_start(qr, g["qw"].rearrange("(j p) d -> p j d", p=P)).then_inc(s["raw_in"], 16)
            for h in range(2):
                for a in range(2):
                    sp.dma_start(owr[:, :, h, a, :], g["ow"].rearrange("o (k a h e) -> a h o k e", k=NKV, a=2, h=2)[a, h])\
                      .then_inc(s["raw_in"], 16)
            sp.dma_start(kvr[:, 0:2, :], g["kw"].rearrange("(j p) d -> p j d", p=P)).then_inc(s["raw3_in"], 16)
            sp.dma_start(kvr[:, 2:4, :], g["vw"].rearrange("(j p) d -> p j d", p=P)).then_inc(s["raw3_in"], 16)
            sp.dma_start(kvr[:, 4, :], g["pwr"]).then_inc(s["raw3_in"], 16)
            sp.dma_start(kvr[:, 5, :], g["pwi"]).then_inc(s["raw3_in"], 16)
            sp.dma_start(kvr[:, 6, :], g["gw"]).then_inc(s["raw3_in"], 16)
            sp.dma_start(kvr[0:E, 7, :], g["cent"]).then_inc(s["raw3_in"], 16)

            def step(t, X, Y, T):
                if X:
                    sp.wait_ge(s["dft_done"], 2 * t)
                    sp.dma_start(xt[:, :, :], x_t[bass.ds(t, 1), :, :, :].rearrange("b p j d -> p (b j) d")).then_inc(s["x_in"], 16)
                    sp.wait_ge(s["whi_done"], 2 * t)
                    sp.wait_ge(s["wlo_done"], 2 * t)
                    e = bass.ds(t, 1)
                    sp.dma_start(st[:, 0:HF], g["Wg"][e, :, :].rearrange("a d h -> d (a h)")).then_inc(s["w_in"], 16)
                    sp.dma_start(st[:, HF:2 * HF], g["W1"][e, :, :].rearrange("a d h -> d (a h)")).then_inc(s["w_in"], 16)
                    sp.dma_start(st[0:HG, 2 * HF:2 * HF + 3 * D].rearrange("p (k d) -> p k d", k=3),
                                 g["W2"][e, :, :].rearrange("a (k p) d -> p (a k) d", p=HG)).then_inc(s["w_in"], 16)
                if T:
                    sp.wait_ge(s["x1_done"], TB * (t - 1))
                    sp.dma_start(rows_t[bass.ds(t - 2, 1), :, :, 0:D].rearrange("b p j d -> p (b j) d"), x1s[:, :, :]).then_inc(s["rows_out"], 16)
                if Y:
                    if T:
                        sp.wait_ge(s["x1_done"], TB * (t - 1))
                    sp.dma_start(xres[:, :, :], x_t[bass.ds(t - 1, 1), :, :, :].rearrange("b p j d -> p (b j) d")).then_inc(s["xres_in"], 16)

            steps(sp, step)
            sp.wait_ge(s["rows_out"], 16 * B)

        @block.tensor
        def _(pe):
            pe.wait_ge(s["const_in"], 32)
            pe.wait_ge(s["raw_in"], 80)
            for i, (a, r) in enumerate(preps):
                if i == 16:
                    pe.wait_ge(s["raw3_in"], 96)
                pe.transpose(ps[0:P, i // 4, i % 4 * P:i % 4 * P + r], a, ident[0:r, 0:r]).then_inc(s["prep_mm"], 1)
            pe.wait_ge(s["prep_cp"], 10)
            pe.wait_ge(s["prep_cst"], 4)
            pe.matmul(ps[:, 6, 0:E], ones[:, :], cT2[:, :], start=True, stop=True).then_inc(s["prep_mm"], 1)
            pe.wait_ge(s["prep_cp"], 11)

            def step(t, X, Y, T):
                if X:
                    pe.wait_ge(s["x_in"], 16 * (t + 1))
                    if Y:
                        pe.wait_ge(s["vg_done"], 2 * (t - 1))
                    for h in range(2):
                        for j in range(4):
                            mm = pe.matmul(ps[:, h, j * P:(j + 1) * P], xt[:, 4 * h + j, :], fwd, start=True, stop=True)
                        mm.then_inc(s["dft_done"], 1)
                if Y:
                    if T:
                        pe.wait_ge(s["zs_done"], 2 * (t - 1))
                    for i in range(2):
                        pe.wait_ge(s["pn_done"], 2 * (t - 1) + i + 1)
                        for k in range(NKV):
                            mm = pe.transpose(ps[:, 2 + i, k * P:(k + 1) * P],
                                              Pb[:, i, 2 * k:2 * k + 2, :].rearrange("p a k -> p (a k)"), ident)
                        mm.then_inc(s["pt_done"], 1)
                if T:
                    for h in range(2):
                        if h == 0:
                            pe.wait_ge(s["x1_done"], TB * (t - 1))
                        if X:
                            pe.wait_ge(s["v_ev"], 2 * t)
                        else:
                            pe.wait_ge(s["v_ev"], 2 * B)
                        if h == 1:
                            pe.wait_ge(s["x1t_ev"], 2 * (t - 2) + 1)
                        else:
                            pe.wait_ge(s["x1t_ev"], 2 * (t - 2))
                        for j in range(4):
                            mm = pe.transpose(ps[:, 7, j * P:(j + 1) * P], x1s[:, 4 * h + j, :], ident)
                        mm.then_inc(s["t_done"], 1)
                if X:
                    pe.wait_ge(s["xl_done"], 4 * (t + 1))
                    if Y:
                        pe.wait_ge(s["sub_done"], 2 * t)
                        pe.wait_ge(s["exp_done"], 2 * t)
                    for n in range(NHP):
                        mm = pe.matmul(ps[:, 4 + n // 4, n % 4 * P:(n % 4 + 1) * P], qwT[:, n * P:(n + 1) * P],
                                       XL[:, :, 0, :], start=True, stop=True)
                        if n % 4 == 3:
                            mm.then_inc(s["proj_done"], 1)
                    if Y:
                        pe.wait_ge(s["al_done"], t - 1)
                        pe.wait_ge(s["tan_done"], t)
                        if T:
                            pe.wait_ge(s["lg_ev"], t - 2)
                    if Y:
                        pe.wait_ge(s["xln_ev"], t)
                    for k in range(NKV):
                        mm = pe.matmul(ps[:, 6, k * P:(k + 1) * P], kwT[:, k, :, :].rearrange("p a e -> p (a e)"),
                                       XL[:, :, 0, :], start=True, stop=True)
                    mm.then_inc(s["proj_done"], 1)
                    if T:
                        pe.wait_ge(s["x1t_ev"], 2 * (t - 1))
                    for i in range(2):
                        mm = pe.matmul(ps[:, 7, i * 256:(i + 1) * 256], XL[:, i, :, :].rearrange("p a t -> p (a t)"),
                                       vwT[:, :], start=True, stop=True)
                    mm.then_inc(s["proj_done"], 1)
                if Y:
                    for i in range(2):
                        pe.wait_ge(s["pt_ev"], 2 * (t - 1) + i + 1)
                        pe.wait_ge(s["v_ev"], 2 * t)
                        for k in range(NKV):
                            mm = pe.matmul(ps[:, 2 + i, k * P:(k + 1) * P], VB[:, i, k, :, :].rearrange("p a e -> p (a e)"),
                                           PT[:, i, k, :], start=True, stop=True)
                        mm.then_inc(s["ot_done"], 1)
                if X:
                    for i in range(2):
                        pe.wait_ge(s["q_ev"], 4 * (t + 1))
                        pe.wait_ge(s["k_ev"], t + 1)
                        pe.matmul(ps[:, 4 + i, :], mqb[:, :], mkb[:, :], start=True, stop=False)
                        for n in range(NHP):
                            mm = pe.matmul(ps[:, 4 + i, n * LT:(n + 1) * LT], QB[:, i, n, :, :].rearrange("p a t -> p (a t)"),
                                           kT[:, n // 2, i, :], start=False, stop=(n == NHP - 1))
                        mm.then_inc(s["s_done"], 1)
                if X or Y or T:
                    pe.wait_ge(s["k_ev"], (t + 1) if X else B)
                if T:
                    pe.wait_ge(s["x1t_ev"], 2 * (t - 1))
                    pe.wait_ge(s["lg_ev"], t - 2)
                    for j in range(TB):
                        mm = pe.matmul(ps[:, 6, 3 * P + j * E:3 * P + (j + 1) * E], x1T[:, j, :], cT[:, :], start=True, stop=True)
                    mm.then_inc(s["r_done"], 1)
                if Y:
                    pe.wait_ge(s["ot_ev"], 2 * t)
                    for n in range(2 * NKV):
                        mm = pe.matmul(ps[:, 6, 0:P], OT[:, n // 2, n % 2, :, :].rearrange("p i t -> p (i t)"),
                                       owT[:, n // 2, n % 2, :], start=(n == 0), stop=(n == 2 * NKV - 1))
                    mm.then_inc(s["a_done"], 1)
                    pe.wait_ge(s["gate_done"], t)
                    for h in range(2):
                        for j in range(4):
                            mm = pe.matmul(ps[:, 2 + h, j * P:(j + 1) * P], sel[:, 4 * h + j, :], gate[:, :], start=True, stop=True)
                        mm.then_inc(s["g_done"], 1)
                    pe.wait_ge(s["gelu_done"], 2 * t)
                    if X:
                        pe.wait_ge(s["xr_ev"], 2 * (t + 1))
                    for h in range(2):
                        for j in range(4):
                            for i in range(2):
                                mm = pe.matmul(ps[i * C:(i + 1) * C, h, j * P:(j + 1) * P], G[:, i, 4 * h + j, :], pwT[:, i, :],
                                               start=True, stop=True)
                        mm.then_inc(s["pw_done"], 1)
                    for h in range(2):
                        pe.wait_ge(s["g_ev"], 2 * (t - 1) + h + 1)
                        pe.wait_ge(s["vg_done"], 2 * (t - 1) + h + 1)
                        pe.matmul(ps[:, 2 + h, :], high, Vs[:, 4 * h:4 * h + 4, :].rearrange("p j d -> p (j d)"), start=True, stop=False)
                        pe.wait_ge(s["al_done"], t)
                        for j in range(4):
                            mm = pe.matmul(ps[:, 2 + h, j * P:(j + 1) * P], low[:, 4 * h + j, :], AL[:, :], start=False, stop=(j == 3))
                        mm.then_inc(s["z_done"], 1)
                if X:
                    if Y:
                        pe.wait_ge(s["al_done"], t)
                    if T:
                        pe.wait_ge(s["lg_ev"], t - 1)
                    pe.matmul(ps[0:NC, 6, P:2 * P], XL[:, 0, 0, 0:LT:LOW], pwT[:, 2, :], start=True, stop=True)
                    for i in range(2):
                        mm = pe.matmul(ps[i * LT:(i + 1) * LT, 6, 2 * P:3 * P], XL[:, i, 0, :], ident, start=True, stop=True)
                    mm.then_inc(s["xln_done"], 1)

            steps(pe, step)

        @block.scalar
        def _(act):
            act.dma_start(cs[:, :], g["cst1"]).then_inc(s["const_in"], 16)
            act.dma_start(cr[:, :], g["cst2"]).then_inc(s["const_in"], 16)
            act.dma_start(dw[:, 0, :], g["dwr"].rearrange("d a k -> d (a k)")).then_inc(s["dw_in"], 16)
            act.dma_start(dw[:, 1, :], g["dwi"].rearrange("d a k -> d (a k)")).then_inc(s["dw_in"], 16)
            act.dma_start(araw[:, :], g["alpha"].partition_broadcast(P)).then_inc(s["dw_in"], 16)
            act.wait_ge(s["dw_in"], 48)
            nc.scalar.activation(alz[:, :], araw[:, :], ACT.Tanh, scale=0.5).then_inc(s["prep_al"], 1)
            act.wait_ge(s["prep_al"], 1)
            nc.scalar.activation(al[:, :], alz[:, :], ACT.Copy, bias=0.5, scale=0.5).then_inc(s["prep_al"], 1)
            for j in range(2):
                act.wait_ge(s["prep_mm"], 4 * (j + 1))
                nc.scalar.activation(qwT[:, j * 512:(j + 1) * 512], ps[:, j, :], ACT.Copy).then_inc(s["prep_cp"], 1)
            for j in range(2):
                act.wait_ge(s["prep_mm"], 8 + 4 * (j + 1))
                nc.scalar.activation(owT[:, 2 * j:2 * j + 2, :, :].rearrange("p k h d -> p (k h d)"), ps[:, 2 + j, :],
                                     ACT.Copy).then_inc(s["prep_cp"], 1)
            act.wait_ge(s["prep_mm"], 24)
            for d in range(2):
                nc.scalar.activation(kwT[:, :, d, :], ps[:, 4, 0:256].rearrange("p (k e) -> p k e", k=NKV), ACT.Copy).then_inc(s["prep_cp"], 1)
            nc.scalar.activation(vwT[:, :], ps[:, 4, 256:512], ACT.Copy).then_inc(s["prep_cp"], 1)
            nc.scalar.activation(pwT[:, :, :].rearrange("p a d -> p (a d)"), ps[:, 5, 0:3 * D], ACT.Copy).then_inc(s["prep_cp"], 1)
            nc.scalar.activation(cT[:, :], ps[:, 5, 3 * D:3 * D + E], ACT.Copy, scale=-2.0).then_inc(s["prep_cp"], 1)
            nc.scalar.activation(cT2[:, :], ps[:, 5, 3 * D:3 * D + E], ACT.Square).then_inc(s["prep_cp"], 1)
            act.wait_ge(s["prep_mm"], 25)
            nc.scalar.activation(cn[:, :], ps[:, 6, 0:E], ACT.Copy).then_inc(s["prep_cp"], 1)

            def step(t, X, Y, T):
                if Y:
                    for i in range(2):
                        act.wait_ge(s["pt_done"], 2 * (t - 1) + i + 1)
                        if T:
                            act.wait_ge(s["ot_done"], 2 * (t - 1))
                        nc.scalar.activation(PT[:, i, :, :].rearrange("p k m -> p (k m)"), ps[:, 2 + i, :], ACT.Copy).then_inc(s["pt_ev"], 1)
                if X:
                    for h in range(2):
                        act.wait_ge(s["dft_done"], 2 * t + h + 1)
                        act.wait_ge(s["conv_done"], 2 * t)
                        nc.scalar.activation(XF[:, 8 * h:8 * h + 8, :].rearrange("p c f -> p (c f)"), ps[:, h, :], ACT.Copy).then_inc(s["xr_ev"], 1)
                if T:
                    for h in range(2):
                        act.wait_ge(s["t_done"], 2 * (t - 2) + h + 1)
                        act.wait_ge(s["r_done"], t - 2)
                        nc.scalar.activation(x1T[:, 4 * h:4 * h + 4, :].rearrange("p j m -> p (j m)"), ps[:, 7, :], ACT.Copy).then_inc(s["x1t_ev"], 1)
                if X:
                    if Y:
                        act.wait_ge(s["s_done"], 2 * t)
                    else:
                        act.wait_ge(s["prep_cst"], 4)
                    for r in range(2):
                        act.wait_ge(s["proj_done"], 4 * t + r + 1)
                        for h in range(2):
                            q0 = h * HD
                            nc.scalar.activation(QB[q0:q0 + HD, :, 4 * r:4 * r + 4, h, :].rearrange("p i n t -> p n i t"),
                                                 ps[q0:q0 + HD, 4 + r, :].rearrange("p (n i t) -> p n i t", n=4, i=2),
                                                 ACT.Copy).then_inc(s["q_ev"], 1)
                    act.wait_ge(s["proj_done"], 4 * t + 3)
                    nc.scalar.activation(kT[:, :, :, :].rearrange("p k i t -> p (k i t)"), ps[:, 6, :], ACT.Copy).then_inc(s["k_ev"], 1)
                if Y:
                    for i in range(2):
                        act.wait_ge(s["ot_done"], 2 * (t - 1) + i + 1)
                        if T:
                            act.wait_ge(s["a_done"], t - 1)
                        nc.scalar.activation(OT[:, :, :, i, :], ps[:, 2 + i, :].rearrange("p (k h t) -> p k h t", k=NKV, h=2),
                                             ACT.Copy).then_inc(s["ot_ev"], 1)
                if X:
                    act.wait_ge(s["proj_done"], 4 * t + 4)
                    for d in range(2):
                        q0 = d * HD
                        nc.scalar.activation(VB[q0:q0 + HD, :, :, d, :], ps[q0:q0 + HD, 7, :].rearrange("p (i k e) -> p i k e", i=2, k=NKV),
                                             ACT.Copy).then_inc(s["v_ev"], 1)
                if Y:
                    for h in range(2):
                        act.wait_ge(s["g_done"], 2 * (t - 1) + h + 1)
                        if T:
                            act.wait_ge(s["vg_done"], 2 * (t - 1))
                        nc.scalar.activation(Gs[:, 4 * h:4 * h + 4, :].rearrange("p j d -> p (j d)"), ps[:, 2 + h, :], ACT.Copy).then_inc(s["g_ev"], 1)
                if X:
                    for i in range(2):
                        act.wait_ge(s["sub_done"], 2 * t + i + 1)
                        nc.scalar.activation(Sb[:, i, :, :], Sb[:, i, :, :], ACT.Exp, scale=1.0 / 8).then_inc(s["exp_done"], 1)
                    for i, (y, n) in enumerate(((YR, HR), (YI, HI))):
                        act.wait_ge(s["conv_done"], 2 * t + i + 1)
                        if Y:
                            act.wait_ge(s["pw_done"], 2 * t)
                        nc.scalar.activation(G[:, i, :, 0:2 * n], y[:, :, :].rearrange("p (j c) f -> p j (c f)", c=2), ACT.Gelu).then_inc(s["gelu_done"], 1)
                    act.wait_ge(s["w_in"], 48 * (t + 1))
                    e = bass.ds(t, 1)
                    nc.scalar.activation(w13h[:, e, :].rearrange("p a h -> p (a h)"), st[:, 0:2 * HF], ACT.Copy).then_inc(s["whi_done"], 1)
                    nc.scalar.activation(w2h[:, e, :, :].rearrange("p a k d -> p (a k d)"), st[0:HG, 2 * HF:2 * HF + 3 * D],
                                         ACT.Copy).then_inc(s["whi_done"], 1)
                    act.wait_ge(s["xln_done"], t + 1)
                    nc.scalar.activation(gtan[:, :], ps[0:NC, 6, P:2 * P], ACT.Tanh, scale=0.5 / C).then_inc(s["tan_done"], 1)
                    act.wait_ge(s["tan_done"], t + 1)
                    if Y:
                        act.wait_ge(s["g_done"], 2 * t)
                    nc.scalar.activation(gate[:, :], gtan[:, :], ACT.Copy, bias=0.5, scale=0.5).then_inc(s["gate_done"], 1)
                    act.wait_ge(s["xln_done"], t + 1)
                    if Y:
                        act.wait_ge(s["al_done"], t)
                    else:
                        act.wait_ge(s["prep_al"], 2)
                    nc.scalar.activation(xln[:, :], ps[:, 6, 2 * P:3 * P], ACT.Copy, scale=al[:, 0:1]).then_inc(s["xln_ev"], 1)

            steps(act, step)

        @block.vector
        def _(dve):
            v = nc.vector
            v.memset(ones[:, :], 1.0).then_inc(s["prep_cst"], 1)
            v.memset(QB[:, :, :, :, :], 0.0).then_inc(s["prep_cst"], 1)
            v.memset(VB[:, :, :, :, :], 0.0).then_inc(s["prep_cst"], 1)
            v.memset(G[:, :, :, :], 0.0).then_inc(s["prep_cst"], 1)
            v.memset(XL[:, :, :, :], 0.0).then_inc(s["prep_cst"], 1)
            dve.wait_ge(s["const_in"], 32)
            v.tensor_copy(mqb[:, :], mq[0:NC, :]).then_inc(s["prep_cst"], 1)
            v.tensor_copy(mkb[:, :], mk[0:NC, :]).then_inc(s["prep_cst"], 1)
            dve.wait_ge(s["prep_al"], 2)
            dve.wait_ge(s["prep_cst"], 7)
            dve.wait_ge(s["prep_cp"], 11)

            def conv(t, i, first):
                y, x, n, off = ((YR, XR, HR, LOW), (YI, XI, HI, LOW - 1))[i]
                for k in range(KS):
                    m = n - k
                    src = x[:, :, off:off + m]
                    w = dw[:, i, KS - 1 - k:KS - k]
                    if k == 0:
                        if not first:
                            dve.wait_ge(s["gelu_done"], 2 * t)
                        v.tensor_scalar(y[:, :, :], src, w, None, ALU.mult).then_inc(s["conv"], 1)
                    else:
                        dve.wait_ge(s["conv"], 14 * t + 7 * i + k)
                        ins = v.scalar_tensor_tensor(out=y[:, :, k:n], in0=src, scalar=w, in1=y[:, :, k:n], op0=ALU.mult, op1=ALU.add)
                        ins.then_inc(s["conv"], 1)
                dve.wait_ge(s["conv"], 14 * t + 7 * i + 7)
                dve.sem_inc(s["conv_done"], 1)

            def step(t, X, Y, T):
                if X:
                    if Y:
                        dve.wait_ge(s["proj_done"], 4 * t)
                        dve.wait_ge(s["xln_done"], t)
                    dve.wait_ge(s["xr_ev"], 2 * (t + 1))
                    for d in range(2):
                        for i in range(2):
                            ins = v.tensor_copy(XL[:, i, d, :].rearrange("p (c f) -> p c f", f=LOW)[:, :, i:LOW],
                                                (XR, XI)[i][:, :, 0:LOW - i]).then_inc(s["xl_done"], 1)
                if T:
                    dve.wait_ge(s["rstd_done"], t - 1)
                    dve.wait_ge(s["t_done"], 2 * (t - 2))
                    dve.wait_ge(s["rows_out"], 16 * (t - 2))
                    dve.wait_ge(s["xsq_done"], t - 2)
                    for j in range(TB):
                        v.tensor_scalar(x1s[:, j, :], xres[:, j, :], mv[:, j, 0:1], y0[:, j:j + 1], ALU.subtract, ALU.mult).then_inc(s["x1_done"], 1)
                if X:
                    conv(t, 0, not Y)
                    for i in range(2):
                        dve.wait_ge(s["s_done"], 2 * t + i + 1)
                        sc = ps[:, 4 + i, :].rearrange("p (n k) -> p n k", n=NHP)
                        v.tensor_reduce(mx[:, i, :], sc, AX, ALU.max).then_inc(s["max_done"], 1)
                        dve.wait_ge(s["max_done"], 2 * t + i + 1)
                        if Y:
                            dve.wait_ge(s["pn_done"], 2 * t)
                        v.tensor_tensor(Sb[:, i, :, :], sc, mx[:, i, :].unsqueeze(2).broadcast_to((P, NHP, LT)), ALU.subtract).then_inc(s["sub_done"], 1)
                if T:
                    dve.wait_ge(s["r_done"], t - 1)
                    if Y:
                        dve.wait_ge(s["a_done"], t)
                    v.tensor_copy(lg[:, bass.ds((t - 2) * TB, TB), :].rearrange("p j e -> p (j e)"), ps[:, 6, 3 * P:3 * P + TB * E]).then_inc(s["lg_ev"], 1)
                    dve.wait_ge(s["xsq_done"], t - 1)
                    v.tensor_reduce(sq[:, bass.ds((t - 2) * TB, TB)], xsq[:, :, :], AX, ALU.add).then_inc(s["sq_done"], 1)
                if Y:
                    dve.wait_ge(s["a_done"], t)
                    if T:
                        dve.wait_ge(s["z_done"], 2 * (t - 1))
                    dve.wait_ge(s["xln_ev"], t)
                    v.scalar_tensor_tensor(out=AL[:, :], in0=ps[:, 6, 0:P], scalar=al[:, 0:1], in1=xln[:, :],
                                           op0=ALU.mult, op1=ALU.subtract).then_inc(s["al_done"], 1)
                    for h in range(2):
                        dve.wait_ge(s["pw_done"], 2 * (t - 1) + h + 1)
                        dve.wait_ge(s["g_ev"], 2 * (t - 1) + h + 1)
                        v.tensor_tensor(Vs[:, 4 * h:4 * h + 4, :].rearrange("p j d -> p (j d)"), ps[:, h, :],
                                        Gs[:, 4 * h:4 * h + 4, :].rearrange("p j d -> p (j d)"), ALU.mult).then_inc(s["vg_done"], 1)
                if X:
                    conv(t, 1, not Y)
                    for i in range(2):
                        dve.wait_ge(s["exp_done"], 2 * t + i + 1)
                        v.tensor_reduce(sm[:, i, :], Sb[:, i, :, :], AX, ALU.add).then_inc(s["sum_done"], 1)
                        dve.wait_ge(s["sum_done"], 2 * t + i + 1)
                        v.reciprocal(rs[:, i, :], sm[:, i, :]).then_inc(s["rec_done"], 1)
                    dve.wait_ge(s["whi_done"], 2 * (t + 1))
                    e = bass.ds(t, 1)
                    v.tensor_tensor(w13l[:, e, :].rearrange("p a h -> p (a h)"), st[:, 0:2 * HF],
                                    w13h[:, e, :].rearrange("p a h -> p (a h)").bitcast(F32), ALU.subtract).then_inc(s["wlo_done"], 1)
                    v.tensor_tensor(w2l[:, e, :, :].rearrange("p a k d -> p (a k d)"), st[0:HG, 2 * HF:2 * HF + 3 * D],
                                    w2h[:, e, :, :].rearrange("p a k d -> p (a k d)").bitcast(F32), ALU.subtract).then_inc(s["wlo_done"], 1)
                if Y:
                    dve.wait_ge(s["xres_in"], 16 * t)
                    if T:
                        dve.wait_ge(s["x1_done"], TB * (t - 1))
                    for h in range(2):
                        dve.wait_ge(s["z_done"], 2 * (t - 1) + h + 1)
                        xr = xres[:, 4 * h:4 * h + 4, :].rearrange("p j d -> p (j d)")
                        v.scalar_tensor_tensor(out=xr, in0=xr, scalar=2.0, in1=ps[:, 2 + h, :], op0=ALU.mult, op1=ALU.add).then_inc(s["zs_done"], 1)
                    for j in range(TB):
                        if j % 4 == 0:
                            dve.wait_ge(s["zs_done"], 2 * (t - 1) + j // 4 + 1)
                        v.bn_stats(bn[:, j, :], xres[:, j, :]).then_inc(s["bn_done"], 1)
                    dve.wait_ge(s["bn_done"], TB * t)
                    dve.sem_inc(s["bn_seen"], 1)
                    for j in range(TB):
                        v.bn_aggr(mv[:, j, :], bn[:, j, :]).then_inc(s["mv_done"], 1)
                    dve.wait_ge(s["mv_done"], TB * t)
                    v.tensor_scalar(vh[:, :], mv[:, :, 1], EPS, None, ALU.add).then_inc(s["seed_done"], 1)
                    dve.wait_ge(s["seed_done"], 4 * (t - 1) + 1)
                    v.tensor_scalar(ya[:, :].bitcast(I32), vh[:, :].bitcast(I32), 1, None, ALU.arith_shift_right).then_inc(s["seed_done"], 1)
                    dve.wait_ge(s["seed_done"], 4 * (t - 1) + 2)
                    v.tensor_scalar(y0[:, :].bitcast(I32), ya[:, :].bitcast(I32), -1, MAGIC, ALU.mult, ALU.add).then_inc(s["seed_done"], 1)
                    v.tensor_scalar(vh[:, :], vh[:, :], 0.5, None, ALU.mult).then_inc(s["seed_done"], 1)

            steps(dve, step)

        @block.gpsimd
        def _(pool):
            v = nc.gpsimd
            v.memset(c15[:, :], 1.5).then_inc(s["c15_done"], 1)
            pool.wait_ge(s["c15_done"], 1)

            def step(t, X, Y, T):
                if T:
                    pool.wait_ge(s["x1_done"], TB * (t - 1))
                    pool.wait_ge(s["sq_done"], t - 2)
                    v.tensor_tensor(xsq[:, :, :], x1s[:, :, :], x1s[:, :, :], ALU.mult).then_inc(s["xsq_done"], 1)
                if X:
                    for i in range(2):
                        pool.wait_ge(s["rec_done"], 2 * t + i + 1)
                        if Y:
                            pool.wait_ge(s["pt_done"], 2 * t)
                        v.tensor_tensor(Pb[:, i, :, :], Sb[:, i, :, :], rs[:, i, :].unsqueeze(2).broadcast_to((P, NHP, LT)), ALU.mult).then_inc(s["pn_done"], 1)
                if Y:
                    pool.wait_ge(s["seed_done"], 4 * t)
                    for n in range(3):
                        v.tensor_tensor(ya[:, :], y0[:, :], y0[:, :], ALU.mult).then_inc(s["newton"], 1)
                        pool.wait_ge(s["newton"], 12 * (t - 1) + 4 * n + 1)
                        v.tensor_tensor(yb[:, :], ya[:, :], vh[:, :], ALU.mult).then_inc(s["newton"], 1)
                        pool.wait_ge(s["newton"], 12 * (t - 1) + 4 * n + 2)
                        v.tensor_tensor(yb[:, :], c15[:, :], yb[:, :], ALU.subtract).then_inc(s["newton"], 1)
                        pool.wait_ge(s["newton"], 12 * (t - 1) + 4 * n + 3)
                        ins = v.tensor_tensor(y0[:, :], y0[:, :], yb[:, :], ALU.mult).then_inc(s["newton"], 1)
                        pool.wait_ge(s["newton"], 12 * (t - 1) + 4 * n + 4)
                    pool.sem_inc(s["rstd_done"], 1)

            steps(pool, step)



def phase2(nc, g):
    route(nc, g)
    experts(nc, g)


def route(nc, g):
    ps, cr, ident, c2, lg, sq, cn, rows_t, idx, tab = (g[k] for k in ("ps", "cr", "ident", "c2", "lg", "sq", "cn", "rows_t", "idx", "tab"))
    order = pair_order()
    NP = len(order)
    with ExitStack() as ctx:
        def sb(name, shape, dt=F32):
            return ctx.enter_context(nc.sbuf_tensor(name, shape, dt))

        def sem(name):
            return ctx.enter_context(nc.semaphore("rt_" + name))

        def con(name, rows=P):
            return cr[0:rows, c2[name][0]:c2[name][1]]

        full = [P, NT, E]
        dist = sb("dist", full)
        eq = sb("eq", full)
        oh1 = sb("oh1", full)
        oh2 = sb("oh2", full)
        we = sb("we", full)
        m1, m2, km, s1, s2, df, ew, dn, w1, w2 = (sb("r_" + n, [P, NT]) for n in ("m1", "m2", "km", "s1", "s2", "df", "ew", "dn", "w1", "w2"))
        maskT = sb("maskT", [P, E, NT], BF16)
        OH = sb("OH", [P, NP * NT], BF16)
        onesf = sb("onesf", [P, 448])
        onesb = sb("onesb", [P, P], BF16)
        trimb = sb("trimb", [P, P], BF16)
        iob = sb("iob", [P, P], BF16)
        zb = sb("zb", [P, P], BF16)
        csum = sb("csum", [P, NP * NT])
        posm = sb("posm", [P, NP * NT])
        pos = sb("pos", [P, NT])
        posi = sb("posi", [P, NT], I32)
        hii = sb("hii", [P, NT], I32)
        hif = sb("hif", [P, NT])
        lof = sb("lof", [P, NT])
        lohot = sb("lohot", [P, NT, P], BF16)
        hihot = sb("hihot", [P, NT, 2, NT], BF16)
        inv = sb("inv", [P, 2 * NT])
        En = sb("En", [NT, NP])
        Sn = sb("Sn", [NT, NP])
        pr = sb("pr", [NT, NP])
        pb = sb("pb", [NT, NP])
        prT = sb("prT", [NP, NT])
        need = sb("need", [NT, E])
        cexc = sb("cexc", [NT, E])
        ubase = sb("ubase", [NT, 1])
        uinc = sb("uinc", [NT, E])
        upos = sb("upos", [NT, E])
        uhot = sb("uhot", [NT, E, UPAD], BF16)
        ulhs = sb("ulhs", [NT, E, 3], BF16)
        onese = sb("onese", [NT, E])
        s_d, s_w, s_oh, s_mm, s_hot, s_inv, s_pr, s_prc, s_nd, s_cx, s_sq, s_ex, s_we, s_wd, s_df, s_rank, s_u, s_tab = (
            sem(n) for n in ("chain", "w", "onehot", "ranks", "hot", "inverse", "present", "present_copy", "need", "before", "sqrt", "exp",
                             "weights", "weights_out", "difference", "rank_read", "units", "table"))
        assert NP * NT == 4 * 448

        block = ctx.enter_context(nc.Block())

        @block.vector
        def _(dve):
            v = nc.vector
            n = [0]

            def link(ins):
                n[0] += 1
                ins.then_inc(s_d, 1)
                dve.wait_ge(s_d, n[0])

            def over_e(a):
                return a.unsqueeze(2).broadcast_to((P, NT, E))

            def over_t(a):
                return a.unsqueeze(1).broadcast_to((P, NT, E))

            v.memset(onesf[:, :], 1.0)
            v.memset(onesb[:, :], 1.0)
            v.memset(onese[:, :], 1.0)
            v.memset(zb[:, :], 0.0)
            v.tensor_copy(trimb[:, :], con("trim"))
            v.tensor_copy(iob[:, :], con("iota"))
            link(v.tensor_tensor(dist[:, :, :], lg[:, :, :], over_t(cn[:, :]), ALU.add))
            link(v.tensor_tensor(dist[:, :, :], dist[:, :, :], over_e(sq[:, :]), ALU.add))
            link(v.tensor_scalar(dist[:, :, :], dist[:, :, :], 1e-12, None, ALU.max))
            for m, oh in ((m1, oh1), (m2, oh2)):
                link(v.tensor_reduce(m[:, :], dist[:, :, :], AX, ALU.max))
                link(v.tensor_tensor(eq[:, :, :], dist[:, :, :], over_e(m[:, :]), ALU.is_equal))
                link(v.tensor_tensor(eq[:, :, :], eq[:, :, :], over_t(con("rev")), ALU.mult))
                link(v.tensor_reduce(km[:, :], eq[:, :, :], AX, ALU.max))
                link(v.tensor_tensor(oh[:, :, :], eq[:, :, :], over_e(km[:, :]), ALU.is_equal))
                if m is m1:
                    link(v.scalar_tensor_tensor(out=dist[:, :, :], in0=oh[:, :, :], scalar=-BIG, in1=dist[:, :, :], op0=ALU.mult, op1=ALU.add))
            v.sem_inc(s_w, 1)
            link(v.tensor_tensor(maskT[:, :, :].rearrange("p e t -> p t e"), oh1[:, :, :], oh2[:, :, :], ALU.add))
            at = 0
            for a in range(E - 1):
                w = E - 1 - a
                if a % 2 == 0:
                    ins = v.tensor_tensor(OH[:, at * NT:(at + w) * NT].rearrange("p (b t) -> p b t", b=w),
                                          maskT[:, a:a + 1, :].broadcast_to((P, w, NT)), maskT[:, a + 1:E, :], ALU.mult)
                else:
                    for k in range(w):
                        ins = v.tensor_tensor(OH[:, (at + k) * NT:(at + k + 1) * NT], maskT[:, a, :], maskT[:, E - 1 - k, :], ALU.mult)
                at += w
            ins.then_inc(s_oh, 1)
            dve.wait_ge(s_sq, 2)
            v.tensor_tensor(df[:, :], s2[:, :], s1[:, :], ALU.subtract).then_inc(s_df, 1)
            dve.wait_ge(s_mm, 2)
            for c in range(4):
                link(v.tensor_tensor_scan(csum[:, c * 448:(c + 1) * 448], onesf[:, :], ps[:, 4 + c, 0:448],
                                          0.0 if c == 0 else csum[:, c * 448 - 1:c * 448], ALU.mult, ALU.add))
            v.memset(Sn[:, 0:1], 0.0)
            cv = csum[0:NT, :].rearrange("p (a t) -> p a t", t=NT)
            v.tensor_copy(Sn[:, 1:NP], cv[:, 0:NP - 1, NT - 1])
            link(v.tensor_copy(En[:, :], cv[:, :, NT - 1]))
            link(v.tensor_scalar(pr[:, :], Sn[:, :], con("tend", NT), None, ALU.is_lt))
            link(v.scalar_tensor_tensor(out=pr[:, :], in0=En[:, :], scalar=con("tstart", NT), in1=pr[:, :], op0=ALU.is_gt, op1=ALU.mult))
            link(v.tensor_tensor(pb[:, :], En[:, :], Sn[:, :], ALU.is_gt))
            v.tensor_tensor(pr[:, :], pr[:, :], pb[:, :], ALU.mult).then_inc(s_pr, 1)
            for c in range(4):
                ins = v.tensor_tensor(posm[:, c * 448:(c + 1) * 448], csum[:, c * 448:(c + 1) * 448], ps[:, c, 0:448], ALU.add)
            link(ins)
            link(v.tensor_tensor(posm[:, :], posm[:, :], OH[:, :], ALU.mult))
            link(v.tensor_reduce(pos[:, :], posm[:, :].rearrange("p (a t) -> p t a", t=NT), AX, ALU.add))
            link(v.tensor_copy(posi[:, :], pos[:, :]))
            link(v.tensor_scalar(hii[:, :], posi[:, :], 7, None, ALU.arith_shift_right))
            link(v.tensor_copy(hif[:, :], hii[:, :]))
            link(v.scalar_tensor_tensor(out=lof[:, :], in0=hif[:, :], scalar=-float(P), in1=pos[:, :], op0=ALU.mult, op1=ALU.add))
            dve.wait_ge(s_prc, 1)
            link(v.tensor_copy(prT[:, :], ps[0:NP, 4, 0:NT]))
            v.sem_inc(s_nd, 1)
            dve.wait_ge(s_prc, 2)
            link(v.tensor_scalar(need[:, :], ps[0:NT, 5, 0:E], 0.0, None, ALU.is_gt))
            v.sem_inc(s_nd, 1)
            with dve.Fori(0, NT) as t:
                one = bass.ds(t, 1)
                v.tensor_scalar(lohot[:, one, :].rearrange("p a m -> p (a m)"), iob[:, :], lof[:, one], None, ALU.is_equal)
                v.tensor_scalar(hihot[:, one, 0, :].rearrange("p a m -> p (a m)"), iob[:, 0:NT], hif[:, one], con("part"), ALU.is_equal, ALU.mult)
                v.tensor_scalar(hihot[:, one, 1, :].rearrange("p a m -> p (a m)"), iob[:, 0:NT], hif[:, one], con("iota")[:, one], ALU.is_equal, ALU.mult).then_inc(s_hot, 1)
            dve.wait_ge(s_prc, 3)
            link(v.tensor_reduce(ubase[:, :], ps[0:NT, 6, 0:E], AX, ALU.add))
            link(v.tensor_tensor_scan(uinc[:, :], onese[:, :], need[:, :], ubase[:, 0:1], ALU.mult, ALU.add))
            link(v.tensor_tensor(upos[:, :], uinc[:, :], need[:, :], ALU.mult))
            link(v.tensor_scalar(upos[:, :], upos[:, :], -1.0, None, ALU.add))
            for e in range(E):
                v.tensor_scalar(uhot[:, e, :], con("unit", NT), upos[:, e:e + 1], None, ALU.is_equal)
            v.tensor_copy(ulhs[:, :, 0], con("part", NT).broadcast_to((NT, E)))
            v.tensor_copy(ulhs[:, :, 1], con("ev", NT))
            v.tensor_scalar(ulhs[:, :, 2], con("ev", NT), -float(E), None, ALU.add).then_inc(s_u, 1)
            dve.wait_ge(s_ex, 1)
            link(v.tensor_scalar(dn[:, :], ew[:, :], 1.0, None, ALU.add))
            link(v.reciprocal(w1[:, :], dn[:, :]))
            link(v.tensor_tensor(w2[:, :], w1[:, :], ew[:, :], ALU.mult))
            link(v.tensor_tensor(we[:, :, :], oh1[:, :, :], over_e(w1[:, :]), ALU.mult))
            link(v.tensor_tensor(eq[:, :, :], oh2[:, :, :], over_e(w2[:, :]), ALU.mult))
            v.tensor_tensor(we[:, :, :], we[:, :, :], eq[:, :, :], ALU.add).then_inc(s_we, 1)
            dve.wait_ge(s_inv, 1)
            link(v.tensor_copy(inv[:, :], ps[:, 0, 0:2 * NT]))
            link(v.scalar_tensor_tensor(out=idx[:, :], in0=inv[:, NT:], scalar=float(P), in1=inv[:, 0:NT], op0=ALU.mult, op1=ALU.add))
            dve.wait_ge(s_tab, 1)
            v.tensor_scalar(tab[:, :], ps[0:3, 7, 0:UPAD], con("off", 3), None, ALU.add)

        @block.scalar
        def _(act):
            act.wait_ge(s_w, 1)
            nc.scalar.activation(s1[:, :], m1[:, :], ACT.Sqrt).then_inc(s_sq, 1)
            nc.scalar.activation(s2[:, :], m2[:, :], ACT.Sqrt).then_inc(s_sq, 1)
            act.wait_ge(s_df, 1)
            nc.scalar.activation(ew[:, :], df[:, :], ACT.Exp).then_inc(s_ex, 1)

        @block.tensor
        def _(pe):
            pe.wait_ge(s_oh, 1)
            for w, b in ((trimb, 0), (onesb, 4)):
                for c in range(4):
                    mm = pe.matmul(ps[:, b + c, 0:448], w[:, :], OH[:, c * 448:(c + 1) * 448], start=True, stop=True)
                mm.then_inc(s_mm, 1)
            pe.wait_ge(s_pr, 1)
            pe.transpose(ps[0:NP, 4, 0:NT], pr[:, :], ident[0:NT, 0:NT]).then_inc(s_prc, 1)
            pe.wait_ge(s_nd, 1)
            pe.matmul(ps[0:NT, 5, 0:E], prT[:, :], con("inc", NP), start=True, stop=True).then_inc(s_prc, 1)
            pe.wait_ge(s_nd, 2)
            pe.matmul(ps[0:NT, 6, 0:E], con("tri", NT)[:, 0:NT], need[:, :], start=True, stop=True).then_inc(s_prc, 1)
            pe.matmul(ps[:, 0, 0:2 * NT], zb[:, :], zb[:, :], start=True, stop=False)
            with pe.Fori(0, NT) as t:
                one = bass.ds(t, 1)
                pe.wait_ge(s_hot, t + 1)
                pe.matmul(ps[:, 0, 0:2 * NT], lohot[:, one, :].rearrange("p a m -> p (a m)"),
                          hihot[:, one, :, :].rearrange("p a b m -> p (a b m)"), start=False, stop=False)
            pe.matmul(ps[:, 0, 0:2 * NT], zb[:, :], zb[:, :], start=False, stop=True).then_inc(s_inv, 1)
            pe.wait_ge(s_u, 1)
            for e in range(E):
                mm = pe.matmul(ps[0:3, 7, 0:UPAD], ulhs[:, e, :], uhot[:, e, :], start=(e == 0), stop=(e == E - 1))
            mm.then_inc(s_tab, 1)

        @block.sync
        def _(sp):
            sp.wait_ge(s_we, 1)
            for b in range(B):
                sp.dma_start(rows_t[b][:, :, D:RD], we[:, b * TB:(b + 1) * TB, :]).then_inc(s_wd, 16)
            sp.wait_ge(s_wd, 16 * B)


def experts(nc, g):
    ps, cr, ident, idx, tab, rows, out = (g[k] for k in ("ps", "cr", "ident", "idx", "tab", "rows_dram", "out"))
    w13h, w13l, w2h, w2l = (g[k] for k in ("w13h", "w13l", "w2h", "w2l"))
    out_rows = out.rearrange("b s d -> (b s) d")
    with ExitStack() as ctx:
        def sb(name, shape, dt=F32):
            return ctx.enter_context(nc.sbuf_tensor(name, shape, dt))

        bias = sb("bias", [P, E, 2, HF])
        xT = sb("xT", [P, NT, P])
        xs = sb("xs", [P, NT, ROW])
        xg = sb("xg", [P, 2, RD])
        gi = sb("gi", [P, 2], U32)
        si = sb("si", [P, 2], U32)
        xh = sb("xh", [P, 2, 2, P], F32R)
        xl = sb("xl", [P, 2, 2, P], F32R)
        gu = sb("gu", [P, 2, 2, HF])
        sg = sb("sg", [P, 2, HF])
        h = sb("h", [P, 2, HF])
        hh = sb("hh", [HG, 2, 3, P], F32R)
        hl = sb("hl", [HG, 2, 3, P], F32R)
        b2raw = sb("b2raw", [1, E, D])
        b2h = sb("b2h", [1, E, D], F32R)
        b2l = sb("b2l", [1, E, D], F32R)
        one1f = sb("one1f", [1, P])
        one1 = sb("one1", [1, P], F32R)
        ys = sb("ys", [P, 2, D])
        bn = sb("bn2", [P, 6])
        mv = sb("mv2", [P, 2])
        va, vh, ya, yb, y0 = (sb(k + "2", [P, 1]) for k in ("va", "vh", "ya", "yb", "y0"))
        s = {k: ctx.enter_context(nc.semaphore("e_" + k)) for k in (
            "bias_in", "prep", "dma_turn", "gi_done", "gat0", "gat1", "si_done", "sca0", "sca1",
            "t_done", "xT_done", "xs_done", "xh_done", "xl_done", "a_done", "gu_done", "sg_done", "h_done",
            "b_done", "hh_done", "hl_done", "c_done", "acc_done", "bn_done", "norm", "ys_done")}
        gat, sca = (s["gat0"], s["gat1"]), (s["sca0"], s["sca1"])

        FL = LAGF + 7
        LAST = NT + FL

        def flags(t):
            return (t < NT, 2 <= t < NT + 2, 3 <= t < ITER + 3, 4 <= t < ITER + 4, 5 <= t < ITER + 5, 6 <= t < ITER + 6, FL <= t < NT + FL,
                    t > 6, t > FL + 1)

        def steps(eng, step):
            t = 0
            while t < LAST:
                f, m = flags(t), 1
                while t + m < LAST and flags(t + m) == f:
                    m += 1
                if m >= 4:
                    with eng.Fori(0, m // 2) as i:
                        for k in range(2):
                            step(2 * i + (t + k), lambda c, k=k: i + (t + k - c) // 2, (t + k) % 2, *f[:7])
                for k in range(m - m % 2 if m >= 4 else 0, m):
                    step(t + k, lambda c, k=k: (t + k - c) // 2, (t + k) % 2, *f[:7])
                t += m

        block = ctx.enter_context(nc.Block())

        @block.sync
        def _(sp):
            sp.dma_start(bias[:, :, 0, :], g["bg"].partition_broadcast(P)).then_inc(s["bias_in"], 16)
            sp.dma_start(bias[:, :, 1, :], g["b1"].partition_broadcast(P)).then_inc(s["bias_in"], 16)
            sp.dma_start(b2raw[:, :, :], g["b2"].unsqueeze(0)).then_inc(s["bias_in"], 16)

        @block.gpsimd
        def _(pool):
            v = nc.gpsimd
            v.memset(xs[:, :, RD:ROW], 0.0).then_inc(s["prep"], 1)

            def step(t, half, par, G, T, X, A, Bf, Cf, F):
                if G:
                    if T:
                        pool.wait_ge(s["xs_done"], t - 1)
                        pool.wait_ge(s["t_done"], t - 1)
                    v.tensor_copy(gi[:, par:par + 1], idx[:, bass.ds(t, 1)]).then_inc(s["gi_done"], 1)
                    pool.wait_ge(s["gi_done"], t + 1)
                    pool.sem_inc(s["dma_turn"], 1)
                    v.indirect_dma_start(xg[:, par, :], None, rows, bass.IndirectOffsetOnAxis(gi[:, par:par + 1], 0)).then_inc(gat[par], 16)
                if A:
                    for u in range(2):
                        n = 2 * (t - 4) + u
                        pool.wait_ge(s["sg_done"], n + 1)
                        if Bf:
                            pool.wait_ge(s["b_done"], n - 1)
                        v.tensor_tensor(h[:, u, :], gu[:, u, 1, :], sg[:, u, :], ALU.mult).then_inc(s["h_done"], 1)
                if F:
                    k, kp = t - FL, (par + FL) % 2
                    pool.wait_ge(sca[kp], 16 * half(FL))
                    v.tensor_copy(si[:, kp:kp + 1], idx[:, bass.ds(k, 1)]).then_inc(s["si_done"], 1)
                    pool.wait_ge(s["si_done"], k + 1)
                    pool.wait_ge(s["ys_done"], k + 1)
                    pool.sem_inc(s["dma_turn"], 1)
                    v.indirect_dma_start(out_rows, bass.IndirectOffsetOnAxis(si[:, kp:kp + 1], 0), ys[:, kp, :], None).then_inc(sca[kp], 16)

            steps(pool, step)
            pool.wait_ge(sca[0], 16 * NT // 2)
            pool.wait_ge(sca[1], 16 * NT // 2)

        @block.tensor
        def _(pe):
            def down(t, u):
                n = 2 * (t - 6) + u
                e = pe.value_load(tab[1:2, bass.ds(n, 1)], min_val=0, max_val=E - 1)
                one = bass.ds(e, 1)
                pe.wait_ge(s["hl_done"], n + 1)
                pe.wait_ge(s["acc_done"], n)
                first = True
                for k in range(3):
                    for a, w in ((hh, w2h), (hl, w2h), (hh, w2l)):
                        pe.matmul(ps[:, 6, 0:D], a[:, u, k, :], w[:, one, k, :].rearrange("p a d -> p (a d)"), start=first, stop=False)
                        first = False
                pe.matmul(ps[:, 6, 0:D], one1[:, :], b2h[:, one, :].rearrange("p a d -> p (a d)"), start=False, stop=False)
                pe.matmul(ps[:, 6, 0:D], one1[:, :], b2l[:, one, :].rearrange("p a d -> p (a d)"), start=False, stop=True).then_inc(s["c_done"], 1)

            def turn(t, u, Cf):
                n = 2 * (t - 5) + u
                pe.wait_ge(s["h_done"], n + 1)
                if Cf:
                    pe.wait_ge(s["hl_done"], n - 1)
                for k in range(3):
                    mm = pe.transpose(ps[0:HG, 4 + u, k * P:(k + 1) * P], h[:, u, k * HG:(k + 1) * HG], ident)
                mm.then_inc(s["b_done"], 1)

            def up(t, u, par, Bf):
                n = 2 * (t - 4) + u
                e = pe.value_load(tab[1:2, bass.ds(n, 1)], min_val=0, max_val=E - 1)
                one = bass.ds(e, 1)
                pe.wait_ge(s["xl_done"], n + 1)
                if Bf:
                    pe.wait_ge(s["gu_done"], n - 1)
                for w in range(2):
                    for k, (a, b) in enumerate(((xh, w13h), (xl, w13h), (xh, w13l))):
                        mm = pe.matmul(ps[:, 2 * u + w, 0:HF], a[:, 1 - par, u, :],
                                       b[:, one, w * HF:(w + 1) * HF].rearrange("p a h -> p (a h)"), start=(k == 0), stop=(k == 2))
                mm.then_inc(s["a_done"], 1)

            def step(t, half, par, G, T, X, A, Bf, Cf, F):
                if T:
                    pe.wait_ge(gat[par], 16 * half(0))
                    pe.wait_ge(s["xT_done"], t - 2)
                    pe.transpose(ps[:, 7, 0:P], xg[:, par, 0:D], ident).then_inc(s["t_done"], 1)
                for u in range(2):
                    if Cf:
                        down(t, u)
                    if Bf:
                        turn(t, u, Cf)
                    if A:
                        up(t, u, par, Bf)

            pe.wait_ge(s["prep"], 5)
            steps(pe, step)

        @block.scalar
        def _(act):
            def step(t, half, par, G, T, X, A, Bf, Cf, F):
                if T:
                    act.wait_ge(s["t_done"], t - 1)
                    nc.scalar.activation(xT[:, bass.ds(t - 2, 1), :].rearrange("p a m -> p (a m)"), ps[:, 7, 0:P], ACT.Copy).then_inc(s["xT_done"], 1)
                for u in range(2):
                    if Bf:
                        act.wait_ge(s["b_done"], 2 * (t - 5) + u + 1)
                        nc.scalar.activation(hh[:, u, :, :].rearrange("p k m -> p (k m)"), ps[0:HG, 4 + u, 0:3 * P], ACT.Copy).then_inc(s["hh_done"], 1)
                    if A:
                        n = 2 * (t - 4) + u
                        act.wait_ge(s["gu_done"], n + 1)
                        if Bf:
                            act.wait_ge(s["h_done"], n - 1)
                        nc.scalar.activation(sg[:, u, :], gu[:, u, 0, :], ACT.Silu).then_inc(s["sg_done"], 1)
                if X:
                    for u in range(2):
                        n = 2 * (t - 3) + u
                        k = act.value_load(tab[0:1, bass.ds(n, 1)], min_val=0, max_val=NT - 1)
                        act.wait_ge(s["xT_done"], (t - 2) if T else NT)
                        if A:
                            act.wait_ge(s["a_done"], 2 * (t - 4))
                        nc.scalar.activation(xh[:, par, u, :], xT[:, bass.ds(k, 1), :].rearrange("p a m -> p (a m)"), ACT.Copy).then_inc(s["xh_done"], 1)

            steps(act, step)

        @block.vector
        def _(dve):
            v = nc.vector
            v.memset(one1f[:, :], 1.0).then_inc(s["norm"], 1)
            dve.wait_ge(s["norm"], 1)
            dve.wait_ge(s["bias_in"], 48)
            v.tensor_copy(one1[:, :], one1f[:, :]).then_inc(s["prep"], 1)
            v.tensor_copy(b2h[:, :, :], b2raw[:, :, :]).then_inc(s["norm"], 1)
            dve.wait_ge(s["norm"], 2)
            v.tensor_tensor(b2l[:, :, :], b2raw[:, :, :], b2h[:, :, :].bitcast(F32), ALU.subtract).then_inc(s["prep"], 3)

            def norm(t, n, ins):
                ins.then_inc(s["norm"], 1)
                dve.wait_ge(s["norm"], 12 * (t - FL) + n + 2)

            def step(t, half, par, G, T, X, A, Bf, Cf, F):
                if T:
                    dve.wait_ge(gat[par], 16 * half(0))
                    v.tensor_copy(xs[:, bass.ds(t - 2, 1), 0:RD].rearrange("p a m -> p (a m)"), xg[:, par, :]).then_inc(s["xs_done"], 1)
                for u in range(2):
                    if Cf:
                        n = 2 * (t - 6) + u
                        k = dve.value_load(tab[0:1, bass.ds(n, 1)], min_val=0, max_val=NT - 1)
                        c = dve.value_load(tab[2:3, bass.ds(n, 1)], min_val=0, max_val=E)
                        one = bass.ds(k, 1)
                        dve.wait_ge(s["xs_done"], (t - 5) if T else NT)
                        dve.wait_ge(s["acc_done"], n)
                        dve.wait_ge(s["c_done"], n + 1)
                        row = xs[:, one, 0:D].rearrange("p a m -> p (a m)")
                        v.scalar_tensor_tensor(out=row, in0=ps[:, 6, 0:D], scalar=xs[:, one, bass.ds(c + D, 1)].rearrange("p a m -> p (a m)"), in1=row,
                                               op0=ALU.mult, op1=ALU.add).then_inc(s["acc_done"], 1)
                    if Bf:
                        n = 2 * (t - 5) + u
                        dve.wait_ge(s["hh_done"], n + 1)
                        v.tensor_tensor(hl[:, u, :, :].rearrange("p k m -> p (k m)"), ps[0:HG, 4 + u, 0:3 * P],
                                        hh[:, u, :, :].rearrange("p k m -> p (k m)").bitcast(F32), ALU.subtract).then_inc(s["hl_done"], 1)
                    if A:
                        n = 2 * (t - 4) + u
                        e = dve.value_load(tab[1:2, bass.ds(n, 1)], min_val=0, max_val=E - 1)
                        if Bf:
                            dve.wait_ge(s["h_done"], n - 1)
                        dve.wait_ge(s["a_done"], n + 1)
                        v.tensor_tensor(gu[:, u, :, :], ps[:, 2 * u:2 * u + 2, 0:HF],
                                        bias[:, bass.ds(e, 1), :, :].rearrange("p a w h -> p (a w) h"), ALU.add).then_inc(s["gu_done"], 1)
                if X:
                    for u in range(2):
                        n = 2 * (t - 3) + u
                        k = dve.value_load(tab[0:1, bass.ds(n, 1)], min_val=0, max_val=NT - 1)
                        dve.wait_ge(s["xh_done"], n + 1)
                        v.tensor_tensor(xl[:, par, u, :], xT[:, bass.ds(k, 1), :].rearrange("p a m -> p (a m)"),
                                        xh[:, par, u, :].bitcast(F32), ALU.subtract).then_inc(s["xl_done"], 1)
                if F:
                    kp = (par + FL) % 2
                    k = bass.ds(t - FL, 1)
                    row = xs[:, k, 0:D].rearrange("p a m -> p (a m)")
                    dve.wait_ge(s["acc_done"], 2 * (t - 6))
                    norm(t, 1, v.bn_stats(bn[:, :], row))
                    dve.sem_inc(s["bn_done"], 1)
                    norm(t, 2, v.bn_aggr(mv[:, :], bn[:, :]))
                    norm(t, 3, v.tensor_scalar(va[:, :], mv[:, 1:2], EPS, None, ALU.add))
                    norm(t, 4, v.tensor_scalar(ya[:, :].bitcast(I32), va[:, :].bitcast(I32), 1, None, ALU.arith_shift_right))
                    norm(t, 5, v.tensor_scalar(y0[:, :].bitcast(I32), ya[:, :].bitcast(I32), -1, MAGIC, ALU.mult, ALU.add))
                    norm(t, 6, v.tensor_scalar(vh[:, :], va[:, :], -0.5, None, ALU.mult))
                    for q in range(3):
                        norm(t, 7 + 2 * q, v.scalar_tensor_tensor(out=yb[:, :], in0=y0[:, :], scalar=vh[:, 0:1], in1=y0[:, :], op0=ALU.mult, op1=ALU.mult))
                        norm(t, 8 + 2 * q, v.scalar_tensor_tensor(out=y0[:, :], in0=yb[:, :], scalar=1.5, in1=y0[:, :], op0=ALU.add, op1=ALU.mult))
                    dve.wait_ge(sca[kp], 16 * half(FL))
                    v.tensor_scalar(ys[:, kp, :], row, mv[:, 0:1], y0[:, 0:1], ALU.subtract, ALU.mult).then_inc(s["ys_done"], 1)

            dve.wait_ge(s["prep"], 5)
            steps(dve, step)


_INS = ["L0_attn_hidden_states", "L0_attn_q_w", "L0_attn_k_w", "L0_attn_v_w", "L0_attn_o_w", "L0_attn_dw_r", "L0_attn_pw_r",
        "L0_attn_dw_i", "L0_attn_pw_i", "L0_attn_gate_w", "L0_attn_alpha_raw", "L0_ffn_centroid", "L0_ffn_Wg", "L0_ffn_bg",
        "L0_ffn_W1", "L0_ffn_b1", "L0_ffn_W2", "L0_ffn_b2"]
_OUTS = [((B, SEQ, D), "float32")]


def kernel(**inputs):
    import concourse.bacc as _bacc
    from concourse.bass_utils import run_bass_kernel_spmd as _run

    nc = _bacc.Bacc("TRN2", target_bir_lowering=False, num_devices=1)
    arrays, args = {}, []
    for name in _INS:
        a = np.ascontiguousarray(inputs[name])
        arrays[f"in_{name}_dram"] = a
        args.append(nc.dram_tensor(f"in_{name}_dram", a.shape, mybir.dt.from_np(a.dtype), kind="ExternalInput").ap())
    for name, a in (("tables", packed(constants())[0]), ("resident_tables", packed(resident_constants())[0])):
        arrays[name] = a
        args.append(nc.dram_tensor(name, a.shape, F32, kind="ExternalInput").ap())
    for i, (shape, dtype) in enumerate(_OUTS):
        args.append(nc.dram_tensor(f"out_{i}_dram", shape, mybir.dt.from_np(np.dtype(dtype)), kind="ExternalOutput").ap())
    program(nc, *args)
    r = _run(nc, [arrays], core_ids=[0])
    return r.results[0]["out_0_dram"]
```

```python
from contextlib import ExitStack

import numpy as np

import concourse.bass as bass
from concourse import mybir

P = 128
B, SEQ, D = 8, 1024, 128
C = 64
NC = SEQ // C
FR, FI = C // 2 + 1, C // 2
LOW = 4
HR, HI = FR - LOW, FI - LOW
KS = 7
NH, NKV, HD = 16, 4, 64
NHP = NH // 2
TB = SEQ // P
NT = B * TB
LT = NC * LOW
E, HF, TOPK = 8, 342, 2
HG = HF // 3
NPAIR = E * (E - 1) // 2
EPS = 1e-5
ROW = 144
RD = D + E
UNITS = TOPK * NT + NPAIR - 1
ITER = (UNITS + 1) // 2
LAGF = ITER - NT
UPAD = 2 * ITER
WE = 4 * HF + 6 * D
W2 = 4 * HF
FL = LAGF + 10
STEPS = NT + FL + 2

F32 = mybir.dt.float32
F32R = mybir.dt.float32r
BF16 = mybir.dt.bfloat16
U32 = mybir.dt.uint32
I32 = mybir.dt.int32
ALU = mybir.AluOpType
ACT = mybir.ActivationFunctionType
AX = mybir.AxisListType.X
BIG = 3.0e38
MAGIC = 0x5F3759DF


def pair_order():
    out = []
    for a in range(E - 1):
        rest = list(range(a + 1, E))
        out += [(a, b) for b in (rest if a % 2 == 0 else rest[::-1])]
    return out


def constants():
    n = np.arange(C)
    parts = {}
    fwd = np.zeros((P, P))
    for c in range(2):
        for f in range(FR):
            fwd[c * C + n, c * C + f] = np.cos(2 * np.pi * f * n / C)
        for f in range(1, FI):
            fwd[c * C + n, c * C + FR + f - 1] = -np.sin(2 * np.pi * f * n / C)
    parts["fwd"] = fwd
    high = np.zeros((P, P))
    for c in range(2):
        for f in range(LOW, FR):
            high[c * HR + f - LOW, c * C + n] = (2 if f < C // 2 else 1) / C * np.cos(2 * np.pi * f * n / C)
        for f in range(LOW, FI):
            high[C + c * HI + f - LOW, c * C + n] = -2 / C * np.sin(2 * np.pi * f * n / C)
    parts["high"] = high
    low = np.zeros((P, TB, P))
    for j in range(TB):
        for c in range(2):
            for f in range(LOW):
                row = (2 * j + c) * LOW + f
                low[row, j, c * C + n] = (2 if f else 1) / C * np.cos(2 * np.pi * f * n / C)
                if f:
                    low[LT + row, j, c * C + n] = -2 / C * np.sin(2 * np.pi * f * n / C)
    parts["low"] = low.reshape(P, TB * P)
    sel = np.zeros((P, TB, P))
    for j in range(TB):
        for c in range(2):
            sel[2 * j + c, j, c * HR:(c + 1) * HR] = 1
            sel[2 * j + c, j, C + c * HI:C + (c + 1) * HI] = 1
    parts["sel"] = sel.reshape(P, TB * P)
    q = np.arange(P) % C // LOW
    mq = np.zeros((P, P))
    mq[q, np.arange(P)] = 1
    parts["mq"] = mq
    mk = np.zeros((P, NHP, C))
    for c in range(NC):
        mk[c, :, (c + 1) * LOW:] = -BIG
    parts["mk"] = mk.reshape(P, NHP * C)
    return parts


def resident_constants():
    parts = {"ident": np.eye(P)}
    tri = np.triu(np.ones((P, P)), 1)
    parts["tri"] = tri
    parts["trim"] = tri - 1
    inc = np.zeros((P, E))
    for p, (a, b) in enumerate(pair_order()):
        inc[p, a] = inc[p, b] = 1
    parts["inc"] = inc
    parts["rev"] = np.tile(E - np.arange(E), (P, 1))
    parts["iota"] = np.tile(np.arange(P), (P, 1))
    parts["unit"] = np.tile(np.arange(UPAD), (P, 1))
    parts["part"] = np.arange(P)[:, None]
    parts["tstart"] = np.arange(P)[:, None] * P
    parts["tend"] = np.arange(P)[:, None] * P + P
    off = np.zeros((P, 1))
    off[2] = E
    parts["off"] = off
    parts["ev"] = np.tile(np.arange(E), (P, 1))
    return parts


def packed(parts):
    cols, at = {}, 0
    for k, v in parts.items():
        cols[k] = (at, at + v.shape[1])
        at += v.shape[1]
    return np.concatenate(list(parts.values()), axis=1).astype(np.float32), cols


def program(nc, x, qw, kw, vw, ow, dwr, pwr, dwi, pwi, gw, alpha, cent, Wg, bg, W1, b1, W2, b2, cst1, cst2, out):
    c1, c2 = packed(constants())[1], packed(resident_constants())[1]
    n1, n2 = cst1.shape[1], cst2.shape[1]
    rows_dram = nc.dram_tensor("rows_dram", (NT * P, RD), F32).ap()
    rows_t = rows_dram.rearrange("(b j p) d -> b p j d", p=P, j=TB)
    x_t = x.rearrange("b (j p) d -> b p j d", p=P)
    ctx = ExitStack()
    with ctx:
        def sb(name, shape, dt=F32, where=ctx):
            return where.enter_context(nc.sbuf_tensor(name, shape, dt))

        def sem(name):
            return ctx.enter_context(nc.semaphore(name))

        ps = ctx.enter_context(nc.psum_tensor("ps", [P, 8, 512], F32))
        cr = sb("cr", [P, n2])
        ident = cr[:, c2["ident"][0]:c2["ident"][1]]
        wts = sb("wts", [P, E, WE], F32R)
        lg = sb("lg", [P, NT, E])
        sq = sb("sq", [P, NT])
        cn = sb("cn", [P, E])

        idx = sb("idx", [P, NT], U32)
        steptab = sb("steptab", [1, STEPS, 16], I32)
        phase1(nc, locals())
        phase2(nc, locals())


def phase1(nc, g):
    ps, cr, ident, wts = (g[k] for k in ("ps", "cr", "ident", "wts"))
    lg, sq, cn, rows_t, x_t, c1 = (g[k] for k in ("lg", "sq", "cn", "rows_t", "x_t", "c1"))
    ctx = ExitStack()
    with ctx:
        def sb(name, shape, dt=F32):
            return ctx.enter_context(nc.sbuf_tensor(name, shape, dt))

        def sem(name):
            return ctx.enter_context(nc.semaphore(name))

        cs = sb("cs1", [P, g["n1"]])
        fwd, high, mq, mk = (cs[:, c1[k][0]:c1[k][1]] for k in ("fwd", "high", "mq", "mk"))
        low = cs[:, c1["low"][0]:c1["low"][1]].rearrange("p (j m) -> p j m", j=TB)
        sel = cs[0:NC, c1["sel"][0]:c1["sel"][1]].rearrange("p (j m) -> p j m", j=TB)
        mqb = sb("mqb", [NC, P], BF16)
        mkb = sb("mkb", [NC, 512], BF16)
        qwT = sb("qwT", [P, NH * HD])
        kwT = sb("kwT", [P, NKV, 2, HD])
        vwT = sb("vwT", [P, NKV * HD])
        owT = sb("owT", [P, NKV, 2, D])
        pwT = sb("pwT", [P, 3, D])
        cT = sb("cT", [P, E])
        cT2 = sb("cT2", [P, E])
        ones = sb("ones", [P, P])
        dw = sb("dw", [P, 2, KS])
        al = sb("al", [P, 1])
        alz = sb("alz", [P, 1])
        araw = sb("araw", [P, 1])
        xt = sb("xt", [P, TB, D])
        xres = sb("xres", [P, TB, D])
        x1s = sb("x1s", [P, TB, D])
        XF = sb("XF", [P, NC, C])
        XR, XI = XF[:, :, 0:FR], XF[:, :, FR:C]
        XL = sb("XL", [P, 2, 2, LT])
        YR = sb("YR", [P, NC, HR])
        YI = sb("YI", [P, NC, HI])
        G = sb("G", [P, 2, TB, C])
        QB = sb("QB", [P, 2, NHP, 2, LT])
        kT = sb("kT", [P, NKV, 2, LT])
        VB = sb("VB", [P, 2, NKV, 2, HD])
        xln = sb("xln", [P, D])
        gate = sb("gate", [NC, D])
        gtan = sb("gtan", [NC, D])
        Sb = sb("Sb", [P, 2, NHP, LT])
        Pb = sb("Pb", [P, 2, NHP, LT])
        mx = sb("mx", [P, 2, NHP])
        sm = sb("sm", [P, 2, NHP])
        rs = sb("rs", [P, 2, NHP])
        PT = sb("PT", [P, 2, NKV, P])
        OT = sb("OT", [P, NKV, 2, 2, LT])
        AL = sb("AL", [P, D])
        Gs = sb("Gs", [P, TB, D])
        Vs = sb("Vs", [P, TB, D])
        x1T = sb("x1T", [P, TB, P])
        bn = sb("bn", [P, TB, 6])
        mv = sb("mv", [P, TB, 2])
        vh = sb("vh", [P, TB])
        y0 = sb("y0", [P, TB])
        ya = sb("ya", [P, TB])
        yb = sb("yb", [P, TB])
        c15 = sb("c15", [P, TB])
        xsq = sb("xsq", [P, TB, D])
        st = sb("st", [P, 2 * HF + 3 * D])
        st2 = st[0:HG + 1, 2 * HF:2 * HF + 3 * D].rearrange("p (k d) -> p k d", k=3)
        raw = Gs[:, :, :].rearrange("p a b -> p (a b)")
        raw2 = Vs[:, :, :].rearrange("p a b -> p (a b)")
        raw3 = x1T[:, :, :].rearrange("p a b -> p (a b)")

        s = {k: sem("p1_" + k) for k in (
            "const_in", "raw_in", "raw3_in", "x_in", "xres_in", "w_in", "rows_out", "prep_mm", "prep_cp", "prep_cst", "prep_al", "dw_in",
            "dft_done", "proj_done", "s_done", "pt_done", "ot_done", "a_done", "g_done", "pw_done",
            "z_done", "t_done", "r_done", "xln_done",
            "xr_ev", "q_ev", "k_ev", "v_ev", "gelu_done", "pt_ev", "ot_ev", "exp_done", "g_ev", "gate_done", "tan_done",
            "x1t_ev", "whi_done", "xln_ev", "st_zero",
            "xl_done", "conv", "conv_done", "max_done", "sub_done", "sum_done", "rec_done", "al_done", "vg_done", "zs_done",
            "bn_done", "bn_seen", "mv_done", "seed_done", "x1_done", "lg_ev", "sq_done", "wlo_done",
            "pn_done", "c15_done", "xsq_done", "newton", "rstd_done")}

        def bank(i, n=1):
            return ps[:, i, :] if n == 1 else ps[:, i:i + n, :]

        preps = []
        qr = raw.rearrange("p (j d) -> p j d", j=8)
        owr = raw2.rearrange("p (k h a e) -> p k h a e", k=NKV, a=2, h=2)
        kvr = raw3.rearrange("p (j d) -> p j d", j=8)
        for j in range(8):
            preps.append((qr[:, j, :], P))
        for j in range(8):
            preps.append((raw2[:, j * P:(j + 1) * P], P))
        for j in range(8):
            preps.append((kvr[0:E if j == 7 else P, j, :], E if j == 7 else P))

        def steps(eng, step):
            step(0, True, False, False)
            step(1, True, True, False)
            step(2, True, True, True)
            with eng.Fori(3, B) as s_:
                step(s_, True, True, True)
            step(B, False, True, True)
            step(B + 1, False, False, True)

        block = ctx.enter_context(nc.Block())

        @block.sync
        def _(sp):
            sp.dma_start(qr, g["qw"].rearrange("(j p) d -> p j d", p=P)).then_inc(s["raw_in"], 16)
            for h in range(2):
                for a in range(2):
                    sp.dma_start(owr[:, :, h, a, :], g["ow"].rearrange("o (k a h e) -> a h o k e", k=NKV, a=2, h=2)[a, h])\
                      .then_inc(s["raw_in"], 16)
            sp.dma_start(kvr[:, 0:2, :], g["kw"].rearrange("(j p) d -> p j d", p=P)).then_inc(s["raw3_in"], 16)
            sp.dma_start(kvr[:, 2:4, :], g["vw"].rearrange("(j p) d -> p j d", p=P)).then_inc(s["raw3_in"], 16)
            sp.dma_start(kvr[:, 4, :], g["pwr"]).then_inc(s["raw3_in"], 16)
            sp.dma_start(kvr[:, 5, :], g["pwi"]).then_inc(s["raw3_in"], 16)
            sp.dma_start(kvr[:, 6, :], g["gw"]).then_inc(s["raw3_in"], 16)
            sp.dma_start(kvr[0:E, 7, :], g["cent"]).then_inc(s["raw3_in"], 16)

            def step(t, X, Y, T):
                if X:
                    sp.wait_ge(s["dft_done"], 2 * t)
                    sp.dma_start(xt[:, :, :], x_t[bass.ds(t, 1), :, :, :].rearrange("b p j d -> p (b j) d")).then_inc(s["x_in"], 16)
                    if Y:
                        sp.wait_ge(s["whi_done"], 2 * t)
                        sp.wait_ge(s["wlo_done"], 2 * t)
                    else:
                        sp.wait_ge(s["st_zero"], 1)
                    e = bass.ds(t, 1)
                    sp.dma_start(st[:, 0:HF], g["Wg"][e, :, :].rearrange("a d h -> d (a h)")).then_inc(s["w_in"], 16)
                    sp.dma_start(st[:, HF:2 * HF], g["W1"][e, :, :].rearrange("a d h -> d (a h)")).then_inc(s["w_in"], 16)
                    sp.dma_start(st2[0:HG, :, :], g["W2"][e, :, :].rearrange("a (k p) d -> p (a k) d", p=HG)).then_inc(s["w_in"], 16)
                    sp.dma_start(st2[HG:HG + 1, 0, :], g["b2"][e, :]).then_inc(s["w_in"], 16)
                if T:
                    sp.wait_ge(s["x1_done"], TB * (t - 1))
                    sp.dma_start(rows_t[bass.ds(t - 2, 1), :, :, 0:D].rearrange("b p j d -> p (b j) d"), x1s[:, :, :]).then_inc(s["rows_out"], 16)
                if Y:
                    if T:
                        sp.wait_ge(s["x1_done"], TB * (t - 1))
                    sp.dma_start(xres[:, :, :], x_t[bass.ds(t - 1, 1), :, :, :].rearrange("b p j d -> p (b j) d")).then_inc(s["xres_in"], 16)

            steps(sp, step)
            sp.wait_ge(s["rows_out"], 16 * B)

        @block.tensor
        def _(pe):
            pe.wait_ge(s["const_in"], 32)
            pe.wait_ge(s["raw_in"], 80)
            for i, (a, r) in enumerate(preps):
                if i == 16:
                    pe.wait_ge(s["raw3_in"], 96)
                pe.transpose(ps[0:P, i // 4, i % 4 * P:i % 4 * P + r], a, ident[0:r, 0:r]).then_inc(s["prep_mm"], 1)
            pe.wait_ge(s["prep_cp"], 10)
            pe.wait_ge(s["prep_cst"], 4)
            pe.matmul(ps[:, 6, 0:E], ones[:, :], cT2[:, :], start=True, stop=True).then_inc(s["prep_mm"], 1)
            pe.wait_ge(s["prep_cp"], 11)

            def step(t, X, Y, T):
                def turned(h):
                    pe.wait_ge(s["x1t_ev"], 2 * (t - 2) + h)
                    for j in range(4):
                        mm = pe.transpose(ps[:, 7, j * P:(j + 1) * P], x1s[:, 4 * h + j, :], ident)
                    mm.then_inc(s["t_done"], 1)

                if Y:
                    if T:
                        pe.wait_ge(s["zs_done"], 2 * (t - 1))
                    for i in range(2):
                        pe.wait_ge(s["pn_done"], 2 * (t - 1) + i + 1)
                        for k in range(NKV):
                            mm = pe.transpose(ps[:, 2 + i, k * P:(k + 1) * P],
                                              Pb[:, i, 2 * k:2 * k + 2, :].rearrange("p a k -> p (a k)"), ident)
                        mm.then_inc(s["pt_done"], 1)
                if X:
                    pe.wait_ge(s["x_in"], 16 * (t + 1))
                    if T:
                        pe.wait_ge(s["vg_done"], 2 * (t - 1))
                    for h in range(2):
                        for j in range(4):
                            mm = pe.matmul(ps[:, h, j * P:(j + 1) * P], xt[:, 4 * h + j, :], fwd, start=True, stop=True)
                        mm.then_inc(s["dft_done"], 1)
                if Y:
                    pe.wait_ge(s["v_ev"], 2 * t)
                    for i in range(2):
                        pe.wait_ge(s["pt_ev"], 2 * (t - 1) + i + 1)
                        for k in range(NKV):
                            mm = pe.matmul(ps[:, 2 + i, k * P:(k + 1) * P], VB[:, i, k, :, :].rearrange("p a e -> p (a e)"),
                                           PT[:, i, k, :], start=True, stop=True)
                        mm.then_inc(s["ot_done"], 1)
                if X:
                    pe.wait_ge(s["xl_done"], 4 * (t + 1))
                    if Y:
                        pe.wait_ge(s["sub_done"], 2 * t)
                    for n in range(NHP):
                        mm = pe.matmul(ps[:, 4 + n // 4, n % 4 * P:(n % 4 + 1) * P], qwT[:, n * P:(n + 1) * P],
                                       XL[:, :, 0, :], start=True, stop=True)
                        if n % 4 == 3:
                            mm.then_inc(s["proj_done"], 1)
                    if Y:
                        pe.wait_ge(s["tan_done"], t)
                        pe.wait_ge(s["xln_ev"], t)
                    for k in range(NKV):
                        mm = pe.matmul(ps[:, 6, k * P:(k + 1) * P], kwT[:, k, :, :].rearrange("p a e -> p (a e)"),
                                       XL[:, :, 0, :], start=True, stop=True)
                    mm.then_inc(s["proj_done"], 1)
                    if T:
                        pe.wait_ge(s["lg_ev"], t - 2)
                    for i in range(2):
                        mm = pe.matmul(ps[:, 7, i * 256:(i + 1) * 256], XL[:, i, :, :].rearrange("p a t -> p (a t)"),
                                       vwT[:, :], start=True, stop=True)
                    mm.then_inc(s["proj_done"], 1)
                    pe.wait_ge(s["k_ev"], t + 1)
                if Y:
                    pe.wait_ge(s["gelu_done"], 2 * t)
                    if X:
                        pe.wait_ge(s["xr_ev"], 2 * (t + 1))
                    for h in range(2):
                        for j in range(4):
                            for i in range(2):
                                mm = pe.matmul(ps[i * C:(i + 1) * C, h, j * P:(j + 1) * P], G[:, i, 4 * h + j, :], pwT[:, i, :],
                                               start=True, stop=True)
                        mm.then_inc(s["pw_done"], 1)
                if X:
                    pe.wait_ge(s["q_ev"], 4 * (t + 1))
                    for i in range(2):
                        pe.matmul(ps[:, 4 + i, :], mqb[:, :], mkb[:, :], start=True, stop=False)
                        for n in range(NHP):
                            mm = pe.matmul(ps[:, 4 + i, n * LT:(n + 1) * LT], QB[:, i, n, :, :].rearrange("p a t -> p (a t)"),
                                           kT[:, n // 2, i, :], start=False, stop=(n == NHP - 1))
                        mm.then_inc(s["s_done"], 1)
                if T:
                    pe.wait_ge(s["v_ev"], 2 * (t + 1) if X else 2 * B)
                    pe.wait_ge(s["x1_done"], TB * (t - 1))
                    turned(0)
                if Y:
                    pe.wait_ge(s["ot_ev"], 2 * t)
                    for n in range(2 * NKV):
                        mm = pe.matmul(ps[:, 6, 0:P], OT[:, n // 2, n % 2, :, :].rearrange("p i t -> p (i t)"),
                                       owT[:, n // 2, n % 2, :], start=(n == 0), stop=(n == 2 * NKV - 1))
                    mm.then_inc(s["a_done"], 1)
                if T:
                    turned(1)
                if Y:
                    pe.wait_ge(s["gate_done"], t)
                    for h in range(2):
                        for j in range(4):
                            mm = pe.matmul(ps[:, 2 + h, j * P:(j + 1) * P], sel[:, 4 * h + j, :], gate[:, :], start=True, stop=True)
                        mm.then_inc(s["g_done"], 1)
                if Y:
                    pe.wait_ge(s["al_done"], t)
                if X:
                    pe.matmul(ps[0:NC, 6, P:2 * P], XL[:, 0, 0, 0:LT:LOW], pwT[:, 2, :], start=True, stop=True)
                    for i in range(2):
                        mm = pe.matmul(ps[i * LT:(i + 1) * LT, 6, 2 * P:3 * P], XL[:, i, 0, :], ident, start=True, stop=True)
                    mm.then_inc(s["xln_done"], 1)
                if Y:
                    pe.wait_ge(s["g_ev"], 2 * t)
                    for h in range(2):
                        for j in range(4):
                            pe.matmul(ps[:, 2 + h, j * P:(j + 1) * P], low[:, 4 * h + j, :], AL[:, :], start=(j == 0), stop=False)
                        pe.wait_ge(s["vg_done"], 2 * (t - 1) + h + 1)
                        pe.matmul(ps[:, 2 + h, :], high, Vs[:, 4 * h:4 * h + 4, :].rearrange("p j d -> p (j d)"),
                                  start=False, stop=True).then_inc(s["z_done"], 1)
                if T:
                    pe.wait_ge(s["x1t_ev"], 2 * (t - 1))
                    for j in range(TB):
                        mm = pe.matmul(ps[:, 7, j * E:(j + 1) * E], x1T[:, j, :], cT[:, :], start=True, stop=True)
                    mm.then_inc(s["r_done"], 1)

            steps(pe, step)

        @block.scalar
        def _(act):
            act.dma_start(cs[:, :], g["cst1"]).then_inc(s["const_in"], 16)
            act.dma_start(cr[:, :], g["cst2"]).then_inc(s["const_in"], 16)
            act.dma_start(dw[:, 0, :], g["dwr"].rearrange("d a k -> d (a k)")).then_inc(s["dw_in"], 16)
            act.dma_start(dw[:, 1, :], g["dwi"].rearrange("d a k -> d (a k)")).then_inc(s["dw_in"], 16)
            act.dma_start(araw[:, :], g["alpha"].partition_broadcast(P)).then_inc(s["dw_in"], 16)
            act.wait_ge(s["dw_in"], 48)
            nc.scalar.activation(alz[:, :], araw[:, :], ACT.Tanh, scale=0.5).then_inc(s["prep_al"], 1)
            act.wait_ge(s["prep_al"], 1)
            nc.scalar.activation(al[:, :], alz[:, :], ACT.Copy, bias=0.5, scale=0.5).then_inc(s["prep_al"], 1)
            for j in range(2):
                act.wait_ge(s["prep_mm"], 4 * (j + 1))
                nc.scalar.activation(qwT[:, j * 512:(j + 1) * 512], ps[:, j, :], ACT.Copy).then_inc(s["prep_cp"], 1)
            for j in range(2):
                act.wait_ge(s["prep_mm"], 8 + 4 * (j + 1))
                nc.scalar.activation(owT[:, 2 * j:2 * j + 2, :, :].rearrange("p k h d -> p (k h d)"), ps[:, 2 + j, :],
                                     ACT.Copy).then_inc(s["prep_cp"], 1)
            act.wait_ge(s["prep_mm"], 24)
            for d in range(2):
                nc.scalar.activation(kwT[:, :, d, :], ps[:, 4, 0:256].rearrange("p (k e) -> p k e", k=NKV), ACT.Copy).then_inc(s["prep_cp"], 1)
            nc.scalar.activation(vwT[:, :], ps[:, 4, 256:512], ACT.Copy).then_inc(s["prep_cp"], 1)
            nc.scalar.activation(pwT[:, :, :].rearrange("p a d -> p (a d)"), ps[:, 5, 0:3 * D], ACT.Copy).then_inc(s["prep_cp"], 1)
            nc.scalar.activation(cT[:, :], ps[:, 5, 3 * D:3 * D + E], ACT.Copy, scale=-2.0).then_inc(s["prep_cp"], 1)
            nc.scalar.activation(cT2[:, :], ps[:, 5, 3 * D:3 * D + E], ACT.Square).then_inc(s["prep_cp"], 1)
            act.wait_ge(s["prep_mm"], 25)
            nc.scalar.activation(cn[:, :], ps[:, 6, 0:E], ACT.Copy).then_inc(s["prep_cp"], 1)

            def step(t, X, Y, T):
                def turned(h):
                    act.wait_ge(s["t_done"], 2 * (t - 2) + h + 1)
                    act.wait_ge(s["r_done"], t - 2)
                    nc.scalar.activation(x1T[:, 4 * h:4 * h + 4, :].rearrange("p j m -> p (j m)"), ps[:, 7, :], ACT.Copy).then_inc(s["x1t_ev"], 1)

                if Y:
                    for i in range(2):
                        act.wait_ge(s["pt_done"], 2 * (t - 1) + i + 1)
                        if T:
                            act.wait_ge(s["ot_done"], 2 * (t - 1))
                        nc.scalar.activation(PT[:, i, :, :].rearrange("p k m -> p (k m)"), ps[:, 2 + i, :], ACT.Copy).then_inc(s["pt_ev"], 1)
                if X:
                    for h in range(2):
                        act.wait_ge(s["dft_done"], 2 * t + h + 1)
                        act.wait_ge(s["conv_done"], 2 * t)
                        nc.scalar.activation(XF[:, 8 * h:8 * h + 8, :].rearrange("p c f -> p (c f)"), ps[:, h, :], ACT.Copy).then_inc(s["xr_ev"], 1)
                if Y:
                    for i in range(2):
                        act.wait_ge(s["ot_done"], 2 * (t - 1) + i + 1)
                        if T:
                            act.wait_ge(s["a_done"], t - 1)
                        nc.scalar.activation(OT[:, :, :, i, :], ps[:, 2 + i, :].rearrange("p (k h t) -> p k h t", k=NKV, h=2),
                                             ACT.Copy).then_inc(s["ot_ev"], 1)
                if X:
                    if Y:
                        act.wait_ge(s["s_done"], 2 * t)
                    else:
                        act.wait_ge(s["prep_cst"], 4)
                    for r in range(2):
                        act.wait_ge(s["proj_done"], 4 * t + r + 1)
                        for h in range(2):
                            q0 = h * HD
                            nc.scalar.activation(QB[q0:q0 + HD, :, 4 * r:4 * r + 4, h, :].rearrange("p i n t -> p n i t"),
                                                 ps[q0:q0 + HD, 4 + r, :].rearrange("p (n i t) -> p n i t", n=4, i=2),
                                                 ACT.Copy).then_inc(s["q_ev"], 1)
                    act.wait_ge(s["proj_done"], 4 * t + 3)
                    nc.scalar.activation(kT[:, :, :, :].rearrange("p k i t -> p (k i t)"), ps[:, 6, :], ACT.Copy).then_inc(s["k_ev"], 1)
                if X:
                    act.wait_ge(s["proj_done"], 4 * t + 4)
                    for d in range(2):
                        q0 = d * HD
                        nc.scalar.activation(VB[q0:q0 + HD, :, :, d, :], ps[q0:q0 + HD, 7, :].rearrange("p (i k e) -> p i k e", i=2, k=NKV),
                                             ACT.Copy).then_inc(s["v_ev"], 1)
                if X:
                    for i, (y, n) in enumerate(((YR, HR), (YI, HI))):
                        act.wait_ge(s["conv_done"], 2 * t + i + 1)
                        if Y:
                            act.wait_ge(s["pw_done"], 2 * t)
                        nc.scalar.activation(G[:, i, :, 0:2 * n], y[:, :, :].rearrange("p (j c) f -> p j (c f)", c=2), ACT.Gelu).then_inc(s["gelu_done"], 1)
                if T:
                    turned(0)
                for i in range(2):
                    if X:
                        act.wait_ge(s["sub_done"], 2 * t + i + 1)
                        nc.scalar.activation(Sb[:, i, :, :], Sb[:, i, :, :], ACT.Exp, scale=1.0 / 8).then_inc(s["exp_done"], 1)
                    if T and i == 0:
                        turned(1)
                if Y:
                    for h in range(2):
                        act.wait_ge(s["g_done"], 2 * (t - 1) + h + 1)
                        if T:
                            act.wait_ge(s["vg_done"], 2 * (t - 1))
                        nc.scalar.activation(Gs[:, 4 * h:4 * h + 4, :].rearrange("p j d -> p (j d)"), ps[:, 2 + h, :], ACT.Copy).then_inc(s["g_ev"], 1)
                if X:
                    act.wait_ge(s["w_in"], 64 * (t + 1))
                    e = bass.ds(t, 1)
                    nc.scalar.activation(wts[:, e, 0:2 * HF].rearrange("p a h -> p (a h)"), st[:, 0:2 * HF], ACT.Copy).then_inc(s["whi_done"], 1)
                    nc.scalar.activation(wts[0:HG + 1, e, W2:WE].rearrange("p a (k w d) -> p (a k) w d", k=3, w=2)[:, :, 0, :], st2[:, :, :],
                                         ACT.Copy).then_inc(s["whi_done"], 1)
                    act.wait_ge(s["xln_done"], t + 1)
                    nc.scalar.activation(gtan[:, :], ps[0:NC, 6, P:2 * P], ACT.Tanh, scale=0.5 / C).then_inc(s["tan_done"], 1)
                    act.wait_ge(s["tan_done"], t + 1)
                    if Y:
                        act.wait_ge(s["g_done"], 2 * t)
                    nc.scalar.activation(gate[:, :], gtan[:, :], ACT.Copy, bias=0.5, scale=0.5).then_inc(s["gate_done"], 1)
                    act.wait_ge(s["xln_done"], t + 1)
                    if Y:
                        act.wait_ge(s["al_done"], t)
                    else:
                        act.wait_ge(s["prep_al"], 2)
                    nc.scalar.activation(xln[:, :], ps[:, 6, 2 * P:3 * P], ACT.Copy, scale=al[:, 0:1]).then_inc(s["xln_ev"], 1)

            steps(act, step)

        @block.vector
        def _(dve):
            v = nc.vector
            v.memset(st[:, 2 * HF:], 0.0).then_inc(s["st_zero"], 1)
            v.memset(ones[:, :], 1.0).then_inc(s["prep_cst"], 1)
            v.memset(QB[:, :, :, :, :], 0.0).then_inc(s["prep_cst"], 1)
            v.memset(VB[:, :, :, :, :], 0.0).then_inc(s["prep_cst"], 1)
            v.memset(G[:, :, :, :], 0.0).then_inc(s["prep_cst"], 1)
            v.memset(XL[:, :, :, :], 0.0).then_inc(s["prep_cst"], 1)
            dve.wait_ge(s["const_in"], 32)
            v.tensor_copy(mqb[:, :], mq[0:NC, :]).then_inc(s["prep_cst"], 1)
            v.tensor_copy(mkb[:, :], mk[0:NC, :]).then_inc(s["prep_cst"], 1)
            dve.wait_ge(s["prep_al"], 2)
            dve.wait_ge(s["prep_cst"], 7)
            dve.wait_ge(s["prep_cp"], 11)

            def conv(t, i, first):
                y, x, n, off = ((YR, XR, HR, LOW), (YI, XI, HI, LOW - 1))[i]
                for k in range(KS):
                    m = n - k
                    src = x[:, :, off:off + m]
                    w = dw[:, i, KS - 1 - k:KS - k]
                    if k == 0:
                        if not first:
                            dve.wait_ge(s["gelu_done"], 2 * t)
                        v.tensor_scalar(y[:, :, :], src, w, None, ALU.mult).then_inc(s["conv"], 1)
                    else:
                        dve.wait_ge(s["conv"], 14 * t + 7 * i + k)
                        ins = v.scalar_tensor_tensor(out=y[:, :, k:n], in0=src, scalar=w, in1=y[:, :, k:n], op0=ALU.mult, op1=ALU.add)
                        ins.then_inc(s["conv"], 1)
                dve.wait_ge(s["conv"], 14 * t + 7 * i + 7)
                dve.sem_inc(s["conv_done"], 1)

            def step(t, X, Y, T):
                if X:
                    if Y:
                        dve.wait_ge(s["proj_done"], 4 * t)
                        dve.wait_ge(s["xln_done"], t)
                    dve.wait_ge(s["xr_ev"], 2 * (t + 1))
                    for d in range(2):
                        for i in range(2):
                            ins = v.tensor_copy(XL[:, i, d, :].rearrange("p (c f) -> p c f", f=LOW)[:, :, i:LOW],
                                                (XR, XI)[i][:, :, 0:LOW - i]).then_inc(s["xl_done"], 1)
                if X:
                    conv(t, 0, not Y)
                if T:
                    dve.wait_ge(s["rstd_done"], t - 1)
                    dve.wait_ge(s["t_done"], 2 * (t - 2))
                    dve.wait_ge(s["rows_out"], 16 * (t - 2))
                    dve.wait_ge(s["xsq_done"], t - 2)
                    for j in range(TB):
                        v.tensor_scalar(x1s[:, j, :], xres[:, j, :], mv[:, j, 0:1], y0[:, j:j + 1], ALU.subtract, ALU.mult).then_inc(s["x1_done"], 1)
                if X:
                    conv(t, 1, not Y)
                if X:
                    for i in range(2):
                        dve.wait_ge(s["s_done"], 2 * t + i + 1)
                        sc = ps[:, 4 + i, :].rearrange("p (n k) -> p n k", n=NHP)
                        v.tensor_reduce(mx[:, i, :], sc, AX, ALU.max).then_inc(s["max_done"], 1)
                        dve.wait_ge(s["max_done"], 2 * t + i + 1)
                        if Y:
                            dve.wait_ge(s["pn_done"], 2 * t)
                        v.tensor_tensor(Sb[:, i, :, :], sc, mx[:, i, :].unsqueeze(2).broadcast_to((P, NHP, LT)), ALU.subtract).then_inc(s["sub_done"], 1)
                if Y:
                    dve.wait_ge(s["a_done"], t)
                    if T:
                        dve.wait_ge(s["z_done"], 2 * (t - 1))
                    dve.wait_ge(s["xln_ev"], t)
                    v.scalar_tensor_tensor(out=AL[:, :], in0=ps[:, 6, 0:P], scalar=al[:, 0:1], in1=xln[:, :],
                                           op0=ALU.mult, op1=ALU.subtract).then_inc(s["al_done"], 1)
                if X:
                    for i in range(2):
                        dve.wait_ge(s["exp_done"], 2 * t + i + 1)
                        v.tensor_reduce(sm[:, i, :], Sb[:, i, :, :], AX, ALU.add).then_inc(s["sum_done"], 1)
                        dve.wait_ge(s["sum_done"], 2 * t + i + 1)
                        v.reciprocal(rs[:, i, :], sm[:, i, :]).then_inc(s["rec_done"], 1)
                if T:
                    dve.wait_ge(s["xsq_done"], t - 1)
                    v.tensor_reduce(sq[:, bass.ds((t - 2) * TB, TB)], xsq[:, :, :], AX, ALU.add).then_inc(s["sq_done"], 1)
                if Y:
                    for h in range(2):
                        dve.wait_ge(s["pw_done"], 2 * (t - 1) + h + 1)
                        dve.wait_ge(s["g_ev"], 2 * (t - 1) + h + 1)
                        v.tensor_tensor(Vs[:, 4 * h:4 * h + 4, :].rearrange("p j d -> p (j d)"), ps[:, h, :],
                                        Gs[:, 4 * h:4 * h + 4, :].rearrange("p j d -> p (j d)"), ALU.mult).then_inc(s["vg_done"], 1)
                if Y:
                    dve.wait_ge(s["xres_in"], 16 * t)
                    if T:
                        dve.wait_ge(s["x1_done"], TB * (t - 1))
                    for h in range(2):
                        dve.wait_ge(s["z_done"], 2 * (t - 1) + h + 1)
                        xr = xres[:, 4 * h:4 * h + 4, :].rearrange("p j d -> p (j d)")
                        v.scalar_tensor_tensor(out=xr, in0=xr, scalar=2.0, in1=ps[:, 2 + h, :], op0=ALU.mult, op1=ALU.add).then_inc(s["zs_done"], 1)
                    for j in range(TB):
                        if j % 4 == 0:
                            dve.wait_ge(s["zs_done"], 2 * (t - 1) + j // 4 + 1)
                        v.bn_stats(bn[:, j, :], xres[:, j, :]).then_inc(s["bn_done"], 1)
                    dve.wait_ge(s["bn_done"], TB * t)
                    dve.sem_inc(s["bn_seen"], 1)
                    for j in range(TB):
                        v.bn_aggr(mv[:, j, :], bn[:, j, :]).then_inc(s["mv_done"], 1)
                    dve.wait_ge(s["mv_done"], TB * t)
                    v.tensor_scalar(vh[:, :], mv[:, :, 1], EPS, None, ALU.add).then_inc(s["seed_done"], 1)
                    dve.wait_ge(s["seed_done"], 4 * (t - 1) + 1)
                    v.tensor_scalar(ya[:, :].bitcast(I32), vh[:, :].bitcast(I32), 1, None, ALU.arith_shift_right).then_inc(s["seed_done"], 1)
                    dve.wait_ge(s["seed_done"], 4 * (t - 1) + 2)
                    v.tensor_scalar(y0[:, :].bitcast(I32), ya[:, :].bitcast(I32), -1, MAGIC, ALU.mult, ALU.add).then_inc(s["seed_done"], 1)
                    v.tensor_scalar(vh[:, :], vh[:, :], 0.5, None, ALU.mult).then_inc(s["seed_done"], 1)
                if T:
                    dve.wait_ge(s["r_done"], t - 1)
                    v.tensor_copy(lg[:, bass.ds((t - 2) * TB, TB), :].rearrange("p j e -> p (j e)"), ps[:, 7, 0:TB * E]).then_inc(s["lg_ev"], 1)

            steps(dve, step)

        @block.gpsimd
        def _(pool):
            v = nc.gpsimd
            v.memset(c15[:, :], 1.5).then_inc(s["c15_done"], 1)
            pool.wait_ge(s["c15_done"], 1)

            def step(t, X, Y, T):
                if T:
                    pool.wait_ge(s["x1_done"], TB * (t - 1))
                    pool.wait_ge(s["sq_done"], t - 2)
                    v.tensor_tensor(xsq[:, :, :], x1s[:, :, :], x1s[:, :, :], ALU.mult).then_inc(s["xsq_done"], 1)
                if X:
                    for i in range(2):
                        pool.wait_ge(s["rec_done"], 2 * t + i + 1)
                        if Y:
                            pool.wait_ge(s["pt_done"], 2 * t)
                        v.tensor_tensor(Pb[:, i, :, :], Sb[:, i, :, :], rs[:, i, :].unsqueeze(2).broadcast_to((P, NHP, LT)), ALU.mult).then_inc(s["pn_done"], 1)
                if Y:
                    pool.wait_ge(s["seed_done"], 4 * t)
                    for n in range(3):
                        v.tensor_tensor(ya[:, :], y0[:, :], y0[:, :], ALU.mult).then_inc(s["newton"], 1)
                        pool.wait_ge(s["newton"], 12 * (t - 1) + 4 * n + 1)
                        v.tensor_tensor(yb[:, :], ya[:, :], vh[:, :], ALU.mult).then_inc(s["newton"], 1)
                        pool.wait_ge(s["newton"], 12 * (t - 1) + 4 * n + 2)
                        v.tensor_tensor(yb[:, :], c15[:, :], yb[:, :], ALU.subtract).then_inc(s["newton"], 1)
                        pool.wait_ge(s["newton"], 12 * (t - 1) + 4 * n + 3)
                        ins = v.tensor_tensor(y0[:, :], y0[:, :], yb[:, :], ALU.mult).then_inc(s["newton"], 1)
                        pool.wait_ge(s["newton"], 12 * (t - 1) + 4 * n + 4)
                    pool.sem_inc(s["rstd_done"], 1)
                if X:
                    pool.wait_ge(s["whi_done"], 2 * (t + 1))
                    e = bass.ds(t, 1)
                    v.tensor_tensor(wts[:, e, 2 * HF:4 * HF].rearrange("p a h -> p (a h)"), st[:, 0:2 * HF],
                                    wts[:, e, 0:2 * HF].rearrange("p a h -> p (a h)").bitcast(F32), ALU.subtract).then_inc(s["wlo_done"], 1)
                    w2 = wts[0:HG + 1, e, W2:WE].rearrange("p a (k w d) -> p (a k) w d", k=3, w=2)
                    v.tensor_tensor(w2[:, :, 1, :], st2[:, :, :], w2[:, :, 0, :].bitcast(F32), ALU.subtract).then_inc(s["wlo_done"], 1)

            steps(pool, step)



def phase2(nc, g):
    with nc.sbuf_tensor("bias", [P, E, 2, HF], F32) as bias, nc.semaphore("bias_in") as bias_in:
        g = dict(g, bias=bias, bias_in=bias_in)
        route(nc, g)
        experts(nc, g)


def route(nc, g):
    ps, cr, ident, c2, lg, sq, cn, rows_t, idx, steptab = (g[k] for k in ("ps", "cr", "ident", "c2", "lg", "sq", "cn", "rows_t", "idx", "steptab"))
    order = pair_order()
    NP = len(order)
    with ExitStack() as ctx:
        def sb(name, shape, dt=F32):
            return ctx.enter_context(nc.sbuf_tensor(name, shape, dt))

        def sem(name):
            return ctx.enter_context(nc.semaphore("rt_" + name))

        def con(name, rows=P):
            return cr[0:rows, c2[name][0]:c2[name][1]]

        full = [P, NT, E]
        dist = sb("dist", full)
        eq = sb("eq", full)
        oh1 = sb("oh1", full)
        oh2 = sb("oh2", full)
        we = sb("we", full)
        m1, m2, km, s1, s2, df, ew, dn, w1, w2 = (sb("r_" + n, [P, NT]) for n in ("m1", "m2", "km", "s1", "s2", "df", "ew", "dn", "w1", "w2"))
        maskT = sb("maskT", [P, E, NT], BF16)
        OH = sb("OH", [P, NP * NT], BF16)
        onesf = sb("onesf", [P, 448])
        onesb = sb("onesb", [P, P], BF16)
        trimb = sb("trimb", [P, P], BF16)
        iob = sb("iob", [P, P], BF16)
        zb = sb("zb", [P, P], BF16)
        csum = sb("csum", [P, NP * NT])
        posm = sb("posm", [P, NP * NT])
        pos = sb("pos", [P, NT])
        posi = sb("posi", [P, NT], I32)
        hii = sb("hii", [P, NT], I32)
        hif = sb("hif", [P, NT])
        lof = sb("lof", [P, NT])
        lohot = sb("lohot", [P, NT, P], BF16)
        hieq = sb("hieq", [P, NT, NT], BF16)
        hihot = sb("hihot", [P, NT, 2, NT], BF16)
        inv = sb("inv", [P, 2 * NT])
        En = sb("En", [NT, NP])
        Sn = sb("Sn", [NT, NP])
        pr = sb("pr", [NT, NP])
        pb = sb("pb", [NT, NP])
        prT = sb("prT", [NP, NT])
        need = sb("need", [NT, E])
        cexc = sb("cexc", [NT, E])
        ubase = sb("ubase", [NT, 1])
        uinc = sb("uinc", [NT, E])
        upos = sb("upos", [NT, E])
        uhot = sb("uhot", [NT, E, UPAD], BF16)
        ulhs = sb("ulhs", [NT, E, 3], BF16)
        onese = sb("onese", [NT, E])
        ut = sb("ut", [1, UPAD])
        assert NP * NT == 4 * 448
        s_one, s_hi, s_hip, s_hit = (sem(n) for n in ("set", "high", "high_place", "high_tile"))
        s_d, s_w, s_oh, s_mm, s_hot, s_inv, s_pr, s_prc, s_nd, s_cx, s_sq, s_ex, s_we, s_wd, s_df, s_rank, s_u, s_tab = (
            sem(n) for n in ("chain", "w", "onehot", "ranks", "hot", "inverse", "present", "present_copy", "need", "before", "sqrt", "exp",
                             "weights", "weights_out", "difference", "rank_read", "units", "table"))

        block = ctx.enter_context(nc.Block())

        @block.vector
        def _(dve):
            v = nc.vector
            n = [0]

            def link(ins):
                n[0] += 1
                ins.then_inc(s_d, 1)
                dve.wait_ge(s_d, n[0])

            def over_e(a):
                return a.unsqueeze(2).broadcast_to((P, NT, E))

            def over_t(a):
                return a.unsqueeze(1).broadcast_to((P, NT, E))

            v.tensor_copy(trimb[:, :], con("trim"))
            v.tensor_copy(iob[:, :], con("iota"))
            link(v.tensor_tensor(dist[:, :, :], lg[:, :, :], over_t(cn[:, :]), ALU.add))
            link(v.tensor_tensor(dist[:, :, :], dist[:, :, :], over_e(sq[:, :]), ALU.add))
            link(v.tensor_scalar(dist[:, :, :], dist[:, :, :], 1e-12, None, ALU.max))
            for m, oh in ((m1, oh1), (m2, oh2)):
                link(v.tensor_reduce(m[:, :], dist[:, :, :], AX, ALU.max))
                link(v.tensor_tensor(eq[:, :, :], dist[:, :, :], over_e(m[:, :]), ALU.is_equal))
                link(v.tensor_tensor(eq[:, :, :], eq[:, :, :], over_t(con("rev")), ALU.mult))
                link(v.tensor_reduce(km[:, :], eq[:, :, :], AX, ALU.max))
                link(v.tensor_tensor(oh[:, :, :], eq[:, :, :], over_e(km[:, :]), ALU.is_equal))
                if m is m1:
                    link(v.scalar_tensor_tensor(out=dist[:, :, :], in0=oh[:, :, :], scalar=-BIG, in1=dist[:, :, :], op0=ALU.mult, op1=ALU.add))
            v.sem_inc(s_w, 1)
            link(v.tensor_tensor(maskT[:, :, :].rearrange("p e t -> p t e"), oh1[:, :, :], oh2[:, :, :], ALU.add))
            at = 0
            for a in range(E - 1):
                w = E - 1 - a
                if a % 2 == 0:
                    ins = v.tensor_tensor(OH[:, at * NT:(at + w) * NT].rearrange("p (b t) -> p b t", b=w),
                                          maskT[:, a:a + 1, :].broadcast_to((P, w, NT)), maskT[:, a + 1:E, :], ALU.mult)
                else:
                    for k in range(w):
                        ins = v.tensor_tensor(OH[:, (at + k) * NT:(at + k + 1) * NT], maskT[:, a, :], maskT[:, E - 1 - k, :], ALU.mult)
                at += w
            ins.then_inc(s_oh, 1)
            dve.wait_ge(s_sq, 2)
            v.tensor_tensor(df[:, :], s2[:, :], s1[:, :], ALU.subtract).then_inc(s_df, 1)
            dve.wait_ge(s_one, 1)
            dve.wait_ge(s_mm, 2)
            for c in range(4):
                link(v.tensor_tensor_scan(csum[:, c * 448:(c + 1) * 448], onesf[:, :], ps[:, 4 + c, 0:448],
                                          0.0 if c == 0 else csum[:, c * 448 - 1:c * 448], ALU.mult, ALU.add))
            v.memset(Sn[:, 0:1], 0.0)
            cv = csum[0:NT, :].rearrange("p (a t) -> p a t", t=NT)
            v.tensor_copy(Sn[:, 1:NP], cv[:, 0:NP - 1, NT - 1])
            link(v.tensor_copy(En[:, :], cv[:, :, NT - 1]))
            link(v.tensor_scalar(pr[:, :], Sn[:, :], con("tend", NT), None, ALU.is_lt))
            link(v.scalar_tensor_tensor(out=pr[:, :], in0=En[:, :], scalar=con("tstart", NT), in1=pr[:, :], op0=ALU.is_gt, op1=ALU.mult))
            link(v.tensor_tensor(pb[:, :], En[:, :], Sn[:, :], ALU.is_gt))
            v.tensor_tensor(pr[:, :], pr[:, :], pb[:, :], ALU.mult).then_inc(s_pr, 1)
            for c in range(4):
                ins = v.tensor_tensor(posm[:, c * 448:(c + 1) * 448], csum[:, c * 448:(c + 1) * 448], ps[:, c, 0:448], ALU.add)
            link(ins)
            link(v.tensor_tensor(posm[:, :], posm[:, :], OH[:, :], ALU.mult))
            link(v.tensor_reduce(pos[:, :], posm[:, :].rearrange("p (a t) -> p t a", t=NT), AX, ALU.add))
            link(v.tensor_copy(posi[:, :], pos[:, :]))
            link(v.tensor_scalar(hii[:, :], posi[:, :], 7, None, ALU.arith_shift_right))
            link(v.tensor_copy(hif[:, :], hii[:, :]))
            link(v.scalar_tensor_tensor(out=lof[:, :], in0=hif[:, :], scalar=-float(P), in1=pos[:, :], op0=ALU.mult, op1=ALU.add))
            dve.wait_ge(s_ex, 1)
            link(v.tensor_scalar(dn[:, :], ew[:, :], 1.0, None, ALU.add))
            link(v.reciprocal(w1[:, :], dn[:, :]))
            link(v.tensor_tensor(w2[:, :], w1[:, :], ew[:, :], ALU.mult))
            link(v.tensor_tensor(we[:, :, :], oh1[:, :, :], over_e(w1[:, :]), ALU.mult))
            link(v.tensor_tensor(eq[:, :, :], oh2[:, :, :], over_e(w2[:, :]), ALU.mult))
            v.tensor_tensor(we[:, :, :], we[:, :, :], eq[:, :, :], ALU.add).then_inc(s_we, 1)
            dve.wait_ge(s_prc, 1)
            link(v.tensor_copy(prT[:, :], ps[0:NP, 4, 0:NT]))
            v.sem_inc(s_nd, 1)
            dve.wait_ge(s_prc, 2)
            link(v.tensor_scalar(need[:, :], ps[0:NT, 5, 0:E], 0.0, None, ALU.is_gt))
            v.sem_inc(s_nd, 1)
            for c in range(4):
                part = slice(c * NT // 4, (c + 1) * NT // 4)
                shape = (P, NT // 4, P)
                v.tensor_tensor(hieq[:, part, :], iob[:, 0:NT].unsqueeze(1).broadcast_to((P, NT // 4, NT)),
                                hif[:, part].unsqueeze(2).broadcast_to((P, NT // 4, NT)), ALU.is_equal).then_inc(s_hi, 1)
                v.tensor_tensor(lohot[:, part, :], iob[:, :].unsqueeze(1).broadcast_to(shape),
                                lof[:, part].unsqueeze(2).broadcast_to(shape), ALU.is_equal).then_inc(s_hot, 1)
            dve.wait_ge(s_prc, 3)
            link(v.tensor_reduce(ubase[:, :], ps[0:NT, 6, 0:E], AX, ALU.add))
            link(v.tensor_tensor_scan(uinc[:, :], onese[:, :], need[:, :], ubase[:, 0:1], ALU.mult, ALU.add))
            link(v.tensor_tensor(upos[:, :], uinc[:, :], need[:, :], ALU.mult))
            link(v.tensor_scalar(upos[:, :], upos[:, :], -1.0, None, ALU.add))
            for e in range(E):
                v.tensor_scalar(uhot[:, e, :], con("unit", NT), upos[:, e:e + 1], None, ALU.is_equal)
            v.tensor_copy(ulhs[:, :, 0], con("part", NT).broadcast_to((NT, E)))
            v.tensor_copy(ulhs[:, :, 1], con("ev", NT))
            v.tensor_scalar(ulhs[:, :, 2], con("ev", NT), -float(E), None, ALU.add).then_inc(s_u, 1)
            dve.wait_ge(s_inv, 1)
            link(v.tensor_copy(inv[:, :], ps[:, 0, 0:2 * NT]))
            link(v.scalar_tensor_tensor(out=idx[:, :], in0=inv[:, NT:], scalar=float(P), in1=inv[:, 0:NT], op0=ALU.mult, op1=ALU.add))
            dve.wait_ge(s_tab, 1)
            link(v.tensor_copy(ut[:, :], ps[0:1, 4, 0:UPAD]))

            def fields(t, f):
                return steptab[:, t:t + ITER, f:f + 2]

            def unit(a):
                return a.rearrange("p (i u) -> p i u", u=2)

            uexp, uwt = unit(ps[0:1, 5, 0:UPAD]), unit(ps[0:1, 7, 0:UPAD])
            v.tensor_scalar(fields(3, 0), unit(ut[:, :]), float(P), None, ALU.mult)
            v.tensor_scalar(fields(4, 2), uexp, float(2 * HF), None, ALU.mult)
            v.tensor_scalar(fields(7, 4), unit(ut[:, :]), float(ROW), None, ALU.mult)
            v.tensor_scalar(fields(4, 8), uexp, float(WE), None, ALU.mult)
            v.tensor_scalar(fields(7, 10), uexp, float(WE), None, ALU.mult)
            link(v.tensor_scalar(ut[:, :], ut[:, :], float(ROW), float(D + E), ALU.mult, ALU.add))
            v.tensor_tensor(fields(7, 6), uwt, unit(ut[:, :]), ALU.add)

        @block.scalar
        def _(act):
            act.wait_ge(s_w, 1)
            nc.scalar.activation(s1[:, :], m1[:, :], ACT.Sqrt).then_inc(s_sq, 1)
            nc.scalar.activation(s2[:, :], m2[:, :], ACT.Sqrt).then_inc(s_sq, 1)
            act.wait_ge(s_df, 1)
            nc.scalar.activation(ew[:, :], df[:, :], ACT.Exp).then_inc(s_ex, 1)
            for c in range(4):
                part = slice(c * NT // 4, (c + 1) * NT // 4)
                act.wait_ge(s_hi, c + 1)
                nc.scalar.activation(hihot[:, part, 0, :], hieq[:, part, :], ACT.Copy, scale=con("part")).then_inc(s_hip, 1)

        @block.gpsimd
        def _(pool):
            v = nc.gpsimd
            v.memset(onesf[:, :], 1.0)
            v.memset(onesb[:, :], 1.0)
            v.memset(zb[:, :], 0.0)
            v.memset(onese[:, :], 1.0)
            v.memset(steptab[:, :, :], 0).then_inc(s_one, 1)
            for c in range(4):
                part = slice(c * NT // 4, (c + 1) * NT // 4)
                pool.wait_ge(s_hi, c + 1)
                v.tensor_tensor(hihot[:, part, 1, :], hieq[:, part, :], con("iota")[:, part].unsqueeze(2).broadcast_to((P, NT // 4, NT)),
                                ALU.mult).then_inc(s_hit, 1)

        @block.tensor
        def _(pe):
            pe.wait_ge(s_one, 1)
            pe.wait_ge(s_oh, 1)
            for w, b in ((trimb, 0), (onesb, 4)):
                for c in range(4):
                    mm = pe.matmul(ps[:, b + c, 0:448], w[:, :], OH[:, c * 448:(c + 1) * 448], start=True, stop=True)
                mm.then_inc(s_mm, 1)
            pe.wait_ge(s_pr, 1)
            pe.transpose(ps[0:NP, 4, 0:NT], pr[:, :], ident[0:NT, 0:NT]).then_inc(s_prc, 1)
            pe.wait_ge(s_nd, 1)
            pe.matmul(ps[0:NT, 5, 0:E], prT[:, :], con("inc", NP), start=True, stop=True).then_inc(s_prc, 1)
            pe.wait_ge(s_nd, 2)
            pe.matmul(ps[0:NT, 6, 0:E], con("tri", NT)[:, 0:NT], need[:, :], start=True, stop=True).then_inc(s_prc, 1)
            pe.matmul(ps[:, 0, 0:2 * NT], zb[:, :], zb[:, :], start=True, stop=False)
            for c in range(4):
                pe.wait_ge(s_hot, c + 1)
                pe.wait_ge(s_hip, c + 1)
                pe.wait_ge(s_hit, c + 1)
                for t in range(c * NT // 4, (c + 1) * NT // 4):
                    pe.matmul(ps[:, 0, 0:2 * NT], lohot[:, t, :], hihot[:, t, :, :].rearrange("p b m -> p (b m)"), start=False, stop=False)
            pe.matmul(ps[:, 0, 0:2 * NT], zb[:, :], zb[:, :], start=False, stop=True).then_inc(s_inv, 1)
            pe.wait_ge(s_u, 1)
            for f, b in enumerate((4, 5, 7)):
                for e in range(E):
                    mm = pe.matmul(ps[0:1, b, 0:UPAD], ulhs[:, e, f:f + 1], uhot[:, e, :], start=(e == 0), stop=(e == E - 1))
            mm.then_inc(s_tab, 1)

        @block.sync
        def _(sp):
            sp.dma_start(g["bias"][:, :, 0, :], g["bg"].partition_broadcast(P)).then_inc(g["bias_in"], 16)
            sp.dma_start(g["bias"][:, :, 1, :], g["b1"].partition_broadcast(P)).then_inc(g["bias_in"], 16)
            sp.wait_ge(s_we, 1)
            for b in range(B):
                sp.dma_start(rows_t[b][:, :, D:RD], we[:, b * TB:(b + 1) * TB, :]).then_inc(s_wd, 16)
            sp.wait_ge(s_wd, 16 * B)


def experts(nc, g):
    ps, cr, ident, idx, steptab, rows, out, wts = (g[k] for k in ("ps", "cr", "ident", "idx", "steptab", "rows_dram", "out", "wts"))
    out_rows = out.rearrange("b s d -> (b s) d")
    with ExitStack() as ctx:
        def sb(name, shape, dt=F32):
            return ctx.enter_context(nc.sbuf_tensor(name, shape, dt))

        bias = g["bias"]
        xT = sb("xT", [P, NT * P])
        xs = sb("xs", [P, NT, ROW])
        xg = sb("xg", [P, 2, RD])
        gi = sb("gi", [P, 2], U32)
        si = sb("si", [P, 2], U32)
        xh = sb("xh", [P, 2, 2, P], F32R)
        xl = sb("xl", [P, 2, 2, P], F32R)
        gu = sb("gu", [P, 2, 2, HF])
        sg = sb("sg", [P, 2, HF])
        h = sb("h", [P, 2, 2, HF])
        hh = sb("hh", [HG + 1, 2, 2, 3, P], F32R)
        hl = sb("hl", [HG + 1, 2, 2, 3, P], F32R)
        ys = sb("ys", [P, 2, D])
        bn = sb("bn2", [P, 2, 6])
        mv = sb("mv2", [P, 2, 2])
        va, vh, ya, yb, y0 = (sb(k + "2", [P, 2]) for k in ("va", "vh", "ya", "yb", "y0"))
        s = {k: ctx.enter_context(nc.semaphore("e_" + k)) for k in (
            "prep", "dma_turn", "gi_done", "gat0", "gat1", "si_done", "sca0", "sca1",
            "t_done", "xT_done", "xs_done", "xh_done", "xl_done", "a_done", "gu_done", "sg_done", "h_done",
            "b_done", "hh_done", "hl_done", "c_done", "acc_done", "bn_seen", "norm", "ys_done")}
        gat, sca = (s["gat0"], s["gat1"]), (s["sca0"], s["sca1"])
        wflat = wts[:, :, :].rearrange("p e w -> p (e w)")
        w2flat = wts[0:HG + 1, :, :].rearrange("p e w -> p (e w)")
        xsflat = xs[:, :, :].rearrange("p t w -> p (t w)")
        bflat = bias[:, :, :, :].rearrange("p e w h -> p (e w h)")

        LAST = STEPS
        assert FL % 2 == 0 and NT % 2 == 0

        def flags(t):
            return (t < NT, 2 <= t < NT + 2, 3 <= t < ITER + 3, 4 <= t < ITER + 4, 6 <= t < ITER + 6, 7 <= t < ITER + 7, FL <= t < NT + FL, FL + 2 <= t < NT + FL + 2,
                    t > 7, t > FL + 3)

        def steps(eng, step):
            t = 0
            while t < LAST:
                f, m = flags(t), 1
                while t + m < LAST and flags(t + m) == f:
                    m += 1
                if m >= 4:
                    with eng.Fori(0, m // 2) as i:
                        for k in range(2):
                            step(2 * i + (t + k), lambda c, k=k: i + (t + k - c) // 2, (t + k) % 2, *f[:8])
                for k in range(m - m % 2 if m >= 4 else 0, m):
                    step(t + k, lambda c, k=k: (t + k - c) // 2, (t + k) % 2, *f[:8])
                t += m

        def first(t):
            return isinstance(t, int) and t == 4

        def offsets(engine, t, first, tops):
            why = "the table's values are offsets of tiles and experts that exist"
            vals = nc.values_load_multi_w_load_instructions(
                steptab[0:1, bass.ds(t, 1), first:first + len(tops)].rearrange("p a f -> p (a f)"), engines=(engine,),
                min_val=0, max_val=max(tops), skip_runtime_bounds_check_because=why)[1]
            return [nc.s_assert_within(x, 0, top, skip_runtime_bounds_check_because=why) for x, top in zip(vals, tops)]

        XTOP, BTOP, WTOP, RTOP = (NT - 1) * P, (E - 1) * 2 * HF, (E - 1) * WE, (NT - 1) * ROW

        block = ctx.enter_context(nc.Block())

        @block.gpsimd
        def _(pool):
            v = nc.gpsimd
            v.memset(xs[:, :, RD:ROW], 0.0).then_inc(s["prep"], 1)

            def step(t, half, par, G, T, X, A, Bf, Cf, F, O):
                if O:
                    k, b = t - FL - 2, par
                    pool.wait_ge(sca[b], 16 * half(FL + 2))
                    v.tensor_copy(si[:, b:b + 1], idx[:, bass.ds(k, 1)]).then_inc(s["si_done"], 1)
                    pool.wait_ge(s["si_done"], k + 1)
                    pool.wait_ge(s["ys_done"], k + 1)
                    pool.sem_inc(s["dma_turn"], 1)
                    v.indirect_dma_start(out_rows, bass.IndirectOffsetOnAxis(si[:, b:b + 1], 0), ys[:, b, :], None).then_inc(sca[b], 16)
                if A:
                    for u in range(2):
                        n = 2 * (t - 4) + u
                        pool.wait_ge(s["sg_done"], n + 1)
                        if Bf:
                            pool.wait_ge(s["b_done"], 2 * (t - 6) + u + 1)
                        v.tensor_tensor(h[:, par, u, :], gu[:, u, 1, :], sg[:, u, :], ALU.mult).then_inc(s["h_done"], 1)
                if G:
                    if T:
                        pool.wait_ge(s["xs_done"], t - 1)
                        pool.wait_ge(s["t_done"], t - 1)
                    v.tensor_copy(gi[:, par:par + 1], idx[:, bass.ds(t, 1)]).then_inc(s["gi_done"], 1)
                    pool.wait_ge(s["gi_done"], t + 1)
                    pool.sem_inc(s["dma_turn"], 1)
                    v.indirect_dma_start(xg[:, par, :], None, rows, bass.IndirectOffsetOnAxis(gi[:, par:par + 1], 0)).then_inc(gat[par], 16)

            steps(pool, step)
            pool.wait_ge(sca[0], 16 * NT // 2)
            pool.wait_ge(sca[1], 16 * NT // 2)

        @block.tensor
        def _(pe):
            def down(t, u, par, T, w2):
                n = 2 * (t - 7) + u
                pe.wait_ge(s["hl_done"], n + 1)
                if u == 1:
                    pe.wait_ge(s["xT_done"], (t - 1) if T else NT)
                for k in range(3):
                    rows = HG + 1 if k == 0 else HG
                    for j, (a, w) in enumerate(((hh, 0), (hl, 0), (hh, D))):
                        mm = pe.matmul(ps[:, 6 + u, 0:D], a[0:rows, 1 - par, u, k, :], w2flat[0:rows, bass.ds(w2 + (W2 + 2 * k * D + w), D)],
                                       start=(k == 0 and j == 0), stop=(k == 2 and j == 2))
                mm.then_inc(s["c_done"], 1)

            def turn(t, u, par, Cf):
                n = 2 * (t - 6) + u
                pe.wait_ge(s["h_done"], n + 1)
                if Cf:
                    pe.wait_ge(s["hl_done"], n - 1)
                for k in range(3):
                    mm = pe.transpose(ps[0:HG, 4 + u, k * P:(k + 1) * P], h[:, par, u, k * HG:(k + 1) * HG], ident)
                mm.then_inc(s["b_done"], 1)

            def up(t, u, par, Bf, w1):
                n = 2 * (t - 4) + u
                pe.wait_ge(s["xl_done"], n + 1)
                if not first(t):
                    pe.wait_ge(s["gu_done"], n - 1)
                for k, (a, b) in enumerate(((xh, 0), (xl, 0), (xh, 2 * HF))):
                    for w in range(2):
                        mm = pe.matmul(ps[:, 2 * u + w, 0:HF], a[:, 1 - par, u, :], wflat[:, bass.ds(w1 + (b + w * HF), HF)],
                                       start=(k == 0), stop=(k == 2))
                mm.then_inc(s["a_done"], 1)

            def step(t, half, par, G, T, X, A, Bf, Cf, F, O):
                if A or Cf:
                    off = offsets(mybir.EngineType.PE, t, 8, [WTOP] * 4)
                for u in range(2):
                    if Bf:
                        turn(t, u, par, Cf)
                    if A:
                        up(t, u, par, Bf, off[u])
                if T:
                    pe.wait_ge(gat[par], 16 * half(0))
                    pe.wait_ge(s["xT_done"], t - 2)
                    if Cf:
                        pe.wait_ge(s["acc_done"], 2 * (t - 7))
                    pe.transpose(ps[:, 7, P:2 * P], xg[:, par, 0:D], ident).then_inc(s["t_done"], 1)
                if Cf:
                    pe.wait_ge(s["acc_done"], 2 * (t - 7))
                    for u in range(2):
                        down(t, u, par, T, off[2 + u])

            pe.wait_ge(s["prep"], 3)
            steps(pe, step)

        @block.scalar
        def _(act):
            def step(t, half, par, G, T, X, A, Bf, Cf, F, O):
                if X:
                    off = offsets(mybir.EngineType.Activation, t, 0, [XTOP] * 2)
                def turned(u):
                    act.wait_ge(s["b_done"], 2 * (t - 6) + u + 1)
                    if Cf:
                        act.wait_ge(s["c_done"], 2 * (t - 7))
                    nc.scalar.activation(hh[0:HG, par, u, :, :].rearrange("p k m -> p (k m)"), ps[0:HG, 4 + u, 0:3 * P], ACT.Copy).then_inc(s["hh_done"], 1)

                if Bf:
                    turned(0)
                if X:
                    for u in range(2):
                        act.wait_ge(s["xT_done"], (t - 2) if T else NT)
                        if A:
                            act.wait_ge(s["a_done"], 2 * (t - 4))
                        nc.scalar.activation(xh[:, par, u, :], xT[:, bass.ds(off[u], P)], ACT.Copy).then_inc(s["xh_done"], 1)
                if Bf:
                    turned(1)
                for u in range(2):
                    if A:
                        n = 2 * (t - 4) + u
                        act.wait_ge(s["gu_done"], n + 1)
                        if not first(t):
                            act.wait_ge(s["h_done"], n - 1)
                        nc.scalar.activation(sg[:, u, :], gu[:, u, 0, :], ACT.Silu).then_inc(s["sg_done"], 1)
                    if T and u == 0:
                        act.wait_ge(s["t_done"], t - 1)
                        nc.scalar.activation(xT[:, bass.ds((t - 2) * P, P)], ps[:, 7, P:2 * P], ACT.Copy).then_inc(s["xT_done"], 1)
                        nc.scalar.activation(xs[:, bass.ds(t - 2, 1), 0:RD].rearrange("p a m -> p (a m)"), xg[:, par, :], ACT.Copy).then_inc(s["xs_done"], 1)

            steps(act, step)

        @block.vector
        def _(dve):
            v = nc.vector
            v.memset(xs[:, 0, 0:P], 1.0).then_inc(s["norm"], 1)
            dve.wait_ge(s["norm"], 1)
            ones = xs[96:HG + 1, 0:1, 0:P].broadcast_to((HG + 1 - 96, 2, P))
            for b in range(2):
                v.tensor_copy(hh[96:HG + 1, b, :, 0, :], ones).then_inc(s["norm"], 1)
            dve.wait_ge(s["norm"], 3)
            for b in range(2):
                v.tensor_tensor(hl[96:HG + 1, b, :, 0, :], ones, hh[96:HG + 1, b, :, 0, :].bitcast(F32), ALU.subtract).then_inc(s["prep"], 1)
            dve.wait_ge(g["bias_in"], 32)

            def piece(k, pair, at, acc):
                rows2 = xs[:, bass.ds(k, 2), 0:D]

                def after(n):
                    dve.wait_ge(s["norm"], 17 * pair + n + 3)

                if at == 0:
                    dve.wait_ge(s["acc_done"], acc)
                    for j in range(2):
                        v.bn_stats(bn[:, j, :], rows2[:, j, :]).then_inc(s["norm"], 1)
                if at == 1:
                    after(2)
                    dve.sem_inc(s["bn_seen"], 1)
                    for j in range(2):
                        v.bn_aggr(mv[:, j, :], bn[:, j, :]).then_inc(s["norm"], 1)
                if at == 2:
                    after(4)
                    v.tensor_scalar(va[:, :], mv[:, :, 1], EPS, None, ALU.add).then_inc(s["norm"], 1)
                if at == 3:
                    after(5)
                    v.tensor_scalar(ya[:, :].bitcast(I32), va[:, :].bitcast(I32), 1, None, ALU.arith_shift_right).then_inc(s["norm"], 1)
                    v.tensor_scalar(vh[:, :], va[:, :], -0.5, None, ALU.mult).then_inc(s["norm"], 1)
                if at == 4:
                    after(7)
                    v.tensor_scalar(y0[:, :].bitcast(I32), ya[:, :].bitcast(I32), -1, MAGIC, ALU.mult, ALU.add).then_inc(s["norm"], 1)
                if 5 <= at < 14:
                    after(at + 3)
                    if at % 3 == 2:
                        v.tensor_tensor(ya[:, :], y0[:, :], y0[:, :], ALU.mult).then_inc(s["norm"], 1)
                    if at % 3 == 0:
                        v.tensor_tensor(yb[:, :], ya[:, :], vh[:, :], ALU.mult).then_inc(s["norm"], 1)
                    if at % 3 == 1:
                        v.scalar_tensor_tensor(out=y0[:, :], in0=yb[:, :], scalar=1.5, in1=y0[:, :], op0=ALU.add, op1=ALU.mult).then_inc(s["norm"], 1)
                if at == 14:
                    after(17)
                    for j in range(2):
                        dve.wait_ge(sca[j], 16 * pair)
                        v.tensor_scalar(ys[:, j, :], rows2[:, j, :], mv[:, j, 0:1], y0[:, j:j + 1], ALU.subtract, ALU.mult).then_inc(s["ys_done"], 1)
            def step(t, half, par, G, T, X, A, Bf, Cf, F, O):
                at = [8 * par]

                def norm():
                    if F:
                        piece(t - par - FL, half(FL + par), at[0], 2 * (t - 7) if Cf else 2 * ITER)
                    at[0] += 1

                if X or A or Cf:
                    off = offsets(mybir.EngineType.DVE, t, 0, [XTOP] * 2 + [BTOP] * 2 + [RTOP] * 2 + [RTOP + D + E] * 2)
                for u in range(2):
                    if Bf:
                        n = 2 * (t - 6) + u
                        dve.wait_ge(s["hh_done"], n + 1)
                        v.tensor_tensor(hl[0:HG, par, u, :, :].rearrange("p k m -> p (k m)"), ps[0:HG, 4 + u, 0:3 * P],
                                        hh[0:HG, par, u, :, :].rearrange("p k m -> p (k m)").bitcast(F32), ALU.subtract).then_inc(s["hl_done"], 1)
                    norm()
                    if A:
                        n = 2 * (t - 4) + u
                        if not first(t):
                            dve.wait_ge(s["h_done"], n - 1)
                        dve.wait_ge(s["a_done"], n + 1)
                        v.tensor_tensor(gu[:, u, :, :], ps[:, 2 * u:2 * u + 2, 0:HF],
                                        bflat[:, bass.ds(off[2 + u], 2 * HF)].rearrange("p (w h) -> p w h", w=2), ALU.add).then_inc(s["gu_done"], 1)
                    norm()
                for u in range(2):
                    if X:
                        n = 2 * (t - 3) + u
                        dve.wait_ge(s["xh_done"], n + 1)
                        v.tensor_tensor(xl[:, par, u, :], xT[:, bass.ds(off[u], P)], xh[:, par, u, :].bitcast(F32), ALU.subtract).then_inc(s["xl_done"], 1)
                    norm()
                for u in range(2):
                    if Cf:
                        n = 2 * (t - 7) + u
                        dve.wait_ge(s["xs_done"], (t - 6) if T else NT)
                        dve.wait_ge(s["acc_done"], n)
                        dve.wait_ge(s["c_done"], n + 1)
                        row = xsflat[:, bass.ds(off[4 + u], D)]
                        v.scalar_tensor_tensor(out=row, in0=ps[:, 6 + u, 0:D], scalar=xsflat[:, bass.ds(off[6 + u], 1)], in1=row,
                                               op0=ALU.mult, op1=ALU.add).then_inc(s["acc_done"], 1)
                    norm()
            steps(dve, step)


_INS = ["L0_attn_hidden_states", "L0_attn_q_w", "L0_attn_k_w", "L0_attn_v_w", "L0_attn_o_w", "L0_attn_dw_r", "L0_attn_pw_r",
        "L0_attn_dw_i", "L0_attn_pw_i", "L0_attn_gate_w", "L0_attn_alpha_raw", "L0_ffn_centroid", "L0_ffn_Wg", "L0_ffn_bg",
        "L0_ffn_W1", "L0_ffn_b1", "L0_ffn_W2", "L0_ffn_b2"]
_OUTS = [((B, SEQ, D), "float32")]


def kernel(**inputs):
    import concourse.bacc as _bacc
    from concourse.bass_utils import run_bass_kernel_spmd as _run

    nc = _bacc.Bacc("TRN2", target_bir_lowering=False, num_devices=1)
    arrays, args = {}, []
    for name in _INS:
        a = np.ascontiguousarray(inputs[name])
        arrays[f"in_{name}_dram"] = a
        args.append(nc.dram_tensor(f"in_{name}_dram", a.shape, mybir.dt.from_np(a.dtype), kind="ExternalInput").ap())
    for name, a in (("tables", packed(constants())[0]), ("resident_tables", packed(resident_constants())[0])):
        arrays[name] = a
        args.append(nc.dram_tensor(name, a.shape, F32, kind="ExternalInput").ap())
    for i, (shape, dtype) in enumerate(_OUTS):
        args.append(nc.dram_tensor(f"out_{i}_dram", shape, mybir.dt.from_np(np.dtype(dtype)), kind="ExternalOutput").ap())
    program(nc, *args)
    r = _run(nc, [arrays], core_ids=[0])
    return r.results[0]["out_0_dram"]
```

```python
from contextlib import ExitStack

import numpy as np

import concourse.bass as bass
from concourse import mybir

P = 128
B, SEQ, D = 8, 1024, 128
C = 64
NC = SEQ // C
FR, FI = C // 2 + 1, C // 2
LOW = 4
HR, HI = FR - LOW, FI - LOW
KS = 7
NH, NKV, HD = 16, 4, 64
NHP = NH // 2
TB = SEQ // P
NT = B * TB
LT = NC * LOW
E, HF, TOPK = 8, 342, 2
HG = HF // 3
NPAIR = E * (E - 1) // 2
EPS = 1e-5
ROW = 144
RD = D + E
UNITS = TOPK * NT + NPAIR - 1
ITER = (UNITS + 1) // 2
LAGF = ITER - NT
UPAD = 2 * ITER
WE = 4 * HF + 6 * D
W2 = 4 * HF
FL = LAGF + 10
STEPS = NT + FL + 2
BODY = 8

F32 = mybir.dt.float32
F32R = mybir.dt.float32r
BF16 = mybir.dt.bfloat16
U32 = mybir.dt.uint32
I32 = mybir.dt.int32
ALU = mybir.AluOpType
ACT = mybir.ActivationFunctionType
AX = mybir.AxisListType.X
BIG = 3.0e38
MAGIC = 0x5F3759DF


def pair_order():
    out = []
    for a in range(E - 1):
        rest = list(range(a + 1, E))
        out += [(a, b) for b in (rest if a % 2 == 0 else rest[::-1])]
    return out


def constants():
    n = np.arange(C)
    parts = {}
    fwd = np.zeros((P, P))
    for c in range(2):
        for f in range(FR):
            fwd[c * C + n, c * C + f] = np.cos(2 * np.pi * f * n / C)
        for f in range(1, FI):
            fwd[c * C + n, c * C + FR + f - 1] = -np.sin(2 * np.pi * f * n / C)
    parts["fwd"] = fwd
    high = np.zeros((P, P))
    for c in range(2):
        for f in range(LOW, FR):
            high[c * HR + f - LOW, c * C + n] = (2 if f < C // 2 else 1) / C * np.cos(2 * np.pi * f * n / C)
        for f in range(LOW, FI):
            high[C + c * HI + f - LOW, c * C + n] = -2 / C * np.sin(2 * np.pi * f * n / C)
    parts["high"] = high
    q = np.arange(P) % C // LOW
    mq = np.zeros((P, P))
    mq[q, np.arange(P)] = 1
    parts["mq"] = mq
    mk = np.zeros((P, NHP, C))
    for c in range(NC):
        mk[c, :, (c + 1) * LOW:] = -BIG
    parts["mk"] = mk.reshape(P, NHP * C)
    low = np.zeros((P, TB, P))
    for j in range(TB):
        for c in range(2):
            for f in range(LOW):
                row = (2 * j + c) * LOW + f
                low[row, j, c * C + n] = (2 if f else 1) / C * np.cos(2 * np.pi * f * n / C)
                if f:
                    low[LT + row, j, c * C + n] = -2 / C * np.sin(2 * np.pi * f * n / C)
    parts["low"] = low.reshape(P, TB * P)
    return parts


def resident_constants():
    parts = {"ident": np.eye(P)}
    tri = np.triu(np.ones((P, P)), 1)
    parts["tri"] = tri
    parts["trim"] = tri - 1
    inc = np.zeros((P, E))
    for p, (a, b) in enumerate(pair_order()):
        inc[p, a] = inc[p, b] = 1
    parts["inc"] = inc
    parts["rev"] = np.tile(E - np.arange(E), (P, 1))
    parts["iota"] = np.tile(np.arange(P), (P, 1))
    parts["unit"] = np.tile(np.arange(UPAD), (P, 1))
    parts["part"] = np.arange(P)[:, None]
    parts["tstart"] = np.arange(P)[:, None] * P
    parts["tend"] = np.arange(P)[:, None] * P + P
    parts["ev"] = np.tile(np.arange(E), (P, 1))
    return parts


def packed(parts):
    cols, at = {}, 0
    for k, v in parts.items():
        cols[k] = (at, at + v.shape[1])
        at += v.shape[1]
    return np.concatenate(list(parts.values()), axis=1).astype(np.float32), cols


def program(nc, x, qw, kw, vw, ow, dwr, pwr, dwi, pwi, gw, alpha, cent, Wg, bg, W1, b1, W2, b2, cst1, cst2, out):
    c1, c2 = packed(constants())[1], packed(resident_constants())[1]
    n1, n2 = cst1.shape[1], cst2.shape[1]
    rows_dram = nc.dram_tensor("rows_dram", (NT * P, RD), F32).ap()
    rows_t = rows_dram.rearrange("(b j p) d -> b p j d", p=P, j=TB)
    x_t = x.rearrange("b (j p) d -> b p j d", p=P)
    ctx = ExitStack()
    with ctx:
        def sb(name, shape, dt=F32):
            return ctx.enter_context(nc.sbuf_tensor(name, shape, dt))

        ps = ctx.enter_context(nc.psum_tensor("ps", [P, 8, 512], F32))
        cr = sb("cr", [P, n2])
        ident = cr[:, c2["ident"][0]:c2["ident"][1]]
        wts = sb("wts", [P, E, WE], F32R)
        lg = sb("lg", [P, NT, E])
        sq = sb("sq", [P, NT])
        cn = sb("cn", [P, E])

        dist, eq, oh1, oh2 = (sb(k, [P, NT, E]) for k in ("dist", "eq", "oh1", "oh2"))
        m1, m2, km = (sb("r_" + k, [P, NT]) for k in ("m1", "m2", "km"))
        idx = sb("idx", [P, NT], U32)
        steptab = sb("steptab", [1, STEPS, 8], I32)
        petab = sb("petab", [1, STEPS + 1, 8], I32)
        phase1(nc, locals())
        phase2(nc, locals())


def phase1(nc, g):
    ps, cr, ident, wts = (g[k] for k in ("ps", "cr", "ident", "wts"))
    lg, sq, cn, rows_t, x_t, c1 = (g[k] for k in ("lg", "sq", "cn", "rows_t", "x_t", "c1"))
    ctx = ExitStack()
    with ctx:
        def sb(name, shape, dt=F32):
            return ctx.enter_context(nc.sbuf_tensor(name, shape, dt))

        def sem(name):
            return ctx.enter_context(nc.semaphore(name))

        cs = sb("cs1", [P, g["n1"]])
        fwd, high, mq, mk = (cs[:, c1[k][0]:c1[k][1]] for k in ("fwd", "high", "mq", "mk"))
        low = cs[:, c1["low"][0]:c1["low"][1]].rearrange("p (j m) -> p j m", j=TB)
        early = c1["low"][0]
        mqb = sb("mqb", [NC, P], BF16)
        mkb = sb("mkb", [NC, 512], BF16)
        qwT = sb("qwT", [P, NH * HD])
        kwT = sb("kwT", [P, NKV, 2, HD])
        vwT = sb("vwT", [P, NKV * HD])
        owT = sb("owT", [P, NKV, 2, D])
        pwT = sb("pwT", [P, 3, D])
        cT = sb("cT", [P, E])
        cT2 = sb("cT2", [P, E])
        ones = sb("ones", [P, P])
        dw = sb("dw", [P, 2, KS])
        al = sb("al", [P, 1])
        alz = sb("alz", [P, 1])
        araw = sb("araw", [P, 1])
        xt = sb("xt", [P, TB, D])
        xres = sb("xres", [P, TB, D])
        x1s = sb("x1s", [P, TB, D])
        XF = sb("XF", [P, NC, C])
        XR, XI = XF[:, :, 0:FR], XF[:, :, FR:C]
        XL = sb("XL", [P, 2, 2, LT])
        YR = sb("YR", [P, NC, HR])
        YI = sb("YI", [P, NC, HI])
        G = sb("G", [P, 2, TB, C])
        QB = sb("QB", [P, 2, NHP, 2, LT])
        kT = sb("kT", [P, NKV, 2, LT])
        VB = sb("VB", [P, 2, NKV, 2, HD])
        xln = sb("xln", [P, D])
        gate = sb("gate", [P, NC])
        gtan = sb("gtan", [P, NC])
        Sb = sb("Sb", [P, 2, NHP, LT])
        Pb = sb("Pb", [P, 2, NHP, LT])
        mx = sb("mx", [P, 2, NHP])
        sm = sb("sm", [P, 2, NHP])
        rs = sb("rs", [P, 2, NHP])
        PT = sb("PT", [P, 2, NKV, P])
        OT = sb("OT", [P, NKV, 2, 2, LT])
        AL = sb("AL", [P, D])
        VT = sb("VT", [P, TB, 2, C])
        Vs = sb("Vs", [P, TB, D])
        x1T = sb("x1T", [P, TB, P])
        bn = sb("bn", [P, TB, 6])
        mv = sb("mv", [P, TB, 2])
        vh = sb("vh", [P, TB])
        y0 = sb("y0", [P, TB])
        ya = sb("ya", [P, TB])
        yb = sb("yb", [P, TB])
        c15 = sb("c15", [P, TB])
        c0 = sb("c0", [P, TB])
        nmr = sb("nmr", [P, TB])
        xsq = sb("xsq", [P, TB, D])
        st = sb("st", [P, 2 * HF + 3 * D])
        st2 = st[0:HG + 1, 2 * HF:2 * HF + 3 * D].rearrange("p (k d) -> p k d", k=3)
        raw = VT[:, :, :, :].rearrange("p a i b -> p (a i b)")
        raw2 = Vs[:, :, :].rearrange("p a b -> p (a b)")
        raw3 = x1T[:, :, :].rearrange("p a b -> p (a b)")

        s = {k: sem("p1_" + k) for k in (
            "const_in", "late_in", "top_two", "raw_in", "raw3_in", "x_in", "xres_in", "w_in", "rows_out", "prep_mm", "prep_cp", "prep_cst", "prep_al", "dw_in",
            "dft_done", "proj_done", "s_done", "pt_done", "ot_done", "a_done", "vt_done", "pw_done",
            "z_done", "t_done", "r_done", "xln_done",
            "xr_ev", "q_ev", "k_ev", "v_ev", "gelu_done", "pt_ev", "ot_ev", "exp_done", "vs_ev", "gate_done", "tan_done",
            "x1t_ev", "whi_done", "xln_ev", "st_zero",
            "xl_done", "conv", "conv_done", "max_done", "sub_done", "sum_done", "rec_done", "al_done", "vg_done", "zs_done",
            "bn_done", "bn_seen", "mv_done", "seed_done", "x1_done", "lg_ev", "sq_done", "wlo_done",
            "pn_done", "c15_done", "newton", "rstd_done")}

        preps = []
        qr = raw.rearrange("p (j d) -> p j d", j=8)
        owr = raw2.rearrange("p (k h a e) -> p k h a e", k=NKV, a=2, h=2)
        kvr = raw3.rearrange("p (j d) -> p j d", j=8)
        for j in range(8):
            preps.append((qr[:, j, :], P))
        for j in range(8):
            preps.append((raw2[:, j * P:(j + 1) * P], P))
        for j in range(8):
            preps.append((kvr[0:E if j == 7 else P, j, :], E if j == 7 else P))

        def steps(eng, step):
            step(0, True, False, False)
            step(1, True, True, False)
            step(2, True, True, True)
            with eng.Fori(3, B) as s_:
                step(s_, True, True, True)
            step(B, False, True, True)
            step(B + 1, False, False, True)

        block = ctx.enter_context(nc.Block())

        @block.sync
        def _(sp):
            sp.dma_start(qr, g["qw"].rearrange("(j p) d -> p j d", p=P)).then_inc(s["raw_in"], 16)
            for h in range(2):
                for a in range(2):
                    sp.dma_start(owr[:, :, h, a, :], g["ow"].rearrange("o (k a h e) -> a h o k e", k=NKV, a=2, h=2)[a, h])\
                      .then_inc(s["raw_in"], 16)
            sp.dma_start(kvr[:, 0:2, :], g["kw"].rearrange("(j p) d -> p j d", p=P)).then_inc(s["raw3_in"], 16)
            sp.dma_start(kvr[:, 2:4, :], g["vw"].rearrange("(j p) d -> p j d", p=P)).then_inc(s["raw3_in"], 16)
            sp.dma_start(kvr[:, 4, :], g["pwr"]).then_inc(s["raw3_in"], 16)
            sp.dma_start(kvr[:, 5, :], g["pwi"]).then_inc(s["raw3_in"], 16)
            sp.dma_start(kvr[:, 6, :], g["gw"]).then_inc(s["raw3_in"], 16)
            sp.dma_start(kvr[0:E, 7, :], g["cent"]).then_inc(s["raw3_in"], 16)
            sp.dma_start(cs[:, early:], g["cst1"][:, early:]).then_inc(s["late_in"], 16)

            def step(t, X, Y, T):
                if X:
                    sp.wait_ge(s["dft_done"], 2 * t)
                    sp.dma_start(xt[:, :, :], x_t[bass.ds(t, 1), :, :, :].rearrange("b p j d -> p (b j) d")).then_inc(s["x_in"], 16)
                    if Y:
                        sp.wait_ge(s["whi_done"], 2 * t)
                        sp.wait_ge(s["wlo_done"], 2 * t)
                    else:
                        sp.wait_ge(s["st_zero"], 1)
                    e = bass.ds(t, 1)
                    sp.dma_start(st[:, 0:HF], g["Wg"][e, :, :].rearrange("a d h -> d (a h)")).then_inc(s["w_in"], 16)
                    sp.dma_start(st[:, HF:2 * HF], g["W1"][e, :, :].rearrange("a d h -> d (a h)")).then_inc(s["w_in"], 16)
                    sp.dma_start(st2[0:HG, :, :], g["W2"][e, :, :].rearrange("a (k p) d -> p (a k) d", p=HG)).then_inc(s["w_in"], 16)
                    sp.dma_start(st2[HG:HG + 1, 0, :], g["b2"][e, :]).then_inc(s["w_in"], 16)
                if T:
                    sp.wait_ge(s["x1_done"], TB * (t - 1))
                    sp.dma_start(rows_t[bass.ds(t - 2, 1), :, :, 0:D].rearrange("b p j d -> p (b j) d"), x1s[:, :, :]).then_inc(s["rows_out"], 16)
                if Y:
                    if T:
                        sp.wait_ge(s["x1_done"], TB * (t - 1))
                    sp.dma_start(xres[:, :, :], x_t[bass.ds(t - 1, 1), :, :, :].rearrange("b p j d -> p (b j) d")).then_inc(s["xres_in"], 16)

            steps(sp, step)
            sp.wait_ge(s["rows_out"], 16 * B)

        @block.tensor
        def _(pe):
            pe.wait_ge(s["const_in"], 32)
            pe.wait_ge(s["raw_in"], 80)
            for i, (a, r) in enumerate(preps):
                if i == 16:
                    pe.wait_ge(s["raw3_in"], 96)
                pe.transpose(ps[0:P, i // 4, i % 4 * P:i % 4 * P + r], a, ident[0:r, 0:r]).then_inc(s["prep_mm"], 1)
            pe.wait_ge(s["prep_cp"], 10)
            pe.wait_ge(s["prep_cst"], 4)
            pe.matmul(ps[:, 6, 0:E], ones[:, :], cT2[:, :], start=True, stop=True).then_inc(s["prep_mm"], 1)
            pe.wait_ge(s["prep_cp"], 11)

            def step(t, X, Y, T):
                def turned(h):
                    pe.wait_ge(s["x1t_ev"], 2 * (t - 2) + h)
                    for j in range(4):
                        mm = pe.transpose(ps[:, 7, j * P:(j + 1) * P], x1s[:, 4 * h + j, :], ident)
                    mm.then_inc(s["t_done"], 1)

                if Y:
                    if T:
                        pe.wait_ge(s["zs_done"], 2 * (t - 1))
                    for i in range(2):
                        pe.wait_ge(s["pn_done"], 2 * (t - 1) + i + 1)
                        for k in range(NKV):
                            mm = pe.transpose(ps[:, 2 + i, k * P:(k + 1) * P],
                                              Pb[:, i, 2 * k:2 * k + 2, :].rearrange("p a k -> p (a k)"), ident)
                        mm.then_inc(s["pt_done"], 1)
                if X:
                    pe.wait_ge(s["x_in"], 16 * (t + 1))
                    if T:
                        pe.wait_ge(s["vg_done"], 2 * (t - 1))
                    for h in range(2):
                        for j in range(4):
                            mm = pe.matmul(ps[:, h, j * P:(j + 1) * P], xt[:, 4 * h + j, :], fwd, start=True, stop=True)
                        mm.then_inc(s["dft_done"], 1)
                if Y:
                    pe.wait_ge(s["v_ev"], 2 * t)
                    for i in range(2):
                        pe.wait_ge(s["pt_ev"], 2 * (t - 1) + i + 1)
                        for k in range(NKV):
                            mm = pe.matmul(ps[:, 2 + i, k * P:(k + 1) * P], VB[:, i, k, :, :].rearrange("p a e -> p (a e)"),
                                           PT[:, i, k, :], start=True, stop=True)
                        mm.then_inc(s["ot_done"], 1)
                if X:
                    pe.wait_ge(s["xl_done"], 4 * (t + 1))
                    if Y:
                        pe.wait_ge(s["sub_done"], 2 * t)
                    for n in range(NHP):
                        mm = pe.matmul(ps[:, 4 + n // 4, n % 4 * P:(n % 4 + 1) * P], qwT[:, n * P:(n + 1) * P],
                                       XL[:, :, 0, :], start=True, stop=True)
                        if n % 4 == 3:
                            mm.then_inc(s["proj_done"], 1)
                    if Y:
                        pe.wait_ge(s["tan_done"], t)
                        pe.wait_ge(s["xln_ev"], t)
                    for k in range(NKV):
                        mm = pe.matmul(ps[:, 6, k * P:(k + 1) * P], kwT[:, k, :, :].rearrange("p a e -> p (a e)"),
                                       XL[:, :, 0, :], start=True, stop=True)
                    mm.then_inc(s["proj_done"], 1)
                    if T:
                        pe.wait_ge(s["lg_ev"], t - 2)
                    for i in range(2):
                        mm = pe.matmul(ps[:, 7, i * 256:(i + 1) * 256], XL[:, i, :, :].rearrange("p a t -> p (a t)"),
                                       vwT[:, :], start=True, stop=True)
                    mm.then_inc(s["proj_done"], 1)
                    pe.wait_ge(s["k_ev"], t + 1)
                if Y:
                    pe.wait_ge(s["gelu_done"], 2 * t)
                    if X:
                        pe.wait_ge(s["xr_ev"], 2 * (t + 1))
                    for h in range(2):
                        for i in range(2):
                            mm = pe.matmul(ps[:, h, i * 4 * C:(i + 1) * 4 * C], pwT[:, i, :],
                                           G[:, i, 4 * h:4 * h + 4, :].rearrange("p j f -> p (j f)"), start=True, stop=True)
                        mm.then_inc(s["pw_done"], 1)
                if X:
                    pe.wait_ge(s["q_ev"], 4 * (t + 1))
                    for i in range(2):
                        pe.matmul(ps[:, 4 + i, :], mqb[:, :], mkb[:, :], start=True, stop=False)
                        for n in range(NHP):
                            mm = pe.matmul(ps[:, 4 + i, n * LT:(n + 1) * LT], QB[:, i, n, :, :].rearrange("p a t -> p (a t)"),
                                           kT[:, n // 2, i, :], start=False, stop=(n == NHP - 1))
                        mm.then_inc(s["s_done"], 1)
                if Y:
                    pe.wait_ge(s["ot_ev"], 2 * t)
                    for h in range(2):
                        pe.wait_ge(s["vg_done"], 2 * (t - 1) + h + 1)
                        for j in range(4):
                            mm = pe.transpose(ps[:, 2 + h, j * P:(j + 1) * P], VT[:, 4 * h + j, :, :].rearrange("p i f -> p (i f)"), ident)
                        mm.then_inc(s["vt_done"], 1)
                if T:
                    pe.wait_ge(s["v_ev"], 2 * (t + 1) if X else 2 * B)
                    pe.wait_ge(s["lg_ev"], t - 2)
                    pe.wait_ge(s["x1_done"], TB * (t - 1))
                    turned(0)
                if Y:
                    pe.wait_ge(s["ot_ev"], 2 * t)
                    for n in range(2 * NKV):
                        mm = pe.matmul(ps[:, 6, 0:P], OT[:, n // 2, n % 2, :, :].rearrange("p i t -> p (i t)"),
                                       owT[:, n // 2, n % 2, :], start=(n == 0), stop=(n == 2 * NKV - 1))
                    mm.then_inc(s["a_done"], 1)
                if T:
                    turned(1)
                if Y:
                    pe.wait_ge(s["al_done"], t)
                if X:
                    pe.matmul(ps[:, 6, P:P + NC], pwT[:, 2, :], XL[:, 0, 0, 0:LT:LOW], start=True, stop=True)
                    for i in range(2):
                        mm = pe.matmul(ps[i * LT:(i + 1) * LT, 6, 2 * P:3 * P], XL[:, i, 0, :], ident, start=True, stop=True)
                    mm.then_inc(s["xln_done"], 1)
                if Y:
                    if not T:
                        pe.wait_ge(s["late_in"], 16)
                    for h in range(2):
                        pe.wait_ge(s["vs_ev"], 2 * (t - 1) + h + 1)
                        for j in range(4):
                            pe.matmul(ps[:, 2 + h, j * P:(j + 1) * P], low[:, 4 * h + j, :], AL[:, :], start=(j == 0), stop=False)
                        pe.matmul(ps[:, 2 + h, :], high, Vs[:, 4 * h:4 * h + 4, :].rearrange("p j d -> p (j d)"),
                                  start=False, stop=True).then_inc(s["z_done"], 1)
                if T:
                    pe.wait_ge(s["x1t_ev"], 2 * (t - 1))
                    for j in range(TB):
                        mm = pe.matmul(ps[:, 7, j * E:(j + 1) * E], x1T[:, j, :], cT[:, :], start=True, stop=True)
                    mm.then_inc(s["r_done"], 1)

            steps(pe, step)

        @block.scalar
        def _(act):
            act.dma_start(cr[:, :], g["cst2"]).then_inc(s["const_in"], 16)
            act.dma_start(cs[:, 0:early], g["cst1"][:, 0:early]).then_inc(s["const_in"], 16)
            act.dma_start(dw[:, 0, :], g["dwr"].rearrange("d a k -> d (a k)")).then_inc(s["dw_in"], 16)
            act.dma_start(dw[:, 1, :], g["dwi"].rearrange("d a k -> d (a k)")).then_inc(s["dw_in"], 16)
            act.dma_start(araw[:, :], g["alpha"].partition_broadcast(P)).then_inc(s["dw_in"], 16)
            act.wait_ge(s["dw_in"], 48)
            nc.scalar.activation(alz[:, :], araw[:, :], ACT.Tanh, scale=0.5).then_inc(s["prep_al"], 1)
            act.wait_ge(s["prep_al"], 1)
            nc.scalar.activation(al[:, :], alz[:, :], ACT.Copy, bias=0.5, scale=0.5).then_inc(s["prep_al"], 1)
            for j in range(2):
                act.wait_ge(s["prep_mm"], 4 * (j + 1))
                nc.scalar.activation(qwT[:, j * 512:(j + 1) * 512], ps[:, j, :], ACT.Copy).then_inc(s["prep_cp"], 1)
            for j in range(2):
                act.wait_ge(s["prep_mm"], 8 + 4 * (j + 1))
                nc.scalar.activation(owT[:, 2 * j:2 * j + 2, :, :].rearrange("p k h d -> p (k h d)"), ps[:, 2 + j, :],
                                     ACT.Copy).then_inc(s["prep_cp"], 1)
            act.wait_ge(s["prep_mm"], 24)
            for d in range(2):
                nc.scalar.activation(kwT[:, :, d, :], ps[:, 4, 0:256].rearrange("p (k e) -> p k e", k=NKV), ACT.Copy).then_inc(s["prep_cp"], 1)
            nc.scalar.activation(vwT[:, :], ps[:, 4, 256:512], ACT.Copy).then_inc(s["prep_cp"], 1)
            nc.scalar.activation(pwT[:, :, :].rearrange("p a d -> p (a d)"), ps[:, 5, 0:3 * D], ACT.Copy).then_inc(s["prep_cp"], 1)
            nc.scalar.activation(cT[:, :], ps[:, 5, 3 * D:3 * D + E], ACT.Copy, scale=-2.0).then_inc(s["prep_cp"], 1)
            nc.scalar.activation(cT2[:, :], ps[:, 5, 3 * D:3 * D + E], ACT.Square).then_inc(s["prep_cp"], 1)
            act.wait_ge(s["prep_mm"], 25)
            nc.scalar.activation(cn[:, :], ps[:, 6, 0:E], ACT.Copy).then_inc(s["prep_cp"], 1)

            def step(t, X, Y, T):
                def turned(h):
                    act.wait_ge(s["t_done"], 2 * (t - 2) + h + 1)
                    act.wait_ge(s["r_done"], t - 2)
                    nc.scalar.activation(x1T[:, 4 * h:4 * h + 4, :].rearrange("p j m -> p (j m)"), ps[:, 7, :], ACT.Copy).then_inc(s["x1t_ev"], 1)

                if Y:
                    for i in range(2):
                        act.wait_ge(s["pt_done"], 2 * (t - 1) + i + 1)
                        if T:
                            act.wait_ge(s["ot_done"], 2 * (t - 1))
                        nc.scalar.activation(PT[:, i, :, :].rearrange("p k m -> p (k m)"), ps[:, 2 + i, :], ACT.Copy).then_inc(s["pt_ev"], 1)
                if X:
                    for h in range(2):
                        act.wait_ge(s["dft_done"], 2 * t + h + 1)
                        act.wait_ge(s["conv_done"], 2 * t)
                        nc.scalar.activation(XF[:, 8 * h:8 * h + 8, :].rearrange("p c f -> p (c f)"), ps[:, h, :], ACT.Copy).then_inc(s["xr_ev"], 1)
                if Y:
                    for i in range(2):
                        act.wait_ge(s["ot_done"], 2 * (t - 1) + i + 1)
                        if T:
                            act.wait_ge(s["a_done"], t - 1)
                        nc.scalar.activation(OT[:, :, :, i, :], ps[:, 2 + i, :].rearrange("p (k h t) -> p k h t", k=NKV, h=2),
                                             ACT.Copy).then_inc(s["ot_ev"], 1)
                if X:
                    if Y:
                        act.wait_ge(s["s_done"], 2 * t)
                    else:
                        act.wait_ge(s["prep_cst"], 4)
                    for r in range(2):
                        act.wait_ge(s["proj_done"], 4 * t + r + 1)
                        for h in range(2):
                            q0 = h * HD
                            nc.scalar.activation(QB[q0:q0 + HD, :, 4 * r:4 * r + 4, h, :].rearrange("p i n t -> p n i t"),
                                                 ps[q0:q0 + HD, 4 + r, :].rearrange("p (n i t) -> p n i t", n=4, i=2),
                                                 ACT.Copy).then_inc(s["q_ev"], 1)
                    act.wait_ge(s["proj_done"], 4 * t + 3)
                    nc.scalar.activation(kT[:, :, :, :].rearrange("p k i t -> p (k i t)"), ps[:, 6, :], ACT.Copy).then_inc(s["k_ev"], 1)
                if X:
                    act.wait_ge(s["proj_done"], 4 * t + 4)
                    for d in range(2):
                        q0 = d * HD
                        nc.scalar.activation(VB[q0:q0 + HD, :, :, d, :], ps[q0:q0 + HD, 7, :].rearrange("p (i k e) -> p i k e", i=2, k=NKV),
                                             ACT.Copy).then_inc(s["v_ev"], 1)
                if T:
                    act.wait_ge(s["rstd_done"], t - 1)
                    act.wait_ge(s["t_done"], 2 * (t - 2))
                    act.wait_ge(s["rows_out"], 16 * (t - 2))
                    act.wait_ge(s["sq_done"], TB * (t - 2))
                    for j in range(TB):
                        nc.scalar.activation(x1s[:, j, :], xres[:, j, :], ACT.Identity, bias=nmr[:, j:j + 1], scale=y0[:, j:j + 1]).then_inc(s["x1_done"], 1)
                if Y:
                    for h in range(2):
                        act.wait_ge(s["vt_done"], 2 * (t - 1) + h + 1)
                        if T:
                            act.wait_ge(s["z_done"], 2 * (t - 1))
                        nc.scalar.activation(Vs[:, 4 * h:4 * h + 4, :].rearrange("p j d -> p (j d)"), ps[:, 2 + h, :], ACT.Copy).then_inc(s["vs_ev"], 1)
                if T:
                    turned(0)
                for i in range(2):
                    if X:
                        act.wait_ge(s["sub_done"], 2 * t + i + 1)
                        nc.scalar.activation(Sb[:, i, :, :], Sb[:, i, :, :], ACT.Exp, scale=1.0 / 8).then_inc(s["exp_done"], 1)
                    if T and i == 0:
                        turned(1)
                if X:
                    for i, (y, n) in enumerate(((YR, HR), (YI, HI))):
                        act.wait_ge(s["conv_done"], 2 * t + i + 1)
                        if Y:
                            act.wait_ge(s["pw_done"], 2 * t)
                        nc.scalar.activation(G[:, i, :, 0:2 * n], y[:, :, :].rearrange("p (j c) f -> p j (c f)", c=2), ACT.Gelu).then_inc(s["gelu_done"], 1)
                if T:
                    act.wait_ge(s["x1_done"], TB * (t - 1))
                    for j in range(TB):
                        nc.scalar.activation(xsq[:, j, :], x1s[:, j, :], ACT.Square, accum_out=sq[:, bass.ds((t - 2) * TB + j, 1)]).then_inc(s["sq_done"], 1)
                if X:
                    act.wait_ge(s["w_in"], 64 * (t + 1))
                    e = bass.ds(t, 1)
                    nc.scalar.activation(wts[:, e, 0:2 * HF].rearrange("p a h -> p (a h)"), st[:, 0:2 * HF], ACT.Copy).then_inc(s["whi_done"], 1)
                    nc.scalar.activation(wts[0:HG + 1, e, W2:WE].rearrange("p a (k w d) -> p (a k) w d", k=3, w=2)[:, :, 0, :], st2[:, :, :],
                                         ACT.Copy).then_inc(s["whi_done"], 1)
                    act.wait_ge(s["xln_done"], t + 1)
                    nc.scalar.activation(gtan[:, :], ps[:, 6, P:P + NC], ACT.Tanh, scale=0.5 / C).then_inc(s["tan_done"], 1)
                    act.wait_ge(s["tan_done"], t + 1)
                    if Y:
                        act.wait_ge(s["vg_done"], 2 * t)
                    nc.scalar.activation(gate[:, :], gtan[:, :], ACT.Copy, bias=0.5, scale=0.5).then_inc(s["gate_done"], 1)
                    act.wait_ge(s["xln_done"], t + 1)
                    if Y:
                        act.wait_ge(s["al_done"], t)
                    else:
                        act.wait_ge(s["prep_al"], 2)
                    nc.scalar.activation(xln[:, :], ps[:, 6, 2 * P:3 * P], ACT.Copy, scale=al[:, 0:1]).then_inc(s["xln_ev"], 1)

            steps(act, step)

        @block.vector
        def _(dve):
            v = nc.vector
            v.memset(st[:, 2 * HF:], 0.0).then_inc(s["st_zero"], 1)
            v.memset(ones[:, :], 1.0).then_inc(s["prep_cst"], 1)
            v.memset(QB[:, :, :, :, :], 0.0).then_inc(s["prep_cst"], 1)
            v.memset(VB[:, :, :, :, :], 0.0).then_inc(s["prep_cst"], 1)
            v.memset(G[:, :, :, :], 0.0).then_inc(s["prep_cst"], 1)
            v.memset(XL[:, :, :, :], 0.0).then_inc(s["prep_cst"], 1)
            dve.wait_ge(s["const_in"], 32)
            v.tensor_copy(mqb[:, :], mq[0:NC, :]).then_inc(s["prep_cst"], 1)
            v.tensor_copy(mkb[:, :], mk[0:NC, :]).then_inc(s["prep_cst"], 1)
            dve.wait_ge(s["prep_al"], 2)
            dve.wait_ge(s["prep_cst"], 7)
            dve.wait_ge(s["prep_cp"], 11)
            v.memset(VT[:, :, :, :], 0.0).then_inc(s["prep_cst"], 1)
            dve.wait_ge(s["prep_cst"], 8)

            def conv(t, i, first, taps):
                y, x, n, off = ((YR, XR, HR, LOW), (YI, XI, HI, LOW - 1))[i]
                for k in taps:
                    m = n - k
                    src = x[:, :, off:off + m]
                    w = dw[:, i, KS - 1 - k:KS - k]
                    if k == 0:
                        if not first:
                            dve.wait_ge(s["gelu_done"], 2 * t)
                        v.tensor_scalar(y[:, :, :], src, w, None, ALU.mult).then_inc(s["conv"], 1)
                    else:
                        dve.wait_ge(s["conv"], 14 * t + 7 * i + k)
                        ins = v.scalar_tensor_tensor(out=y[:, :, k:n], in0=src, scalar=w, in1=y[:, :, k:n], op0=ALU.mult, op1=ALU.add)
                        ins.then_inc(s["conv"], 1)
                if KS - 1 in taps:
                    dve.wait_ge(s["conv"], 14 * t + 7 * i + 7)
                    dve.sem_inc(s["conv_done"], 1)

            def step(t, X, Y, T):
                if X:
                    if Y:
                        dve.wait_ge(s["proj_done"], 4 * t)
                        dve.wait_ge(s["xln_done"], t)
                    dve.wait_ge(s["xr_ev"], 2 * (t + 1))
                    for d in range(2):
                        for i in range(2):
                            ins = v.tensor_copy(XL[:, i, d, :].rearrange("p (c f) -> p c f", f=LOW)[:, :, i:LOW],
                                                (XR, XI)[i][:, :, 0:LOW - i]).then_inc(s["xl_done"], 1)
                if X:
                    conv(t, 0, not Y, range(KS))
                if Y:
                    dve.wait_ge(s["gate_done"], t)
                    if T:
                        dve.wait_ge(s["vt_done"], 2 * (t - 1))
                    for h in range(2):
                        dve.wait_ge(s["pw_done"], 2 * (t - 1) + h + 1)
                        for i, n in enumerate((HR, HI)):
                            ins = v.tensor_tensor(VT[:, 4 * h:4 * h + 4, i, 0:2 * n].rearrange("p j (c f) -> p j c f", c=2),
                                                  ps[:, h, i * 4 * C:(i + 1) * 4 * C].rearrange("p (j m) -> p j m", j=4)[:, :, 0:2 * n].rearrange("p j (c f) -> p j c f", c=2),
                                                  gate[:, 8 * h:8 * h + 8].rearrange("p (j c) -> p j c", c=2).unsqueeze(3).broadcast_to((P, 4, 2, n)), ALU.mult)
                        ins.then_inc(s["vg_done"], 1)
                if X:
                    for i in range(2):
                        conv(t, 1, not Y, range(2 * i, 2 * i + 2))
                        dve.wait_ge(s["s_done"], 2 * t + i + 1)
                        sc = ps[:, 4 + i, :].rearrange("p (n k) -> p n k", n=NHP)
                        v.tensor_reduce(mx[:, i, :], sc, AX, ALU.max).then_inc(s["max_done"], 1)
                        dve.wait_ge(s["max_done"], 2 * t + i + 1)
                        if Y:
                            dve.wait_ge(s["pn_done"], 2 * t)
                        v.tensor_tensor(Sb[:, i, :, :], sc, mx[:, i, :].unsqueeze(2).broadcast_to((P, NHP, LT)), ALU.subtract).then_inc(s["sub_done"], 1)
                    conv(t, 1, not Y, range(4, KS))
                if Y:
                    dve.wait_ge(s["a_done"], t)
                    if T:
                        dve.wait_ge(s["z_done"], 2 * (t - 1))
                    dve.wait_ge(s["xln_ev"], t)
                    v.scalar_tensor_tensor(out=AL[:, :], in0=ps[:, 6, 0:P], scalar=al[:, 0:1], in1=xln[:, :],
                                           op0=ALU.mult, op1=ALU.subtract).then_inc(s["al_done"], 1)
                if X:
                    for i in range(2):
                        dve.wait_ge(s["exp_done"], 2 * t + i + 1)
                        v.tensor_reduce(sm[:, i, :], Sb[:, i, :, :], AX, ALU.add).then_inc(s["sum_done"], 1)
                        dve.wait_ge(s["sum_done"], 2 * t + i + 1)
                        v.reciprocal(rs[:, i, :], sm[:, i, :]).then_inc(s["rec_done"], 1)
                if Y:
                    dve.wait_ge(s["xres_in"], 16 * t)
                    if T:
                        dve.wait_ge(s["x1_done"], TB * (t - 1))
                    for h in range(2):
                        dve.wait_ge(s["z_done"], 2 * (t - 1) + h + 1)
                        xr = xres[:, 4 * h:4 * h + 4, :].rearrange("p j d -> p (j d)")
                        v.scalar_tensor_tensor(out=xr, in0=xr, scalar=2.0, in1=ps[:, 2 + h, :], op0=ALU.mult, op1=ALU.add).then_inc(s["zs_done"], 1)
                    for j in range(TB):
                        if j % 4 == 0:
                            dve.wait_ge(s["zs_done"], 2 * (t - 1) + j // 4 + 1)
                        v.bn_stats(bn[:, j, :], xres[:, j, :]).then_inc(s["bn_done"], 1)
                    dve.wait_ge(s["bn_done"], TB * t)
                    dve.sem_inc(s["bn_seen"], 1)
                    for j in range(TB):
                        v.bn_aggr(mv[:, j, :], bn[:, j, :]).then_inc(s["mv_done"], 1)
                    dve.wait_ge(s["mv_done"], TB * t)
                    v.tensor_scalar(vh[:, :], mv[:, :, 1], EPS, None, ALU.add).then_inc(s["seed_done"], 1)
                    dve.wait_ge(s["seed_done"], 4 * (t - 1) + 1)
                    v.tensor_scalar(ya[:, :].bitcast(I32), vh[:, :].bitcast(I32), 1, None, ALU.arith_shift_right).then_inc(s["seed_done"], 1)
                    dve.wait_ge(s["seed_done"], 4 * (t - 1) + 2)
                    v.tensor_scalar(y0[:, :].bitcast(I32), ya[:, :].bitcast(I32), -1, MAGIC, ALU.mult, ALU.add).then_inc(s["seed_done"], 1)
                    v.tensor_scalar(vh[:, :], vh[:, :], 0.5, None, ALU.mult).then_inc(s["seed_done"], 1)
                if T and not Y:
                    dve.wait_ge(s["lg_ev"], B - 1)
                    dve.wait_ge(s["sq_done"], TB * (B - 1))
                    links = [0]

                    def link(ins):
                        links[0] += 1
                        ins.then_inc(s["top_two"], 1)
                        dve.wait_ge(s["top_two"], links[0])

                    top_two(nc, g, 0, (B - 1) * TB, link)
                if T:
                    dve.wait_ge(s["r_done"], t - 1)
                    v.tensor_copy(lg[:, bass.ds((t - 2) * TB, TB), :].rearrange("p j e -> p (j e)"), ps[:, 7, 0:TB * E]).then_inc(s["lg_ev"], 1)

            steps(dve, step)

        @block.gpsimd
        def _(pool):
            v = nc.gpsimd
            v.memset(c0[:, :], 0.0)
            v.memset(c15[:, :], 1.5).then_inc(s["c15_done"], 1)
            pool.wait_ge(s["c15_done"], 1)

            def step(t, X, Y, T):
                if X:
                    for i in range(2):
                        pool.wait_ge(s["rec_done"], 2 * t + i + 1)
                        if Y:
                            pool.wait_ge(s["pt_done"], 2 * t)
                        v.tensor_tensor(Pb[:, i, :, :], Sb[:, i, :, :], rs[:, i, :].unsqueeze(2).broadcast_to((P, NHP, LT)), ALU.mult).then_inc(s["pn_done"], 1)
                if Y:
                    pool.wait_ge(s["seed_done"], 4 * t)
                    for n in range(3):
                        v.tensor_tensor(ya[:, :], y0[:, :], y0[:, :], ALU.mult).then_inc(s["newton"], 1)
                        pool.wait_ge(s["newton"], 13 * (t - 1) + 4 * n + 1)
                        v.tensor_tensor(yb[:, :], ya[:, :], vh[:, :], ALU.mult).then_inc(s["newton"], 1)
                        pool.wait_ge(s["newton"], 13 * (t - 1) + 4 * n + 2)
                        v.tensor_tensor(yb[:, :], c15[:, :], yb[:, :], ALU.subtract).then_inc(s["newton"], 1)
                        pool.wait_ge(s["newton"], 13 * (t - 1) + 4 * n + 3)
                        ins = v.tensor_tensor(y0[:, :], y0[:, :], yb[:, :], ALU.mult).then_inc(s["newton"], 1)
                        pool.wait_ge(s["newton"], 13 * (t - 1) + 4 * n + 4)
                    v.tensor_tensor(ya[:, :], mv[:, :, 0], y0[:, :], ALU.mult).then_inc(s["newton"], 1)
                    pool.wait_ge(s["newton"], 13 * t)
                    v.tensor_tensor(nmr[:, :], c0[:, :], ya[:, :], ALU.subtract).then_inc(s["rstd_done"], 1)
                if X:
                    pool.wait_ge(s["whi_done"], 2 * (t + 1))
                    e = bass.ds(t, 1)
                    v.tensor_tensor(wts[:, e, 2 * HF:4 * HF].rearrange("p a h -> p (a h)"), st[:, 0:2 * HF],
                                    wts[:, e, 0:2 * HF].rearrange("p a h -> p (a h)").bitcast(F32), ALU.subtract).then_inc(s["wlo_done"], 1)
                    w2 = wts[0:HG + 1, e, W2:WE].rearrange("p a (k w d) -> p (a k) w d", k=3, w=2)
                    v.tensor_tensor(w2[:, :, 1, :], st2[:, :, :], w2[:, :, 0, :].bitcast(F32), ALU.subtract).then_inc(s["wlo_done"], 1)

            steps(pool, step)



def phase2(nc, g):
    with nc.sbuf_tensor("bias", [2, E * 2 * HF], F32R) as bias:
        g = dict(g, bias=bias)
        route(nc, g)
        experts(nc, g)


def top_two(nc, g, lo, hi, link):
    v = nc.vector
    lg, sq, cn, dist, eq, oh1, oh2, m1, m2, km = (g[k] for k in ("lg", "sq", "cn", "dist", "eq", "oh1", "oh2", "m1", "m2", "km"))
    rev = g["cr"][:, g["c2"]["rev"][0]:g["c2"]["rev"][1]]

    def part(a):
        return a[:, lo:hi, :]

    def over_e(a):
        return a[:, lo:hi].unsqueeze(2).broadcast_to((P, hi - lo, E))

    def over_t(a):
        return a.unsqueeze(1).broadcast_to((P, hi - lo, E))

    link(v.tensor_tensor(part(dist), part(lg), over_t(cn[:, :]), ALU.add))
    link(v.tensor_tensor(part(dist), part(dist), over_e(sq), ALU.add))
    link(v.tensor_scalar(part(dist), part(dist), 1e-12, None, ALU.max))
    for m, oh in ((m1, oh1), (m2, oh2)):
        link(v.tensor_reduce(m[:, lo:hi], part(dist), AX, ALU.max))
        link(v.tensor_tensor(part(eq), part(dist), over_e(m), ALU.is_equal))
        link(v.tensor_tensor(part(eq), part(eq), over_t(rev), ALU.mult))
        link(v.tensor_reduce(km[:, lo:hi], part(eq), AX, ALU.max))
        link(v.tensor_tensor(part(oh), part(eq), over_e(km), ALU.is_equal))
        if m is m1:
            link(v.scalar_tensor_tensor(out=part(dist), in0=part(oh), scalar=-BIG, in1=part(dist), op0=ALU.mult, op1=ALU.add))


def route(nc, g):
    ps, cr, ident, c2, lg, sq, cn, rows_t, idx, steptab, petab = (g[k] for k in ("ps", "cr", "ident", "c2", "lg", "sq", "cn", "rows_t", "idx", "steptab", "petab"))
    order = pair_order()
    NP = len(order)
    QUARTER = NP * NT // 4
    assert NP * NT == 4 * QUARTER and QUARTER <= 512
    with ExitStack() as ctx:
        def sb(name, shape, dt=F32):
            return ctx.enter_context(nc.sbuf_tensor(name, shape, dt))

        def sem(name):
            return ctx.enter_context(nc.semaphore("rt_" + name))

        def con(name, rows=P):
            return cr[0:rows, c2[name][0]:c2[name][1]]

        dist, eq, oh1, oh2, m1, m2, km = (g[k] for k in ("dist", "eq", "oh1", "oh2", "m1", "m2", "km"))
        we = sb("we", [P, NT, E])
        s1, s2, df, ew, dn, w1, w2 = (sb("r_" + n, [P, NT]) for n in ("s1", "s2", "df", "ew", "dn", "w1", "w2"))
        maskT = sb("maskT", [P, E, NT], BF16)
        OH = sb("OH", [P, NP * NT], BF16)
        onesf = sb("onesf", [P, QUARTER])
        onesb = sb("onesb", [P, P], BF16)
        trimb = sb("trimb", [P, P], BF16)
        iob = sb("iob", [P, P], BF16)
        zb = sb("zb", [P, P], BF16)
        csum = sb("csum", [P, NP * NT])
        posm = sb("posm", [P, NP * NT])
        pos = sb("pos", [P, NT])
        posi = sb("posi", [P, NT], I32)
        hii = sb("hii", [P, NT], I32)
        hif = sb("hif", [P, NT])
        lof = sb("lof", [P, NT])
        lohot = sb("lohot", [P, NT, P], BF16)
        hieq = sb("hieq", [P, NT, NT], BF16)
        hihot = sb("hihot", [P, NT, 2, NT], BF16)
        inv = sb("inv", [P, 2 * NT])
        En = sb("En", [NT, NP])
        Sn = sb("Sn", [NT, NP])
        pr = sb("pr", [NT, NP])
        pb = sb("pb", [NT, NP])
        prT = sb("prT", [NP, NT])
        need = sb("need", [NT, E])
        ubase = sb("ubase", [NT, 1])
        uinc = sb("uinc", [NT, E])
        upos = sb("upos", [NT, E])
        uhot = sb("uhot", [NT, E, UPAD], BF16)
        ulhs = sb("ulhs", [NT, E, 3], BF16)
        onese = sb("onese", [NT, E])
        ut = sb("ut", [1, UPAD])
        parts = nc.dram_tensor("bias_parts", (2, E, 2 * HF), F32R).ap()
        braw = sb("braw", [E, 2 * HF])
        bhi = sb("bhi", [E, 2 * HF], F32R)
        blo = sb("blo", [E, 2 * HF], F32R)
        s_bin, s_bsplit, s_bout = (sem(n) for n in ("bias_in", "bias_split", "bias_out"))
        s_one, s_hi, s_hip, s_hit = (sem(n) for n in ("set", "high", "high_place", "high_tile"))
        s_d, s_w, s_oh, s_mm, s_hot, s_inv, s_pr, s_prc, s_nd, s_sq, s_ex, s_we, s_wd, s_df, s_u, s_tab = (
            sem(n) for n in ("chain", "w", "onehot", "ranks", "hot", "inverse", "present", "present_copy", "need", "sqrt", "exp",
                             "weights", "weights_out", "difference", "units", "table"))

        block = ctx.enter_context(nc.Block())

        @block.vector
        def _(dve):
            v = nc.vector
            n = [0]

            def link(ins):
                n[0] += 1
                ins.then_inc(s_d, 1)
                dve.wait_ge(s_d, n[0])

            def over_e(a):
                return a.unsqueeze(2).broadcast_to((P, NT, E))

            def over_t(a):
                return a.unsqueeze(1).broadcast_to((P, NT, E))

            v.tensor_copy(trimb[:, :], con("trim"))
            v.tensor_copy(iob[:, :], con("iota"))
            top_two(nc, g, (B - 1) * TB, NT, link)
            v.sem_inc(s_w, 1)
            link(v.tensor_tensor(maskT[:, :, :].rearrange("p e t -> p t e"), oh1[:, :, :], oh2[:, :, :], ALU.add))
            at = 0
            for a in range(E - 1):
                w = E - 1 - a
                if a % 2 == 0:
                    ins = v.tensor_tensor(OH[:, at * NT:(at + w) * NT].rearrange("p (b t) -> p b t", b=w),
                                          maskT[:, a:a + 1, :].broadcast_to((P, w, NT)), maskT[:, a + 1:E, :], ALU.mult)
                else:
                    for k in range(w):
                        ins = v.tensor_tensor(OH[:, (at + k) * NT:(at + k + 1) * NT], maskT[:, a, :], maskT[:, E - 1 - k, :], ALU.mult)
                at += w
            ins.then_inc(s_oh, 1)
            dve.wait_ge(s_sq, 2)
            v.tensor_tensor(df[:, :], s2[:, :], s1[:, :], ALU.subtract).then_inc(s_df, 1)
            dve.wait_ge(s_one, 1)
            dve.wait_ge(s_mm, 2)
            for c in range(4):
                link(v.tensor_tensor_scan(csum[:, c * QUARTER:(c + 1) * QUARTER], onesf[:, :], ps[:, 4 + c, 0:QUARTER],
                                          0.0 if c == 0 else csum[:, c * QUARTER - 1:c * QUARTER], ALU.mult, ALU.add))
            v.memset(Sn[:, 0:1], 0.0)
            cv = csum[0:NT, :].rearrange("p (a t) -> p a t", t=NT)
            v.tensor_copy(Sn[:, 1:NP], cv[:, 0:NP - 1, NT - 1])
            link(v.tensor_copy(En[:, :], cv[:, :, NT - 1]))
            link(v.tensor_scalar(pr[:, :], Sn[:, :], con("tend", NT), None, ALU.is_lt))
            link(v.scalar_tensor_tensor(out=pr[:, :], in0=En[:, :], scalar=con("tstart", NT), in1=pr[:, :], op0=ALU.is_gt, op1=ALU.mult))
            link(v.tensor_tensor(pb[:, :], En[:, :], Sn[:, :], ALU.is_gt))
            v.tensor_tensor(pr[:, :], pr[:, :], pb[:, :], ALU.mult).then_inc(s_pr, 1)
            for c in range(4):
                ins = v.tensor_tensor(posm[:, c * QUARTER:(c + 1) * QUARTER], csum[:, c * QUARTER:(c + 1) * QUARTER], ps[:, c, 0:QUARTER], ALU.add)
            link(ins)
            link(v.tensor_tensor(posm[:, :], posm[:, :], OH[:, :], ALU.mult))
            link(v.tensor_reduce(pos[:, :], posm[:, :].rearrange("p (a t) -> p t a", t=NT), AX, ALU.add))
            link(v.tensor_copy(posi[:, :], pos[:, :]))
            link(v.tensor_scalar(hii[:, :], posi[:, :], 7, None, ALU.arith_shift_right))
            link(v.tensor_copy(hif[:, :], hii[:, :]))
            link(v.scalar_tensor_tensor(out=lof[:, :], in0=hif[:, :], scalar=-float(P), in1=pos[:, :], op0=ALU.mult, op1=ALU.add))
            dve.wait_ge(s_ex, 1)
            link(v.tensor_scalar(dn[:, :], ew[:, :], 1.0, None, ALU.add))
            link(v.reciprocal(w1[:, :], dn[:, :]))
            link(v.tensor_tensor(w2[:, :], w1[:, :], ew[:, :], ALU.mult))
            link(v.tensor_tensor(we[:, :, :], oh1[:, :, :], over_e(w1[:, :]), ALU.mult))
            link(v.tensor_tensor(eq[:, :, :], oh2[:, :, :], over_e(w2[:, :]), ALU.mult))
            v.tensor_tensor(we[:, :, :], we[:, :, :], eq[:, :, :], ALU.add).then_inc(s_we, 1)
            dve.wait_ge(s_prc, 1)
            link(v.tensor_copy(prT[:, :], ps[0:NP, 4, 0:NT]))
            v.sem_inc(s_nd, 1)
            dve.wait_ge(s_prc, 2)
            link(v.tensor_scalar(need[:, :], ps[0:NT, 5, 0:E], 0.0, None, ALU.is_gt))
            v.sem_inc(s_nd, 1)
            dve.wait_ge(s_prc, 3)
            link(v.tensor_reduce(ubase[:, :], ps[0:NT, 6, 0:E], AX, ALU.add))
            link(v.tensor_tensor_scan(uinc[:, :], onese[:, :], need[:, :], ubase[:, 0:1], ALU.mult, ALU.add))
            link(v.tensor_tensor(upos[:, :], uinc[:, :], need[:, :], ALU.mult))
            link(v.tensor_scalar(upos[:, :], upos[:, :], -1.0, None, ALU.add))
            for e in range(E):
                v.tensor_scalar(uhot[:, e, :], con("unit", NT), upos[:, e:e + 1], None, ALU.is_equal)
            v.tensor_copy(ulhs[:, :, 0], con("part", NT).broadcast_to((NT, E)))
            v.tensor_copy(ulhs[:, :, 1], con("ev", NT))
            v.tensor_scalar(ulhs[:, :, 2], con("ev", NT), -float(E), None, ALU.add).then_inc(s_u, 1)
            for c in range(4):
                part = slice(c * NT // 4, (c + 1) * NT // 4)
                shape = (P, NT // 4, P)
                v.tensor_tensor(hieq[:, part, :], iob[:, 0:NT].unsqueeze(1).broadcast_to((P, NT // 4, NT)),
                                hif[:, part].unsqueeze(2).broadcast_to((P, NT // 4, NT)), ALU.is_equal).then_inc(s_hi, 1)
                v.tensor_tensor(lohot[:, part, :], iob[:, :].unsqueeze(1).broadcast_to(shape),
                                lof[:, part].unsqueeze(2).broadcast_to(shape), ALU.is_equal).then_inc(s_hot, 1)
            dve.wait_ge(s_tab, 1)
            link(v.tensor_copy(ut[:, :], ps[0:1, 4, 0:UPAD]))

            def fields(t, f):
                return steptab[:, t:t + ITER, f:f + 2] if f < 8 else petab[:, t:t + ITER, f - 8:f - 6]

            def unit(a):
                return a.rearrange("p (i u) -> p i u", u=2)

            uexp, uwt = unit(ps[0:1, 5, 0:UPAD]), unit(ps[0:1, 7, 0:UPAD])
            v.tensor_scalar(fields(3, 0), unit(ut[:, :]), float(P), None, ALU.mult)
            v.tensor_scalar(fields(7, 2), unit(ut[:, :]), float(ROW), None, ALU.mult)
            v.tensor_scalar(fields(4, 8), uexp, float(WE), None, ALU.mult)
            v.tensor_scalar(fields(7, 10), uexp, float(WE), None, ALU.mult)
            v.tensor_scalar(fields(4, 12), uexp, float(2 * HF), None, ALU.mult)
            link(v.tensor_scalar(ut[:, :], ut[:, :], float(ROW), float(D + E), ALU.mult, ALU.add))
            v.tensor_tensor(fields(7, 4), uwt, unit(ut[:, :]), ALU.add)
            dve.wait_ge(s_inv, 1)
            link(v.tensor_copy(inv[:, :], ps[:, 0, 0:2 * NT]))
            link(v.scalar_tensor_tensor(out=idx[:, :], in0=inv[:, NT:], scalar=float(P), in1=inv[:, 0:NT], op0=ALU.mult, op1=ALU.add))

        @block.scalar
        def _(act):
            act.wait_ge(s_w, 1)
            nc.scalar.activation(s1[:, :], m1[:, :], ACT.Sqrt).then_inc(s_sq, 1)
            nc.scalar.activation(s2[:, :], m2[:, :], ACT.Sqrt).then_inc(s_sq, 1)
            act.wait_ge(s_df, 1)
            nc.scalar.activation(ew[:, :], df[:, :], ACT.Exp).then_inc(s_ex, 1)
            for c in range(4):
                part = slice(c * NT // 4, (c + 1) * NT // 4)
                act.wait_ge(s_hi, c + 1)
                nc.scalar.activation(hihot[:, part, 0, :], hieq[:, part, :], ACT.Copy, scale=con("part")).then_inc(s_hip, 1)

        @block.gpsimd
        def _(pool):
            v = nc.gpsimd
            v.memset(onesf[:, :], 1.0)
            v.memset(onesb[:, :], 1.0)
            v.memset(zb[:, :], 0.0)
            v.memset(onese[:, :], 1.0)
            v.memset(petab[:, :, :], 0)
            v.memset(steptab[:, :, :], 0).then_inc(s_one, 1)
            pool.wait_ge(s_bin, 32)
            v.tensor_copy(bhi[:, :], braw[:, :]).then_inc(s_bsplit, 1)
            pool.wait_ge(s_bsplit, 1)
            v.tensor_tensor(blo[:, :], braw[:, :], bhi[:, :].bitcast(F32), ALU.subtract).then_inc(s_bsplit, 1)
            for k, part in enumerate((bhi, blo)):
                pool.wait_ge(s_bsplit, k + 1)
                pool.dma_start(parts[k], part[:, :]).then_inc(s_bout, 16)
            pool.wait_ge(s_bout, 32)
            pool.dma_start(g["bias"][:, :], parts.rearrange("k e h -> k (e h)")).then_inc(s_bout, 16)
            for c in range(4):
                part = slice(c * NT // 4, (c + 1) * NT // 4)
                pool.wait_ge(s_hi, c + 1)
                v.tensor_tensor(hihot[:, part, 1, :], hieq[:, part, :], con("iota")[:, part].unsqueeze(2).broadcast_to((P, NT // 4, NT)),
                                ALU.mult).then_inc(s_hit, 1)
            pool.wait_ge(s_bout, 48)

        @block.tensor
        def _(pe):
            pe.wait_ge(s_one, 1)
            pe.wait_ge(s_oh, 1)
            for w, b in ((trimb, 0), (onesb, 4)):
                for c in range(4):
                    mm = pe.matmul(ps[:, b + c, 0:QUARTER], w[:, :], OH[:, c * QUARTER:(c + 1) * QUARTER], start=True, stop=True)
                mm.then_inc(s_mm, 1)
            pe.wait_ge(s_pr, 1)
            pe.transpose(ps[0:NP, 4, 0:NT], pr[:, :], ident[0:NT, 0:NT]).then_inc(s_prc, 1)
            pe.wait_ge(s_nd, 1)
            pe.matmul(ps[0:NT, 5, 0:E], prT[:, :], con("inc", NP), start=True, stop=True).then_inc(s_prc, 1)
            pe.wait_ge(s_nd, 2)
            pe.matmul(ps[0:NT, 6, 0:E], con("tri", NT)[:, 0:NT], need[:, :], start=True, stop=True).then_inc(s_prc, 1)
            pe.wait_ge(s_u, 1)
            for f, b in enumerate((4, 5, 7)):
                for e in range(E):
                    mm = pe.matmul(ps[0:1, b, 0:UPAD], ulhs[:, e, f:f + 1], uhot[:, e, :], start=(e == 0), stop=(e == E - 1))
            mm.then_inc(s_tab, 1)
            pe.matmul(ps[:, 0, 0:2 * NT], zb[:, :], zb[:, :], start=True, stop=False)
            for c in range(4):
                pe.wait_ge(s_hot, c + 1)
                pe.wait_ge(s_hip, c + 1)
                pe.wait_ge(s_hit, c + 1)
                for t in range(c * NT // 4, (c + 1) * NT // 4):
                    pe.matmul(ps[:, 0, 0:2 * NT], lohot[:, t, :], hihot[:, t, :, :].rearrange("p b m -> p (b m)"), start=False, stop=False)
            pe.matmul(ps[:, 0, 0:2 * NT], zb[:, :], zb[:, :], start=False, stop=True).then_inc(s_inv, 1)

        @block.sync
        def _(sp):
            sp.dma_start(braw[:, 0:HF], g["bg"]).then_inc(s_bin, 16)
            sp.dma_start(braw[:, HF:], g["b1"]).then_inc(s_bin, 16)
            sp.wait_ge(s_we, 1)
            for b in range(B):
                sp.dma_start(rows_t[b][:, :, D:RD], we[:, b * TB:(b + 1) * TB, :]).then_inc(s_wd, 16)
            sp.wait_ge(s_wd, 16 * B)


def experts(nc, g):
    ps, cr, ident, idx, steptab, petab, rows, out, wts = (g[k] for k in ("ps", "cr", "ident", "idx", "steptab", "petab", "rows_dram", "out", "wts"))
    out_rows = out.rearrange("b s d -> (b s) d")
    with ExitStack() as ctx:
        def sb(name, shape, dt=F32):
            return ctx.enter_context(nc.sbuf_tensor(name, shape, dt))

        bias = g["bias"]
        xT = sb("xT", [P, NT * P])
        xs = sb("xs", [P, NT, ROW])
        xg = sb("xg", [P, 2, RD])
        gi = sb("gi", [P, 2], U32)
        si = sb("si", [P, 2], U32)
        xh = sb("xh", [P, 2, 2, P], F32R)
        xl = sb("xl", [P, 2, 2, P], F32R)
        sg = sb("sg", [P, 2, HF])
        h = sb("h", [P, 2, 2, HF])
        hh = sb("hh", [HG + 1, 2, 2, 3, P], F32R)
        hl = sb("hl", [HG + 1, 2, 2, 3, P], F32R)
        ones = sb("ones_f", [P, P])
        two = sb("two", [2, P], F32R)
        ys = sb("ys", [P, 2, D])
        bn = sb("bn2", [P, 2, 6])
        mv = sb("mv2", [P, 2, 2])
        va, vh, ya, yb, y0 = (sb(k + "2", [P, 2]) for k in ("va", "vh", "ya", "yb", "y0"))
        s = {k: ctx.enter_context(nc.semaphore("e_" + k)) for k in (
            "prep", "dma_turn", "gi_done", "gat0", "gat1", "si_done", "sca0", "sca1",
            "t_done", "xT_done", "xs_done", "xh_done", "xl_done", "a_done", "sg_done", "h_done",
            "b_done", "hh_done", "hl_done", "c_done", "acc_done", "bn_seen", "norm", "ys_done")}
        gat, sca = (s["gat0"], s["gat1"]), (s["sca0"], s["sca1"])
        wflat = wts[:, :, :].rearrange("p e w -> p (e w)")
        w2flat = wts[0:HG + 1, :, :].rearrange("p e w -> p (e w)")
        xsflat = xs[:, :, :].rearrange("p t w -> p (t w)")

        assert FL % 2 == 0 and NT % 2 == 0

        def flags(t):
            return (t < NT, 2 <= t < NT + 2, 3 <= t < ITER + 3, 4 <= t < ITER + 4, 6 <= t < ITER + 6, 7 <= t < ITER + 7, FL <= t < NT + FL, FL + 2 <= t < NT + FL + 2,
                    t > 7, t > FL + 3)

        def steps(eng, step):
            t = 0
            while t < STEPS:
                f, m = flags(t), 1
                while t + m < STEPS and flags(t + m) == f:
                    m += 1
                if m >= 2 * BODY:
                    with eng.Fori(0, m // BODY) as i:
                        for k in range(BODY):
                            step(BODY * i + (t + k), lambda c, k=k: BODY // 2 * i + (t + k - c) // 2, (t + k) % 2, *f[:8], k % 2)
                for k in range(m - m % BODY if m >= 2 * BODY else 0, m):
                    step(t + k, lambda c, k=k: (t + k - c) // 2, (t + k) % 2, *f[:8], None)
                t += m

        def first(t):
            return isinstance(t, int) and t == 4

        def offsets(engine, t, first, tops, table=None):
            why = "the table's values are offsets of tiles and experts that exist"
            vals = nc.values_load_multi_w_load_instructions(
                table if table is not None else steptab[0:1, bass.ds(t, 1), first:first + len(tops)].rearrange("p a f -> p (a f)"), engines=(engine,),
                min_val=0, max_val=max(tops), skip_runtime_bounds_check_because=why)[1]
            return [nc.s_assert_within(x, 0, top, skip_runtime_bounds_check_because=why) for x, top in zip(vals, tops)]

        XTOP, BTOP, WTOP, RTOP = (NT - 1) * P, (E - 1) * 2 * HF, (E - 1) * WE, (NT - 1) * ROW

        block = ctx.enter_context(nc.Block())

        @block.gpsimd
        def _(pool):
            v = nc.gpsimd
            v.memset(xs[:, :, RD:ROW], 0.0).then_inc(s["prep"], 1)

            def step(t, half, par, G, T, X, A, Bf, Cf, F, O, place):
                if X:
                    off = offsets(mybir.EngineType.Pool, t, 0, [XTOP] * 2)
                if O:
                    k, b = t - FL - 2, par
                    pool.wait_ge(sca[b], 16 * half(FL + 2))
                    v.tensor_copy(si[:, b:b + 1], idx[:, bass.ds(k, 1)]).then_inc(s["si_done"], 1)
                    pool.wait_ge(s["si_done"], k + 1)
                    pool.wait_ge(s["ys_done"], k + 1)
                    pool.sem_inc(s["dma_turn"], 1)
                    v.indirect_dma_start(out_rows, bass.IndirectOffsetOnAxis(si[:, b:b + 1], 0), ys[:, b, :], None).then_inc(sca[b], 16)
                if X:
                    for u in range(2):
                        n = 2 * (t - 3) + u
                        pool.wait_ge(s["xh_done"], n + 1)
                        v.tensor_tensor(xl[:, par, u, :], xT[:, bass.ds(off[u], P)], xh[:, par, u, :].bitcast(F32), ALU.subtract).then_inc(s["xl_done"], 1)
                if G:
                    if T:
                        pool.wait_ge(s["xs_done"], t - 1)
                        pool.wait_ge(s["t_done"], t - 1)
                    v.tensor_copy(gi[:, par:par + 1], idx[:, bass.ds(t, 1)]).then_inc(s["gi_done"], 1)
                    pool.wait_ge(s["gi_done"], t + 1)
                    pool.sem_inc(s["dma_turn"], 1)
                    v.indirect_dma_start(xg[:, par, :], None, rows, bass.IndirectOffsetOnAxis(gi[:, par:par + 1], 0)).then_inc(gat[par], 16)

            steps(pool, step)
            pool.wait_ge(sca[0], 16 * NT // 2)
            pool.wait_ge(sca[1], 16 * NT // 2)

        @block.tensor
        def _(pe):
            def down(t, u, par, T, w2):
                n = 2 * (t - 7) + u
                pe.wait_ge(s["hl_done"], n + 1)
                if u == 1:
                    pe.wait_ge(s["xT_done"], (t - 1) if T else NT)
                for k in range(3):
                    rows, at = HG + 1 if k == 0 else HG, w2 + (W2 + 2 * k * D)
                    pe.matmul(ps[:, 6 + u, 0:2 * D], hh[0:rows, 1 - par, u, k, :], w2flat[0:rows, bass.ds(at, 2 * D)], start=(k == 0), stop=False)
                    mm = pe.matmul(ps[:, 6 + u, 0:D], hl[0:rows, 1 - par, u, k, :], w2flat[0:rows, bass.ds(at, D)], start=False, stop=(k == 2))
                mm.then_inc(s["c_done"], 1)

            def turn(t, u, par, Cf):
                n = 2 * (t - 6) + u
                pe.wait_ge(s["h_done"], n + 1)
                if Cf:
                    pe.wait_ge(s["hl_done"], n - 1)
                for k in range(3):
                    mm = pe.transpose(ps[0:HG, 4 + u, k * P:(k + 1) * P], h[:, par, u, k * HG:(k + 1) * HG], ident)
                mm.then_inc(s["b_done"], 1)

            def up(t, u, par, w1, b1):
                n = 2 * (t - 4) + u
                if not first(t):
                    pe.wait_ge(s["sg_done"], n - 1)
                    pe.wait_ge(s["h_done"], n - 1)
                for w in range(2):
                    pe.matmul(ps[:, 2 * u + w, 0:HF], two[:, :], bias[:, bass.ds(b1 + w * HF, HF)], start=True, stop=False)
                pe.wait_ge(s["xl_done"], n + 1)
                for k, (a, b) in enumerate(((xh, 0), (xl, 0), (xh, 2 * HF))):
                    for w in range(2):
                        mm = pe.matmul(ps[:, 2 * u + w, 0:HF], a[:, 1 - par, u, :], wflat[:, bass.ds(w1 + (b + w * HF), HF)],
                                       start=False, stop=(k == 2))
                mm.then_inc(s["a_done"], 1)

            both = []

            def step(t, half, par, G, T, X, A, Bf, Cf, F, O, place):
                if A or Cf:
                    tops = [WTOP] * 4 + [BTOP] * 2
                    if place == 0:
                        both[:] = offsets(mybir.EngineType.PE, t, 0, tops + [WTOP] * 2 + tops,
                                          petab[0:1, bass.ds(t, 2), :].rearrange("p a f -> p (a f)")[:, 0:14])
                        off = both[0:6]
                    elif place == 1:
                        off = both[8:14]
                    else:
                        off = offsets(mybir.EngineType.PE, t, 0, tops, petab[0:1, bass.ds(t, 1), 0:6].rearrange("p a f -> p (a f)"))
                for u in range(2):
                    if Bf:
                        turn(t, u, par, Cf)
                    if A:
                        up(t, u, par, off[u], off[4 + u])
                if T:
                    pe.wait_ge(gat[par], 16 * half(0))
                    pe.wait_ge(s["xT_done"], t - 2)
                    if Cf:
                        pe.wait_ge(s["acc_done"], 4 * (t - 7))
                    pe.transpose(ps[:, 7, 2 * P:3 * P], xg[:, par, 0:D], ident).then_inc(s["t_done"], 1)
                if Cf:
                    pe.wait_ge(s["acc_done"], 4 * (t - 7))
                    for u in range(2):
                        down(t, u, par, T, off[2 + u])

            pe.wait_ge(s["prep"], 4)
            steps(pe, step)

        @block.scalar
        def _(act):
            def step(t, half, par, G, T, X, A, Bf, Cf, F, O, place):
                if X:
                    off = offsets(mybir.EngineType.Activation, t, 0, [XTOP] * 2)
                def turned(u):
                    act.wait_ge(s["b_done"], 2 * (t - 6) + u + 1)
                    if Cf:
                        act.wait_ge(s["c_done"], 2 * (t - 7))
                    nc.scalar.activation(hh[0:HG, par, u, :, :].rearrange("p k m -> p (k m)"), ps[0:HG, 4 + u, 0:3 * P], ACT.Copy).then_inc(s["hh_done"], 1)

                if Bf:
                    turned(0)
                if X:
                    for u in range(2):
                        act.wait_ge(s["xT_done"], (t - 2) if T else NT)
                        if A:
                            act.wait_ge(s["a_done"], 2 * (t - 4))
                        nc.scalar.activation(xh[:, par, u, :], xT[:, bass.ds(off[u], P)], ACT.Copy).then_inc(s["xh_done"], 1)
                def silu(u):
                    n = 2 * (t - 4) + u
                    act.wait_ge(s["a_done"], n + 1)
                    if not first(t):
                        act.wait_ge(s["h_done"], n - 1)
                    nc.scalar.activation(sg[:, u, :], ps[:, 2 * u, 0:HF], ACT.Silu).then_inc(s["sg_done"], 1)

                if A:
                    silu(0)
                if Bf:
                    turned(1)
                if A:
                    silu(1)
                if T:
                    act.wait_ge(s["t_done"], t - 1)
                    nc.scalar.activation(xT[:, bass.ds((t - 2) * P, P)], ps[:, 7, 2 * P:3 * P], ACT.Copy).then_inc(s["xT_done"], 1)
                    nc.scalar.activation(xs[:, bass.ds(t - 2, 1), 0:RD].rearrange("p a m -> p (a m)"), xg[:, par, :], ACT.Copy).then_inc(s["xs_done"], 1)

            steps(act, step)

        @block.vector
        def _(dve):
            v = nc.vector
            v.memset(ones[:, :], 1.0).then_inc(s["norm"], 1)
            dve.wait_ge(s["norm"], 1)
            v.tensor_copy(two[:, :], ones[0:2, :]).then_inc(s["prep"], 1)
            last = ones[96:HG + 1, :].unsqueeze(1).broadcast_to((HG + 1 - 96, 2, P))
            for b in range(2):
                v.tensor_copy(hh[96:HG + 1, b, :, 0, :], last).then_inc(s["norm"], 1)
            dve.wait_ge(s["norm"], 3)
            for b in range(2):
                v.tensor_tensor(hl[96:HG + 1, b, :, 0, :], last, hh[96:HG + 1, b, :, 0, :].bitcast(F32), ALU.subtract).then_inc(s["prep"], 1)

            def piece(k, pair, at, acc):
                rows2 = xs[:, bass.ds(k, 2), 0:D]

                def after(n):
                    dve.wait_ge(s["norm"], 17 * pair + n + 3)

                if at == 0:
                    dve.wait_ge(s["acc_done"], acc)
                    for j in range(2):
                        v.bn_stats(bn[:, j, :], rows2[:, j, :]).then_inc(s["norm"], 1)
                if at == 1:
                    after(2)
                    dve.sem_inc(s["bn_seen"], 1)
                    for j in range(2):
                        v.bn_aggr(mv[:, j, :], bn[:, j, :]).then_inc(s["norm"], 1)
                if at == 2:
                    after(4)
                    v.tensor_scalar(va[:, :], mv[:, :, 1], EPS, None, ALU.add).then_inc(s["norm"], 1)
                if at == 3:
                    after(5)
                    v.tensor_scalar(ya[:, :].bitcast(I32), va[:, :].bitcast(I32), 1, None, ALU.arith_shift_right).then_inc(s["norm"], 1)
                    v.tensor_scalar(vh[:, :], va[:, :], -0.5, None, ALU.mult).then_inc(s["norm"], 1)
                if at == 4:
                    after(7)
                    v.tensor_scalar(y0[:, :].bitcast(I32), ya[:, :].bitcast(I32), -1, MAGIC, ALU.mult, ALU.add).then_inc(s["norm"], 1)
                if 5 <= at < 14:
                    after(at + 3)
                    if at % 3 == 2:
                        v.tensor_tensor(ya[:, :], y0[:, :], y0[:, :], ALU.mult).then_inc(s["norm"], 1)
                    if at % 3 == 0:
                        v.tensor_tensor(yb[:, :], ya[:, :], vh[:, :], ALU.mult).then_inc(s["norm"], 1)
                    if at % 3 == 1:
                        v.scalar_tensor_tensor(out=y0[:, :], in0=yb[:, :], scalar=1.5, in1=y0[:, :], op0=ALU.add, op1=ALU.mult).then_inc(s["norm"], 1)
                if at == 14:
                    after(17)
                    for j in range(2):
                        dve.wait_ge(sca[j], 16 * pair)
                        v.tensor_scalar(ys[:, j, :], rows2[:, j, :], mv[:, j, 0:1], y0[:, j:j + 1], ALU.subtract, ALU.mult).then_inc(s["ys_done"], 1)
            def step(t, half, par, G, T, X, A, Bf, Cf, F, O, place):
                at = [8 * par]

                def norm():
                    if F:
                        piece(t - par - FL, half(FL + par), at[0], 4 * (t - 7) if Cf else 4 * ITER)
                    at[0] += 1

                if Cf:
                    off = offsets(mybir.EngineType.DVE, t, 0, [XTOP] * 2 + [RTOP] * 2 + [RTOP + D + E] * 2)
                for u in range(2):
                    if Bf:
                        n = 2 * (t - 6) + u
                        dve.wait_ge(s["hh_done"], n + 1)
                        v.tensor_tensor(hl[0:HG, par, u, :, :].rearrange("p k m -> p (k m)"), ps[0:HG, 4 + u, 0:3 * P],
                                        hh[0:HG, par, u, :, :].rearrange("p k m -> p (k m)").bitcast(F32), ALU.subtract).then_inc(s["hl_done"], 1)
                    norm()
                    if A:
                        n = 2 * (t - 4) + u
                        if Bf:
                            dve.wait_ge(s["b_done"], 2 * (t - 6) + u + 1)
                        dve.wait_ge(s["sg_done"], n + 1)
                        v.tensor_tensor(h[:, par, u, :], ps[:, 2 * u + 1, 0:HF], sg[:, u, :], ALU.mult).then_inc(s["h_done"], 1)
                    norm()
                norm()
                norm()
                for u in range(2):
                    if Cf:
                        n = 2 * (t - 7) + u
                        dve.wait_ge(s["xs_done"], (t - 6) if T else NT)
                        dve.wait_ge(s["c_done"], n + 1)
                        row = xsflat[:, bass.ds(off[2 + u], D)]
                        for k in range(2):
                            dve.wait_ge(s["acc_done"], 2 * n + k)
                            v.scalar_tensor_tensor(out=row, in0=ps[:, 6 + u, k * D:(k + 1) * D], scalar=xsflat[:, bass.ds(off[4 + u], 1)], in1=row,
                                                   op0=ALU.mult, op1=ALU.add).then_inc(s["acc_done"], 1)
                    norm()
            steps(dve, step)


_INS = ["L0_attn_hidden_states", "L0_attn_q_w", "L0_attn_k_w", "L0_attn_v_w", "L0_attn_o_w", "L0_attn_dw_r", "L0_attn_pw_r",
        "L0_attn_dw_i", "L0_attn_pw_i", "L0_attn_gate_w", "L0_attn_alpha_raw", "L0_ffn_centroid", "L0_ffn_Wg", "L0_ffn_bg",
        "L0_ffn_W1", "L0_ffn_b1", "L0_ffn_W2", "L0_ffn_b2"]
_OUTS = [((B, SEQ, D), "float32")]


def kernel(**inputs):
    import concourse.bacc as _bacc
    from concourse.bass_utils import run_bass_kernel_spmd as _run

    nc = _bacc.Bacc("TRN2", target_bir_lowering=False, num_devices=1)
    arrays, args = {}, []
    for name in _INS:
        a = np.ascontiguousarray(inputs[name])
        arrays[f"in_{name}_dram"] = a
        args.append(nc.dram_tensor(f"in_{name}_dram", a.shape, mybir.dt.from_np(a.dtype), kind="ExternalInput").ap())
    for name, a in (("tables", packed(constants())[0]), ("resident_tables", packed(resident_constants())[0])):
        arrays[name] = a
        args.append(nc.dram_tensor(name, a.shape, F32, kind="ExternalInput").ap())
    for i, (shape, dtype) in enumerate(_OUTS):
        args.append(nc.dram_tensor(f"out_{i}_dram", shape, mybir.dt.from_np(np.dtype(dtype)), kind="ExternalOutput").ap())
    program(nc, *args)
    r = _run(nc, [arrays], core_ids=[0])
    return r.results[0]["out_0_dram"]
```
